# Optimizing a Trainium2 kernel written in Bass

```python
import numpy as np
import jax
import jax.numpy as jnp

def _softmax(x, axis=-1):
    return jax.nn.softmax(x, axis=axis)

def _gelu(x):
    return jax.nn.gelu(x, approximate=True)

def _silu(x):
    return jax.nn.silu(x)

def _sigmoid(x):
    return jax.nn.sigmoid(x)

def _layernorm(x, axis=-1, eps=1e-05):
    m = jnp.mean(x, axis=axis, keepdims=True)
    v = jnp.var(x, axis=axis, keepdims=True)
    return (x - m) / jnp.sqrt(v + eps)

def _scatter_add(tgt, idx, src, axis=0):
    return tgt.at[idx].add(src)

def _segment_sum(src, seg, n):
    return jax.ops.segment_sum(src, seg, n)
kernel_name = 'mk_gnn_ffn_d1_gnn_r8_1947c7'

def setup_inputs(seed: int=0):
    np.random.seed(seed)
    _w = jnp.asarray

    def _rec_inputs():
        import jax
        import jax.numpy as jnp
        _gk = jax.random.key(seed)
        x = -6.415e-05 + 1 * jax.random.normal(jax.random.fold_in(_gk, 1), (2500, 512), jnp.float32)
        src = jax.random.randint(jax.random.fold_in(_gk, 2), (40000,), 0, 2500, jnp.int32)
        dst = jax.random.randint(jax.random.fold_in(_gk, 3), (40000,), 0, 2500, jnp.int32)
        _o = jnp.argsort(dst, stable=True)
        src = src[_o]
        dst = dst[_o]
        return (x, src, dst)
    x, src, dst = _rec_inputs()

    def _L0_gnn_setup():
        import jax, jax.numpy as jnp
        import numpy as np
        N = 2500
        E = 40000
        F_IN = 512
        HEADS = 8
        D = 64
        ALPHA = 0.2
        EPS = 1e-16

        def _gat_forward(x, edge_index, W_e, W_r, a):
            src = edge_index[0]
            dst = edge_index[1]
            h_e = jnp.einsum('nf,hfd->hnd', x, W_e)
            h_r = jnp.einsum('nf,hfd->hnd', x, W_r)
            a_src, a_dst, a_dif, a_abs, a_prd = jnp.split(a, 5, axis=1)
            s_src = jnp.einsum('hnd,hd->hn', h_e, a_src)[:, src]
            s_dst = jnp.einsum('hnd,hd->hn', h_e, a_dst)[:, dst]
            hr_src = h_r[:, src]
            hr_dst = h_r[:, dst]
            diff = hr_dst - hr_src
            score = s_src + s_dst + jnp.einsum('hed,hd->he', diff, a_dif) + jnp.einsum('hed,hd->he', jnp.abs(diff), a_abs) + jnp.einsum('hed,hd->he', hr_src * hr_dst, a_prd)
            alpha = jax.nn.leaky_relu(score, negative_slope=ALPHA)
            alpha_t = alpha.T
            m = jax.ops.segment_max(alpha_t, src, num_segments=N)
            ex = jnp.exp(alpha_t - m[src])
            denom = jax.ops.segment_sum(ex, src, num_segments=N)[src]
            att = ex / (denom + EPS)
            msg = att[:, :, None] * jnp.transpose(h_e[:, dst], (1, 0, 2))
            out = jax.ops.segment_sum(msg, src, num_segments=N)
            return out.reshape(N, HEADS * D)
        key = jax.random.key(seed)
        k1, k2, k3, k4, k5 = jax.random.split(key, 5)
        x = jax.random.normal(k1, (N, F_IN), dtype=jnp.float32)
        edge_index = jax.random.randint(k2, (2, E), 0, N, dtype=jnp.int64)
        s_w = np.sqrt(2.0 / (F_IN + D))
        W_e = jax.random.normal(k3, (HEADS, F_IN, D), dtype=jnp.float32) * s_w
        W_r = jax.random.normal(k4, (HEADS, F_IN, D), dtype=jnp.float32) * s_w
        s_a = np.sqrt(2.0 / (1 + 5 * D))
        a = jax.random.normal(k5, (HEADS, 5 * D), dtype=jnp.float32) * s_a
        return {'x': x, 'edge_index': edge_index, 'W_e': W_e, 'W_r': W_r, 'a': a}
    _L0_gnn_all = _L0_gnn_setup()
    _L0_gnn_in = {k: v for k, v in _L0_gnn_all.items() if k in ('W_e', 'W_r', 'a')}
    del _L0_gnn_all

    def _L0_ffn_setup():
        import jax, jax.numpy as jnp
        import numpy as np
        B, L, D, H, E, K = (8, 1024, 512, 256, 8, 2)
        SCALE = 0.02
        key = jax.random.key(seed)
        ks = jax.random.split(key, 6)
        return {'x': jax.random.normal(ks[0], (B, L, D), dtype=jnp.float32), 'Wg': jax.random.normal(ks[1], (D, E), dtype=jnp.float32) * SCALE, 'W1': jax.random.normal(ks[2], (E, D, H), dtype=jnp.float32) * SCALE, 'b1': jax.random.normal(ks[3], (E, H), dtype=jnp.float32) * SCALE, 'W2': jax.random.normal(ks[4], (E, H, D), dtype=jnp.float32) * SCALE, 'b2': jax.random.normal(ks[5], (E, D), dtype=jnp.float32) * SCALE}
    _L0_ffn_all = _L0_ffn_setup()
    _L0_ffn_in = {k: v for k, v in _L0_ffn_all.items() if k in ('Wg', 'W1', 'b1', 'W2', 'b2')}
    del _L0_ffn_all
    return {'x': x, 'src': src, 'dst': dst, 'L0_gnn_W_e': _L0_gnn_in['W_e'], 'L0_gnn_W_r': _L0_gnn_in['W_r'], 'L0_gnn_a': _L0_gnn_in['a'], 'L0_ffn_Wg': _L0_ffn_in['Wg'], 'L0_ffn_W1': _L0_ffn_in['W1'], 'L0_ffn_b1': _L0_ffn_in['b1'], 'L0_ffn_W2': _L0_ffn_in['W2'], 'L0_ffn_b2': _L0_ffn_in['b2']}

def reference(x, src, dst, L0_gnn_W_e, L0_gnn_W_r, L0_gnn_a, L0_ffn_Wg, L0_ffn_W1, L0_ffn_b1, L0_ffn_W2, L0_ffn_b2):
    import jax
    import jax.numpy as jnp

    def _L0_gnn_ref(x, edge_index, W_e, W_r, a):
        import jax, jax.numpy as jnp
        import numpy as np
        N = 2500
        E = 40000
        F_IN = 512
        HEADS = 8
        D = 64
        ALPHA = 0.2
        EPS = 1e-16

        def _gat_forward(x, edge_index, W_e, W_r, a):
            src = edge_index[0]
            dst = edge_index[1]
            h_e = jnp.einsum('nf,hfd->hnd', x, W_e)
            h_r = jnp.einsum('nf,hfd->hnd', x, W_r)
            a_src, a_dst, a_dif, a_abs, a_prd = jnp.split(a, 5, axis=1)
            s_src = jnp.einsum('hnd,hd->hn', h_e, a_src)[:, src]
            s_dst = jnp.einsum('hnd,hd->hn', h_e, a_dst)[:, dst]
            hr_src = h_r[:, src]
            hr_dst = h_r[:, dst]
            diff = hr_dst - hr_src
            score = s_src + s_dst + jnp.einsum('hed,hd->he', diff, a_dif) + jnp.einsum('hed,hd->he', jnp.abs(diff), a_abs) + jnp.einsum('hed,hd->he', hr_src * hr_dst, a_prd)
            alpha = jax.nn.leaky_relu(score, negative_slope=ALPHA)
            alpha_t = alpha.T
            m = jax.ops.segment_max(alpha_t, src, num_segments=N)
            ex = jnp.exp(alpha_t - m[src])
            denom = jax.ops.segment_sum(ex, src, num_segments=N)[src]
            att = ex / (denom + EPS)
            msg = att[:, :, None] * jnp.transpose(h_e[:, dst], (1, 0, 2))
            out = jax.ops.segment_sum(msg, src, num_segments=N)
            return out.reshape(N, HEADS * D)
        return _gat_forward(x, edge_index, W_e, W_r, a)

    def _L0_ffn_ref(x, Wg, W1, b1, W2, b2):
        import jax, jax.numpy as jnp
        import numpy as np
        B, L, D, H, E, K = (8, 1024, 512, 256, 8, 2)
        SCALE = 0.02
        b, l, d = x.shape
        xt = x.reshape(-1, d)
        T = xt.shape[0]
        gate = jax.nn.softmax(xt @ Wg, axis=-1)
        topv, topi = jax.lax.top_k(gate, K)
        topv = topv / (jnp.sum(topv, axis=-1, keepdims=True) + 1e-06)
        scores = jnp.zeros((T, E), dtype=xt.dtype).at[jnp.arange(T)[:, None], topi].set(topv)
        out = jnp.zeros_like(xt)
        for e in range(E):
            h = jax.nn.gelu(xt @ W1[e] + b1[e], approximate=False)
            ye = h @ W2[e] + b2[e]
            out = out + ye * scores[:, e:e + 1]
        return out.reshape(b, l, d)
    edge_index = jnp.stack([src, dst])
    x = x + _L0_gnn_ref(_layernorm(x, axis=-1), edge_index, L0_gnn_W_e, L0_gnn_W_r, L0_gnn_a)
    x = x + _L0_ffn_ref(_layernorm(x, axis=-1)[None], L0_ffn_Wg, L0_ffn_W1, L0_ffn_b1, L0_ffn_W2, L0_ffn_b2)[0]
    return x

_drawn_inputs = setup_inputs


def setup_inputs(seed=0):
    import zlib

    import numpy as np

    out = dict(_drawn_inputs(seed))
    spreads = {}
    factors = {'L0_ffn_b1': 25.5, 'L0_ffn_b2': 4.487}
    for name, (base, spread) in spreads.items():
        noise = np.random.default_rng([zlib.crc32(name.encode()), seed]).standard_normal(out[name].shape)
        drawn = base * np.exp(spread * noise) if base else spread * noise
        out[name] = jnp.asarray(drawn.astype(out[name].dtype))
    for name, factor in factors.items():
        out[name] = (out[name] * factor).astype(out[name].dtype)
    return out
```

```python
from contextlib import ExitStack

import concourse.bass as bass
from concourse import mybir

F32 = mybir.dt.float32
BF16 = mybir.dt.bfloat16
I32 = mybir.dt.int32
U32 = mybir.dt.uint32
ALU = mybir.AluOpType
ACT = mybir.ActivationFunctionType
AX_X = mybir.AxisListType.X

P = 128
N = 2500
F = 512
NB = -(-N // P)
TAIL = N - (NB - 1) * P
HEADS = 8
D = F // HEADS
CH = F // P
E = 40000
EP = 125
T = E // EP
GT = 4
GROUPS = T // GT
Q = 336
STRIPS = P // HEADS
SQ = Q // STRIPS
CAP = Q * P
DUMP = (P - EP) * T
RW = 12
TW = F + 2 * HEADS
CPB = 16
SLOPE = 0.2
EPS = 1e-5
BIG = 1.0e30
EXPERTS = 8
HID = 256
HCH = HID // P
NG = 5
assert Q * P >= E + NB * (P - 1) and NB * P == NG * 512 and EP * T == E and GROUPS * GT == T


def bcast(ap, axis, n):
    ap = ap.unsqueeze(axis)
    shape = list(ap.shape)
    shape[axis] = n
    return ap.to_broadcast(shape)


class Space:

    def __init__(self, nc, ctx):
        self.nc, self.ctx = nc, ctx

    def sb(self, name, shape, dt=F32):
        return self.ctx.enter_context(self.nc.sbuf_tensor(name, shape, dt))

    def ps(self, name, shape, dt=F32):
        return self.ctx.enter_context(self.nc.psum_tensor(name, shape, dt))


def chained(eng, sem):
    count = [0]

    def link(ins):
        count[0] += 1
        ins.then_inc(sem, 1)
        eng.wait_ge(sem, count[0])

    return link


def build_constants(nc, k, sem):
    made = sem("constants_made")
    block_ctx = nc.Block()
    with block_ctx as block:
        @block.gpsimd
        def _(pool):
            link = chained(pool, made)
            link(pool.iota(k["iota_i"][:, :], pattern=[[1, P]], base=0, channel_multiplier=0))
            link(pool.tensor_copy(k["iota"][:, :], k["iota_i"][:, :]))
            link(pool.memset(k["ident"][:, :], 0.0))
            link(pool.affine_select(out=k["ident"][:, :], in_=k["ident"][:, :], compare_op=ALU.not_equal,
                                    fill=1.0, base=0, pattern=[[-1, P]], channel_multiplier=1))
            link(pool.tensor_copy(k["ident_bf"][:, :], k["ident"][:, :]))
            link(pool.memset(k["ones"][:, :], 1.0))
            link(pool.affine_select(out=k["before"][:, :], in_=k["ones"][:, :], compare_op=ALU.is_gt,
                                    fill=0.0, base=0, pattern=[[1, P]], channel_multiplier=-1))
            link(pool.memset(k["shift"][:, :], 0.0))
            link(pool.affine_select(out=k["shift"][:, :], in_=k["shift"][:, :], compare_op=ALU.not_equal,
                                    fill=1.0, base=HEADS, pattern=[[-1, P]], channel_multiplier=1))


def rank_edges(nc, k, sem, src, dst, sorted_d):
    with ExitStack() as ctx:
        s = Space(nc, ctx)
        src_i = s.sb("src_i", [P, T], I32)
        dst_i = s.sb("dst_i", [P, T], I32)
        blk_i = s.sb("blk_i", [P, T], I32)
        loc_i = s.sb("loc_i", [P, T], I32)
        blk = s.sb("blk", [P, T])
        loc = s.sb("loc", [P, T])
        oh_loc = s.sb("oh_loc", [P, T, P], BF16)
        oh_blk = s.sb("oh_blk", [P, T, NB], BF16)
        first = s.sb("first", [P, NB, T + 1])
        same = s.sb("same", [P, NB, T + 1], BF16)
        total = s.sb("total", [P, NB])
        bi = s.sb("bi", [P, NB], I32)
        nt = s.sb("nt", [P, NB])
        ends = s.sb("ends", [P, NB])
        start = s.sb("start", [P, NB])
        oh_t = s.sb("oh_t", [P, 2, GT, P])
        earlier = s.sb("earlier", [P, 2, GT, P], BF16)
        picked = s.sb("picked", [P, 2, GT, NB])
        pos = s.sb("pos", [P, T])
        dump_i = s.sb("dump_i", [P, T], I32)
        dump = s.sb("dump", [P, T])
        fill = s.sb("fill", [P, 21, RW], U32)
        counts_ps = s.ps("counts_ps", [P, 2, 512])
        tr_ps = s.ps("tr_ps", [P, 2, 1024], BF16)
        same_ps = s.ps("same_ps", [P, 2, GT, P])
        look_ps = s.ps("look_ps", [P, 2, 512])

        loaded, cleared, edge_ids = sem("edges_loaded"), sem("edges_cleared"), sem("edge_ids")
        valid, hot, counted, kept = sem("edges_valid"), sem("one_hots"), sem("tiles_counted"), sem("counts_kept")
        tot, totps, chain = sem("totals"), sem("totals_ps"), sem("rank_chain")
        firsts = sem("firsts_ready")
        tr_done, oht_ready, same_done = sem("rank_tr"), sem("rank_oht"), sem("rank_same")
        early_ready, look_done, pos_done, mul_done = sem("rank_early"), sem("rank_look"), sem("rank_pos"), sem("rank_mul")
        dumped, filled, fill_out = sem("dump_ready"), sem("fill_ready"), sem("fill_out")
        pool_chain = sem("rank_pool_chain")

        with nc.Block() as block:
            @block.sync
            def _(sp):
                sp.wait_ge(cleared, 2)
                sp.dma_start(src_i[0:EP, :], src.rearrange("(p t) -> p t", t=T)).then_inc(loaded, 16)
                sp.dma_start(dst_i[0:EP, :], dst.rearrange("(p t) -> p t", t=T)).then_inc(loaded, 16)
                sp.wait_ge(filled, 3)
                rows = sorted_d[0:CAP, :].rearrange("(p g t) w -> p g t w", p=P, t=21)
                for g in range(Q // 21):
                    sp.dma_start(rows[:, g, :, :], fill[:, :, :]).then_inc(fill_out, 16)
                sp.wait_ge(fill_out, 16 * (Q // 21))

            @block.gpsimd
            def _(pool):
                pool.memset(fill[:, :, :], 0).then_inc(filled, 1)
                pool.wait_ge(filled, 1)
                pool.memset(fill[:, :, HEADS:HEADS + 1], 4096).then_inc(filled, 2)
                pool.iota(dump_i[:, :], pattern=[[1, T]], base=CAP - EP * T, channel_multiplier=T).then_inc(pool_chain, 1)
                pool.wait_ge(pool_chain, 1)
                pool.tensor_copy(dump[:, :], dump_i[:, :]).then_inc(pool_chain, 1)
                pool.wait_ge(pool_chain, 2)
                pool.affine_select(out=dump[:, :], in_=dump[:, :], compare_op=ALU.is_ge, fill=0.0,
                                   base=-EP, pattern=[[0, T]], channel_multiplier=1).then_inc(dumped, 1)
                pool.wait_ge(edge_ids, 4)
                pool.affine_select(out=blk[:, :], in_=blk[:, :], compare_op=ALU.is_ge, fill=-1.0,
                                   base=EP - 1, pattern=[[0, T]], channel_multiplier=-1).then_inc(valid, 1)
                pool.affine_select(out=loc[:, :], in_=loc[:, :], compare_op=ALU.is_ge, fill=-1.0,
                                   base=EP - 1, pattern=[[0, T]], channel_multiplier=-1).then_inc(valid, 1)
                pool.memset(same[:, :, :], 1.0).then_inc(pool_chain, 1)
                pool.wait_ge(pool_chain, 3)
                pool.memset(same[:, :, 0:1], 0.0).then_inc(firsts, 1)

            @block.vector
            def _(dve):
                link = chained(dve, chain)
                dve.memset(src_i[:, :], 0).then_inc(cleared, 1)
                dve.memset(dst_i[:, :], 0).then_inc(cleared, 1)
                dve.wait_ge(loaded, 32)
                dve.tensor_scalar(blk_i[:, :], src_i[:, :], 7, None, ALU.logical_shift_right).then_inc(edge_ids, 1)
                dve.tensor_scalar(loc_i[:, :], src_i[:, :], P - 1, None, ALU.bitwise_and).then_inc(edge_ids, 1)
                dve.wait_ge(edge_ids, 2)
                dve.tensor_copy(blk[:, :], blk_i[:, :]).then_inc(edge_ids, 1)
                dve.tensor_copy(loc[:, :], loc_i[:, :]).then_inc(edge_ids, 1)
                link(dve.tensor_scalar(k["ids"][:, :, 0], src_i[:, :], 1, None, ALU.add))
                link(dve.tensor_copy(k["ids"][:, :, 1], dst_i[:, :]))
                link(dve.tensor_copy(k["ends"][:, :, 0], src_i[:, :]))
                link(dve.tensor_copy(k["ends"][:, :, 1], dst_i[:, :]))
                dve.wait_ge(valid, 2)
                dve.tensor_tensor(oh_blk[:, :, :], bcast(blk[:, :], 2, NB), bcast(k["iota"][:, 0:NB], 1, T),
                                  ALU.is_equal).then_inc(hot, 1)
                for c in range(10):
                    t0, t1 = c * T // 10, (c + 1) * T // 10
                    dve.tensor_tensor(oh_loc[:, t0:t1, :], bcast(loc[:, t0:t1], 2, P),
                                      bcast(k["iota"][:, :], 1, t1 - t0), ALU.is_equal).then_inc(hot, 1)
                dve.wait_ge(kept, T // CPB)
                dve.tensor_reduce(total[:, :], first[:, :, 1:T + 1], AX_X, ALU.add).then_inc(tot, 1)
                dve.wait_ge(totps, 1)
                link(dve.tensor_scalar(bi[:, :], look_ps[:, 1, 0:NB], float(P - 1), None, ALU.add))
                link(dve.tensor_scalar(bi[:, :], bi[:, :], 7, None, ALU.logical_shift_right))
                link(dve.tensor_copy(nt[:, :], bi[:, :]))
                link(dve.tensor_tensor_scan(ends[:, :], k["ones"][:, 0:NB], nt[:, :], 0.0, ALU.mult, ALU.add))
                link(dve.tensor_tensor(start[:, :], ends[:, :], nt[:, :], ALU.subtract))
                link(dve.tensor_copy(k["first_tile"][:, :], start[:, :]))
                link(dve.scalar_tensor_tensor(first[:, :, 0], start[:, :], float(P), look_ps[:, 0, 0:NB],
                                              ALU.mult, ALU.add))
                dve.wait_ge(firsts, 1)
                flat = first[:, :, :].rearrange("p b t -> p (b t)")
                dve.tensor_tensor_scan(flat, same[:, :, :].rearrange("p b t -> p (b t)"), flat, 0.0,
                                       ALU.mult, ALU.add).then_inc(firsts, 1)

                def mark_earlier(g, j):
                    dve.wait_ge(same_done, g + 1)
                    dve.tensor_tensor(earlier[:, j, :, :], same_ps[:, j, :, :],
                                      bcast(k["before"][:, :], 1, GT), ALU.mult).then_inc(early_ready, 1)

                def pick(g, j):
                    dve.wait_ge(look_done, g + 1)
                    dve.tensor_tensor(picked[:, j, :, :], look_ps[:, j, 0:GT * NB].rearrange("p (t b) -> p t b", t=GT),
                                      oh_blk[:, bass.ds(g * GT, GT), :], ALU.mult).then_inc(mul_done, 1)
                    dve.wait_ge(mul_done, g + 1)
                    dve.tensor_reduce(pos[:, bass.ds(g * GT, GT)], picked[:, j, :, :], AX_X, ALU.add).then_inc(pos_done, 1)

                mark_earlier(0, 0)
                mark_earlier(1, 1)
                pick(0, 0)
                with dve.Fori(1, GROUPS // 2) as i:
                    for j in range(2):
                        dve.wait_ge(look_done, 2 * i + j - 1)
                        mark_earlier(2 * i + j, j)
                        pick(2 * i + j - 1, 1 - j)
                pick(GROUPS - 1, 1)
                dve.wait_ge(pos_done, GROUPS)
                link(dve.tensor_copy(blk_i[:, :], pos[:, :]))
                link(dve.tensor_scalar(loc_i[:, :], blk_i[:, :], P - 1, None, ALU.bitwise_and))
                link(dve.tensor_scalar(blk_i[:, :], blk_i[:, :], 7, None, ALU.logical_shift_right))
                link(dve.tensor_copy(blk[:, :], blk_i[:, :]))
                link(dve.tensor_copy(loc[:, :], loc_i[:, :]))
                link(dve.scalar_tensor_tensor(pos[:, :], loc[:, :], float(Q), blk[:, :], ALU.mult, ALU.add))
                dve.wait_ge(dumped, 1)
                link(dve.tensor_tensor(pos[:, :], pos[:, :], dump[:, :], ALU.add))
                link(dve.tensor_copy(k["ends"][:, :, 2], pos[:, :]))

            @block.scalar
            def _(act):
                for c in range(T // CPB):
                    act.wait_ge(counted, c + 1)
                    act.copy(first[:, :, 1 + c * CPB:1 + (c + 1) * CPB].rearrange("p b t -> p t b"),
                             counts_ps[:, c % 2, 0:CPB * NB].rearrange("p (t b) -> p t b", b=NB)).then_inc(kept, 1)

                def keep(g, j):
                    act.wait_ge(tr_done, g + 1)
                    act.copy(oh_t[:, j, :, :], tr_ps[:, j, 0:GT * P].rearrange("p (t e) -> p t e", t=GT)).then_inc(oht_ready, 1)

                keep(0, 0)
                keep(1, 1)
                with act.Fori(1, GROUPS // 2) as i:
                    for j in range(2):
                        act.wait_ge(look_done, 2 * i + j - 1)
                        keep(2 * i + j, j)

            @block.tensor
            def _(pe):
                def count(c, j):
                    for t in range(CPB):
                        last = pe.matmul(counts_ps[:, j, t * NB:(t + 1) * NB],
                                         oh_loc[:, bass.ds(c * CPB + t, 1), :].rearrange("p a b -> p (a b)"),
                                         oh_blk[:, bass.ds(c * CPB + t, 1), :].rearrange("p a b -> p (a b)"),
                                         start=True, stop=True)
                    last.then_inc(counted, 1)

                for c in range(2):
                    pe.wait_ge(hot, 2 + c // 2)
                    count(c, c)
                with pe.Fori(1, T // CPB // 2) as i:
                    pe.wait_ge(hot, i + 2)
                    for j in range(2):
                        pe.wait_ge(kept, 2 * i + j - 1)
                        count(2 * i + j, j)
                pe.wait_ge(tot, 1)
                pe.matmul(look_ps[:, 0, 0:NB], k["before"][:, :], total[:, :], start=True, stop=True)
                pe.matmul(look_ps[:, 1, 0:NB], k["ones"][:, :], total[:, :], start=True, stop=True).then_inc(totps, 1)
                pe.wait_ge(firsts, 2)

                def turn(g, j):
                    for t in range(GT):
                        last = pe.transpose(tr_ps[:, j, t * P:(t + 1) * P],
                                            oh_loc[:, bass.ds(g * GT + t, 1), :].rearrange("p a b -> p (a b)"),
                                            k["ident_bf"][:, :])
                    last.then_inc(tr_done, 1)

                def compare(g, j):
                    pe.wait_ge(oht_ready, g + 1)
                    for t in range(GT):
                        last = pe.matmul(same_ps[:, j, t, :], oh_t[:, j, t, :], oh_t[:, j, t, :], start=True, stop=True)
                    last.then_inc(same_done, 1)

                def look(g, j):
                    pe.wait_ge(early_ready, g + 1)
                    for t in range(GT):
                        out = look_ps[:, j, t * NB:(t + 1) * NB]
                        pe.matmul(out, earlier[:, j, t, :], oh_blk[:, bass.ds(g * GT + t, 1), :].rearrange("p a b -> p (a b)"),
                                  start=True, stop=False)
                        last = pe.matmul(out, oh_t[:, j, t, :], first[:, :, bass.ds(g * GT + t, 1)].rearrange("p b a -> p (b a)"),
                                         start=False, stop=True)
                    last.then_inc(look_done, 1)

                turn(0, 0)
                turn(1, 1)
                compare(0, 0)
                with pe.Fori(1, GROUPS // 2) as i:
                    for j in range(2):
                        g = 2 * i + j
                        pe.wait_ge(oht_ready, g - 1)
                        turn(g, j)
                        if j == 1:
                            pe.wait_ge(early_ready, g - 2)
                        compare(g - 1, 1 - j)
                        look(g - 2, j)
                compare(GROUPS - 1, 1)
                look(GROUPS - 2, 0)
                look(GROUPS - 1, 1)


def normalise_stats(dve, act_ready, act_done, link, mv, var, root, rstd):
    link(dve.tensor_scalar(var, mv[:, :, 1], EPS, None, ALU.add))
    dve.nop().then_inc(act_ready, 1)
    dve.wait_ge(act_done, 1)
    link(dve.reciprocal(rstd, root))
    link(dve.tensor_tensor(rstd, rstd, var, ALU.mult))
    link(dve.tensor_tensor(root, rstd, root, ALU.add))
    link(dve.tensor_scalar(root, root, 0.5, None, ALU.mult))
    link(dve.reciprocal(rstd, root))


def project(nc, k, sem, x, we, wr, a, table_d, he_d):
    x_sb = k["x_sb"]
    with ExitStack() as ctx:
        s = Space(nc, ctx)
        w_e = s.sb("w_e", [P, CH, F])
        w_r = s.sb("w_r", [P, CH, F])
        a_all = s.sb("a_all", [P, HEADS, 5 * D])
        half = s.sb("half", [P, HEADS, D])
        prod = s.sb("prod", [P, CH, HEADS, D])
        lin = s.sb("lin", [P, CH, 2 * HEADS])
        dif = s.sb("dif", [P, CH, HEADS])
        st = s.sb("st", [P, NB, 6])
        mv = s.sb("mv", [P, NB, 2])
        var = s.sb("var", [P, NB])
        root = s.sb("root", [P, NB])
        rstd = s.sb("rstd", [P, NB])
        xn = s.sb("xn", [P, 2, F])
        xt = s.sb("xt", [P, 2, CH, P])
        row = s.sb("row", [P, 2, TW])
        he = s.sb("he", [P, 2, F])
        sq = s.sb("sq", [P, 2, HEADS, D])
        sqa = s.sb("sqa", [P, 2, HEADS, D])
        own = s.sb("own", [P, 2, HEADS])
        t_ps = s.ps("t_ps", [P, 2, F])
        r_ps = s.ps("r_ps", [P, 2, F])
        e_ps = s.ps("e_ps", [P, 2, F])
        l_ps = s.ps("l_ps", [P, 2, 512])

        xin = [sem(f"x_in{c}") for c in range(5)]
        win, ain, tailz = sem("weights_in"), sem("a_in"), sem("tail_zero")
        stats, chain, rready, rdone = sem("stats"), sem("project_chain"), sem("var_ready"), sem("root_done")
        linr, xn_ready, tp, xt_ready, proj = sem("lin_ready"), sem("xn_ready"), sem("x_turned"), sem("xt_ready"), sem("projected")
        he_ready, sq_ready, row_ready, sqa_ready = sem("he_ready"), sem("sq_ready"), sem("row_ready"), sem("sqa_ready")
        hr_copied, own_ready, pq = sem("hr_copied"), sem("own_ready"), sem("pq_ready")
        row_out = [sem(f"row_out{j}") for j in range(2)]
        he_out = [sem(f"he_out{j}") for j in range(2)]

        with nc.Block() as block:
            @block.sync
            def _(sp):
                for c in range(4):
                    sp.dma_start(x_sb[:, 4 * c:4 * c + 4, :],
                                 x[512 * c:512 * (c + 1), :].rearrange("(b p) f -> p b f", p=P)).then_inc(xin[c], 16)
                sp.dma_start(x_sb[:, 16:NB - 1, :],
                             x[2048:(NB - 1) * P, :].rearrange("(b p) f -> p b f", p=P)).then_inc(xin[4], 16)
                sp.wait_ge(tailz, 1)
                sp.dma_start(x_sb[0:TAIL, NB - 1, :], x[(NB - 1) * P:N, :]).then_inc(xin[4], 16)

                def store(b, j):
                    sp.wait_ge(row_ready, b + 1)
                    sp.dma_start(table_d[bass.ds(b * P, P), :], row[:, j, :]).then_inc(row_out[j], 16)
                    sp.wait_ge(he_ready, b + 1)
                    sp.dma_start(he_d[bass.ds(b * P, P), :], he[:, j, :]).then_inc(he_out[j], 16)

                with sp.Fori(0, NB // 2) as i:
                    for j in range(2):
                        store(2 * i + j, j)
                for j in range(2):
                    sp.wait_ge(row_out[j], 16 * NB // 2)
                    sp.wait_ge(he_out[j], 16 * NB // 2)

            @block.scalar
            def _(act):
                act.dma_start(a_all[:, :, :], a.partition_broadcast(P)).then_inc(ain, 16)
                for c in range(CH):
                    act.dma_start(w_e[:, c, :].rearrange("p (h d) -> p h d", h=HEADS),
                                  we[:, c * P:(c + 1) * P, :].rearrange("h p d -> p h d")).then_inc(win, 16)
                    act.dma_start(w_r[:, c, :].rearrange("p (h d) -> p h d", h=HEADS),
                                  wr[:, c * P:(c + 1) * P, :].rearrange("h p d -> p h d")).then_inc(win, 16)
                act.wait_ge(rready, 1)
                act.activation(root[:, :], var[:, :], ACT.Sqrt).then_inc(rdone, 1)

                def turned(b, j):
                    act.wait_ge(tp, b + 1)
                    act.copy(xt[:, j, :, :], t_ps[:, j, :].rearrange("p (c n) -> p c n", c=CH)).then_inc(xt_ready, 1)

                def keep(b, j):
                    act.wait_ge(proj, b + 1)
                    act.activation(sq[:, j, :, :].rearrange("p h d -> p (h d)"), r_ps[:, j, :], ACT.Square).then_inc(sq_ready, 1)
                    act.copy(he[:, j, :], e_ps[:, j, :]).then_inc(he_ready, 1)

                turned(0, 0)
                turned(1, 1)
                keep(0, 0)

                def pair(i):
                    for j in range(2):
                        b = 2 * i + j
                        act.wait_ge(proj, b - 1)
                        turned(b, j)
                        if not (isinstance(b, int) and b == 2):
                            act.wait_ge(he_out[1 - j], 16 * (i + j) - 16)
                            act.wait_ge(row_ready, b - 2)
                        keep(b - 1, 1 - j)

                pair(1)
                with act.Fori(2, NB // 2) as i:
                    pair(i)
                act.wait_ge(he_out[1], 16 * (NB // 2 - 1))
                act.wait_ge(row_ready, NB - 2)
                keep(NB - 1, 1)

            @block.tensor
            def _(pe):
                def turn(b, j):
                    pe.wait_ge(xn_ready, b + 1)
                    for c in range(CH):
                        last = pe.transpose(t_ps[:, j, c * P:(c + 1) * P], xn[:, j, c * P:(c + 1) * P], k["ident"][:, :])
                    last.then_inc(tp, 1)

                def multiply(b, j):
                    pe.wait_ge(xt_ready, b + 1)
                    for out, w in ((r_ps[:, j, :], w_r), (e_ps[:, j, :], w_e), (l_ps[:, j, 0:2 * HEADS], lin)):
                        for c in range(CH):
                            last = pe.matmul(out, xt[:, j, c, :], w[:, c, :], start=(c == 0), stop=(c == CH - 1))
                    last.then_inc(proj, 1)

                turn(0, 0)
                turn(1, 1)
                pe.wait_ge(win, 32 * CH)
                pe.wait_ge(linr, 1)
                multiply(0, 0)

                def pair(i):
                    for j in range(2):
                        b = 2 * i + j
                        pe.wait_ge(xt_ready, b - 1)
                        turn(b, j)
                        if not (isinstance(b, int) and b == 2):
                            pe.wait_ge(row_ready, b - 2)
                            pe.wait_ge(he_ready, b - 2)
                        multiply(b - 1, 1 - j)

                pair(1)
                with pe.Fori(2, NB // 2) as i:
                    pair(i)
                pe.wait_ge(row_ready, NB - 2)
                pe.wait_ge(he_ready, NB - 2)
                multiply(NB - 1, 1)

            @block.vector
            def _(dve):
                link = chained(dve, chain)
                dve.memset(x_sb[:, NB - 1, :], 0.0).then_inc(tailz, 1)
                for b in range(NB):
                    if b % 4 == 0:
                        dve.wait_ge(xin[b // 4], 16 if b < 16 else 32)
                    dve.bn_stats(st[:, b, :], x_sb[:, b, :]).then_inc(stats, 1)
                dve.wait_ge(stats, NB)
                for b in range(NB):
                    dve.bn_aggr(mv[:, b, :], st[:, b, :]).then_inc(stats, 1)
                dve.wait_ge(stats, 2 * NB)
                normalise_stats(dve, rready, rdone, link, mv, var[:, :], root[:, :], rstd[:, :])

                def normalise(b, j):
                    dve.tensor_scalar(xn[:, j, :], x_sb[:, bass.ds(b, 1), :].rearrange("p a f -> p (a f)"),
                                      mv[:, bass.ds(b, 1), 0], rstd[:, bass.ds(b, 1)],
                                      ALU.subtract, ALU.mult).then_inc(xn_ready, 1)

                def finish(b, j):
                    dve.wait_ge(sq_ready, b + 1)
                    dve.tensor_copy(row[:, j, 0:F], r_ps[:, j, :]).then_inc(hr_copied, 1)
                    dve.tensor_tensor(sqa[:, j, :, :], sq[:, j, :, :], half[:, :, :], ALU.mult).then_inc(sqa_ready, 1)
                    dve.wait_ge(sqa_ready, b + 1)
                    dve.tensor_reduce(own[:, j, :], sqa[:, j, :, :], AX_X, ALU.add).then_inc(own_ready, 1)
                    dve.wait_ge(own_ready, b + 1)
                    dve.wait_ge(hr_copied, b + 1)
                    dve.tensor_tensor(row[:, j, F:TW].rearrange("p (a h) -> p a h", a=2),
                                      l_ps[:, j, 0:2 * HEADS].rearrange("p (a h) -> p a h", a=2),
                                      bcast(own[:, j, :], 1, 2), ALU.add).then_inc(row_ready, 1)

                normalise(0, 0)
                normalise(1, 1)
                dve.wait_ge(win, 32 * CH)
                dve.wait_ge(ain, 16)
                w4e = w_e[:, :, :].rearrange("p c (h d) -> p c h d", h=HEADS)
                w4r = w_r[:, :, :].rearrange("p c (h d) -> p c h d", h=HEADS)
                for w, part, out in ((w4r, 2, dif[:, :, :]), (w4e, 0, lin[:, :, 0:HEADS]), (w4e, 1, lin[:, :, HEADS:])):
                    link(dve.tensor_tensor(prod[:, :, :, :], w, bcast(a_all[:, :, part * D:(part + 1) * D], 1, CH), ALU.mult))
                    link(dve.tensor_reduce(out, prod[:, :, :, :], AX_X, ALU.add))
                link(dve.tensor_scalar(half[:, :, :], a_all[:, :, 4 * D:], 0.5, None, ALU.mult))
                dve.tensor_tensor(lin[:, :, 0:HEADS], lin[:, :, 0:HEADS], dif[:, :, :], ALU.subtract).then_inc(chain, 1)
                dve.tensor_tensor(lin[:, :, HEADS:], lin[:, :, HEADS:], dif[:, :, :], ALU.add).then_inc(linr, 1)
                finish(0, 0)

                def pair(i):
                    for j in range(2):
                        b = 2 * i + j
                        dve.wait_ge(tp, b - 1)
                        normalise(b, j)
                        if not (isinstance(b, int) and b == 2):
                            dve.wait_ge(row_out[1 - j], 16 * (i + j) - 16)
                        finish(b - 1, 1 - j)

                pair(1)
                with dve.Fori(2, NB // 2) as i:
                    pair(i)
                dve.wait_ge(row_out[1], 16 * (NB // 2 - 1))
                finish(NB - 1, 1)


def score_edges(nc, k, sem, a, table_d, sorted_d):
    SL, AHEAD, LAG = 8, 5, 2
    with ExitStack() as ctx:
        s = Space(nc, ctx)
        ix = s.sb("ix", [P, SL, 3], U32)
        gs = s.sb("gs", [P, SL, TW])
        gd = s.sb("gd", [P, SL, TW])
        dif = s.sb("diff", [P, 2, F])
        ab = s.sb("ab", [P, 2, CH, P])
        sq = s.sb("dsq", [P, 2, CH, P])
        rowt = s.sb("rowt", [P, SL, RW], U32)
        sc = s.sb("sc", [P, 2, HEADS])
        raw = s.sb("raw_a", [P, 2, CH])
        wab = s.sb("wab", [P, CH, HEADS])
        wsq = s.sb("wsq", [P, CH, HEADS])
        d_ps = s.ps("d_ps", [P, 2, F])
        s_ps = s.ps("s_ps", [P, 2, 512])

        ain, az, wready, chain = sem("score_a_in"), sem("score_a_zero"), sem("score_weights"), sem("score_chain")
        ixr = sem("indices_ready")
        got = [sem(f"rows_in{j}") for j in range(SL)]
        out = [sem(f"scores_out{j}") for j in range(SL)]
        dready, dturned, abr, sqr, red = sem("diff_ready"), sem("diff_turned"), sem("abs_ready"), sem("dsq_ready"), sem("reduced")
        s1, s2, scored, idr = sem("score_p"), sem("score_pq"), sem("scored"), sem("row_ids")

        with nc.Block() as block:
            @block.sync
            def _(sp):
                for half in range(2):
                    for n, part in enumerate((3, 4)):
                        sp.dma_start(raw[half * D:(half + 1) * D, n, :],
                                     a.rearrange("(c t) f -> f c t", t=2)[part * D:(part + 1) * D, :, half],
                                     allow_slow_non_contiguous=True
                                     ).then_inc(ain, 16)

            @block.gpsimd
            def _(pool):
                def gather(t, j):
                    pool.tensor_copy(ix[:, j, :], k["ends"][:, bass.ds(t, 1), :].rearrange("p a w -> p (a w)")).then_inc(ixr, 1)
                    pool.wait_ge(ixr, t + 1)
                    pool.nop(nofuse=True)
                    pool.indirect_dma_start(gs[:, j, :], None, table_d,
                                            bass.IndirectOffsetOnAxis(ap=ix[:, j, 0:1], axis=0)).then_inc(got[j], 16)
                    pool.indirect_dma_start(gd[:, j, :], None, table_d,
                                            bass.IndirectOffsetOnAxis(ap=ix[:, j, 1:2], axis=0)).then_inc(got[j], 16)

                def scatter(t, j):
                    pool.wait_ge(scored, t + 1)
                    pool.nop(nofuse=True)
                    pool.indirect_dma_start(sorted_d, bass.IndirectOffsetOnAxis(ap=ix[:, j, 2:3], axis=0),
                                            rowt[:, j, :], None).then_inc(out[j], 16)

                def step(t, j, i):
                    scatter(t, j)
                    if isinstance(t, int) and t + AHEAD >= T:
                        return
                    if not (isinstance(t, int) and t + AHEAD < SL):
                        pool.wait_ge(out[(j + AHEAD) % SL], 16 * (i + (j >= SL - AHEAD)))
                    gather(t + AHEAD, (j + AHEAD) % SL)

                for j in range(AHEAD):
                    gather(j, j)
                for j in range(SL):
                    step(j, j, 0)
                with pool.Fori(1, T // SL - 1) as i:
                    for j in range(SL):
                        step(SL * i + j, j, i)
                for j in range(SL):
                    step(T - SL + j, j, T // SL - 1)
                for j in range(SL):
                    pool.wait_ge(out[j], 16 * (T // SL))

            @block.vector
            def _(dve):
                link = chained(dve, chain)
                dve.memset(wab[:, :, :], 0.0).then_inc(az, 1)
                dve.memset(wsq[:, :, :], 0.0).then_inc(az, 1)
                dve.memset(rowt[:, :, :], 0).then_inc(az, 1)
                dve.wait_ge(az, 3)
                dve.wait_ge(ain, 64)
                for c in range(CH):
                    for half in range(2):
                        ps = slice(half * D, (half + 1) * D)
                        dve.tensor_copy(wab[ps, c, 2 * c + half:2 * c + half + 1], raw[ps, 0, c:c + 1]).then_inc(wready, 1)
                        dve.tensor_scalar(wsq[ps, c, 2 * c + half:2 * c + half + 1], raw[ps, 1, c:c + 1], -0.5, None,
                                          ALU.mult).then_inc(wready, 1)

                def subtract(t, j, j2, n):
                    dve.wait_ge(got[j], 32 * n + 32)
                    dve.tensor_tensor(dif[:, j2, :], gd[:, j, 0:F], gs[:, j, 0:F], ALU.subtract).then_inc(dready, 1)

                def score(t, j, j2):
                    dve.wait_ge(red, t + 1)
                    dve.tensor_tensor(sc[:, j2, :], s_ps[:, j2, 0:HEADS], gs[:, j, F:F + HEADS], ALU.add).then_inc(s1, 1)
                    dve.wait_ge(s1, t + 1)
                    dve.tensor_tensor(sc[:, j2, :], sc[:, j2, :], gd[:, j, F + HEADS:TW], ALU.add).then_inc(s2, 1)
                    dve.tensor_copy(rowt[:, j, HEADS:HEADS + 2],
                                    k["ids"][:, bass.ds(t, 1), :].rearrange("p a w -> p (a w)")).then_inc(idr, 1)
                    dve.wait_ge(s2, t + 1)
                    dve.wait_ge(idr, t + 1)
                    dve.scalar_tensor_tensor(rowt[:, j, 0:HEADS].bitcast(F32), sc[:, j2, :], SLOPE, sc[:, j2, :],
                                             ALU.mult, ALU.max).then_inc(scored, 1)

                for t in range(SL):
                    if t >= LAG:
                        score(t - LAG, t - LAG, t % 2)
                    subtract(t, t, t % 2, 0)
                with dve.Fori(1, T // SL) as i:
                    for j in range(SL):
                        t = SL * i + j
                        score(t - LAG, (j - LAG) % SL, j % 2)
                        subtract(t, j, j % 2, i)
                for t in range(T - LAG, T):
                    score(t, t % SL, t % 2)

            @block.tensor
            def _(pe):
                def turn(t, j2):
                    pe.wait_ge(dready, t + 1)
                    for c in range(CH):
                        last = pe.transpose(d_ps[:, j2, c * P:(c + 1) * P], dif[:, j2, c * P:(c + 1) * P], k["ident"][:, :])
                    last.then_inc(dturned, 1)

                def reduce(t, j2):
                    pe.wait_ge(abr, t + 1)
                    for c in range(CH):
                        pe.matmul(s_ps[:, j2, 0:HEADS], ab[:, j2, c, :], wab[:, c, :], start=(c == 0), stop=False)
                    pe.wait_ge(sqr, t + 1)
                    for c in range(CH):
                        last = pe.matmul(s_ps[:, j2, 0:HEADS], sq[:, j2, c, :], wsq[:, c, :], start=False, stop=(c == CH - 1))
                    last.then_inc(red, 1)

                pe.wait_ge(wready, 4 * CH)
                turn(0, 0)
                turn(1, 1)
                reduce(0, 0)
                with pe.Fori(1, T // 2) as i:
                    for j in range(2):
                        t = 2 * i + j
                        pe.wait_ge(sqr, t - 1)
                        turn(t, j)
                        reduce(t - 1, 1 - j)
                reduce(T - 1, 1)

            @block.scalar
            def _(act):
                def features(t, j2):
                    act.wait_ge(dturned, t + 1)
                    act.activation(ab[:, j2, :, :].rearrange("p c e -> p (c e)"), d_ps[:, j2, :], ACT.Abs).then_inc(abr, 1)
                    act.activation(sq[:, j2, :, :].rearrange("p c e -> p (c e)"), d_ps[:, j2, :], ACT.Square).then_inc(sqr, 1)

                features(0, 0)
                features(1, 1)
                with act.Fori(1, T // 2) as i:
                    for j in range(2):
                        act.wait_ge(red, 2 * i + j - 1)
                        features(2 * i + j, j)


def edge_softmax(nc, k, sem, sorted_d):
    L = SQ * P
    with ExitStack() as ctx:
        s = Space(nc, ctx)
        rows = s.sb("rows", [P, Q, RW], U32)
        keys = s.sb("keys", [P, SQ, STRIPS, HEADS])
        scores = s.sb("scores", [P, SQ, STRIPS, HEADS])
        keyq = s.sb("keyq", [P, Q])
        cmp = s.sb("cmp", [P, Q, NB - 1], BF16)
        qi = s.sb("qi", [P, Q], I32)
        qf = s.sb("qf", [P, Q])
        tb = s.sb("tb", [P, Q])
        al = s.sb("al", [P, L])
        ky = s.sb("ky", [P, L])
        cont = s.sb("cont", [P, L + 1])
        pen = s.sb("pen", [P, L + 1])
        fw = s.sb("fw", [P, L])
        top = s.sb("top", [P, L])
        ex = s.sb("ex", [P, L])
        den = s.sb("den", [P, L])
        whole = s.sb("whole", [P, 4])
        edge = s.sb("edge", [P, 1])
        carry = s.sb("carry", [P, 1])
        hm = s.sb("hm", [1, 2, HEADS, STRIPS])
        run = s.sb("run", [1, HEADS, STRIPS])
        cin = s.sb("cin", [1, STRIPS, HEADS])
        shift_t = s.sb("shift_t", [P, P])
        a_ps = s.ps("a_ps", [P, 2, 512])
        k_ps = s.ps("k_ps", [P, 2, 512])
        c_ps = s.ps("c_ps", [P, 4, 512])

        rin, qr, kready, chain = sem("rows_in"), sem("tile_numbers"), sem("keys_ready"), sem("softmax_chain")
        kready0, scready = sem("key_read"), sem("scores_laid")
        ta, tk, ea, ek = sem("scores_turned"), sem("keys_turned"), sem("scores_kept"), sem("keys_kept")
        ask, answer = sem("carry_ask"), sem("carry_answer")
        sub, exped, att_ready, tb_done, tkept = sem("shifted"), sem("exped"), sem("att_ready"), sem("att_turned"), sem("att_kept")
        groups = [range(g, min(g + 4, SQ)) for g in range(0, SQ, 4)]

        with nc.Block() as block:
            @block.sync
            def _(sp):
                sp.dma_start(rows[:, :, :], sorted_d[0:CAP, :].rearrange("(p q) w -> p q w", p=P)).then_inc(rin, 16)

            @block.gpsimd
            def _(pool):
                pool.iota(qi[:, :], pattern=[[1, Q]], base=0, channel_multiplier=0).then_inc(qr, 1)
                pool.wait_ge(qr, 1)
                pool.tensor_copy(qf[:, :], qi[:, :]).then_inc(qr, 1)
                pool.wait_ge(rin, 16)
                pool.tensor_copy(k["target"][:, :], rows[:, :, HEADS + 1]).then_inc(qr, 1)

            @block.tensor
            def _(pe):
                pe.wait_ge(rin, 16)
                pe.wait_ge(kready, 1)
                pe.wait_ge(scready, 1)
                for g, ts in enumerate(groups):
                    if g >= 2:
                        pe.wait_ge(ea, g - 1)
                        pe.wait_ge(ek, g - 1)
                    for n, t in enumerate(ts):
                        la = pe.transpose(a_ps[:, g % 2, n * P:(n + 1) * P], scores[:, t, :, :].rearrange("p s h -> p (s h)"), k["ident"][:, :])
                    la.then_inc(ta, 1)
                    for n, t in enumerate(ts):
                        lk = pe.transpose(k_ps[:, g % 2, n * P:(n + 1) * P], keys[:, t, :, :].rearrange("p s h -> p (s h)"), k["ident"][:, :])
                    lk.then_inc(tk, 1)
                pe.wait_ge(ask, 1)
                pe.transpose(c_ps[:, 0, 0:P], k["shift"][:, :], k["ident"][:, :]).then_inc(answer, 1)
                pe.matmul(c_ps[:, 1, 0:1], k["shift"][:, :], ky[:, L - 1:L], start=True, stop=True).then_inc(answer, 1)
                pe.wait_ge(ask, 2)
                pe.matmul(c_ps[:, 2, 0:1], shift_t[:, :], cont[:, 0:1], start=True, stop=True).then_inc(answer, 1)
                n = 3
                for whole_col in (1, 3, 0, 3):
                    pe.wait_ge(ask, n)
                    pe.transpose(c_ps[0:1, 0, 0:P], whole[:, whole_col:whole_col + 1], k["ident"][:, :])
                    pe.transpose(c_ps[0:1, 1, 0:P], edge[:, :], k["ident"][:, :]).then_inc(answer, 1)
                    pe.wait_ge(ask, n + 1)
                    pe.transpose(c_ps[:, 2, 0:1], cin[:, :, :].rearrange("p s h -> p (s h)"), k["ident"][0:1, 0:1]).then_inc(answer, 1)
                    n += 2
                pe.wait_ge(att_ready, 1)
                for g, ts in enumerate(groups):
                    if g >= 2:
                        pe.wait_ge(tkept, g - 1)
                    for n, t in enumerate(ts):
                        last = pe.transpose(a_ps[:, g % 2, n * P:(n + 1) * P], ex[:, t * P:(t + 1) * P], k["ident"][:, :])
                    last.then_inc(tb_done, 1)

            @block.scalar
            def _(act):
                act.wait_ge(rin, 16)
                act.copy(scores[:, :, :, :],
                         rows[:, :, 0:HEADS].bitcast(F32).rearrange("p (s t) h -> p t s h", t=SQ)).then_inc(scready, 1)
                for g, ts in enumerate(groups):
                    act.wait_ge(ta, g + 1)
                    act.copy(al[:, ts[0] * P:(ts[-1] + 1) * P], a_ps[:, g % 2, 0:len(ts) * P]).then_inc(ea, 1)
                act.wait_ge(sub, 1)
                act.activation(ex[:, :], top[:, :], ACT.Exp).then_inc(exped, 1)
                att4 = k["att"][:, :, :].rearrange("p (s t) h -> p t s h", t=SQ)
                for g, ts in enumerate(groups):
                    act.wait_ge(tb_done, g + 1)
                    act.copy(att4[:, ts[0]:ts[-1] + 1, :, :],
                             a_ps[:, g % 2, 0:len(ts) * P].rearrange("p (t s h) -> p t s h", s=STRIPS, h=HEADS)).then_inc(tkept, 1)

            @block.vector
            def _(dve):
                link = chained(dve, chain)
                dve.wait_ge(rin, 16)
                dve.tensor_copy(keyq[:, :], rows[:, :, HEADS]).then_inc(kready0, 1)
                dve.wait_ge(kready0, 1)
                dve.tensor_copy(keys[:, :, :, :], bcast(keyq[:, :].rearrange("p (s t) -> p t s", t=SQ), 3, HEADS)).then_inc(kready, 1)
                dve.wait_ge(qr, 2)
                link(dve.tensor_tensor(cmp[:, :, :], bcast(qf[:, :], 2, NB - 1), bcast(k["first_tile"][:, 1:NB], 1, Q), ALU.is_ge))
                link(dve.tensor_reduce(tb[:, :], cmp[:, :, :], AX_X, ALU.add))
                link(dve.tensor_copy(k["tile_block"][:, :], tb[:, :]))
                dve.wait_ge(kready, 1)
                link(dve.scalar_tensor_tensor(k["local"][:, :], tb[:, :], -float(P), keyq[:, :], ALU.mult, ALU.add))
                link(dve.tensor_scalar(k["local"][:, :], k["local"][:, :], -1.0, None, ALU.add))
                for g, ts in enumerate(groups):
                    dve.wait_ge(tk, g + 1)
                    dve.tensor_copy(ky[:, ts[0] * P:(ts[-1] + 1) * P], k_ps[:, g % 2, 0:len(ts) * P]).then_inc(ek, 1)
                dve.wait_ge(ek, len(groups))
                dve.nop().then_inc(ask, 1)
                dve.wait_ge(answer, 2)
                link(dve.tensor_copy(shift_t[:, :], c_ps[:, 0, 0:P]))
                link(dve.tensor_tensor(cont[:, 1:L], ky[:, 1:L], ky[:, 0:L - 1], ALU.is_equal))
                dve.tensor_tensor(cont[:, 0:1], ky[:, 0:1], c_ps[:, 1, 0:1], ALU.is_equal).then_inc(ask, 1)
                dve.wait_ge(answer, 3)
                link(dve.tensor_copy(cont[:, L:L + 1], c_ps[:, 2, 0:1]))
                link(dve.tensor_scalar(pen[:, :], cont[:, :], -1.0, BIG, ALU.add, ALU.mult))
                link(dve.tensor_reduce(whole[:, 0:1], cont[:, 0:L], AX_X, ALU.min))
                link(dve.tensor_reduce(whole[:, 1:2], pen[:, 0:L], AX_X, ALU.min))
                link(dve.tensor_reduce(whole[:, 3:4], pen[:, 1:L + 1], AX_X, ALU.min))
                link(dve.memset(cin[:, :, :], 0.0))
                asked = [2]
                answered = [3]

                def segments(out, gate, data, neutral, op0, op1, back):
                    flip = (lambda ap: ap[:, ::-1]) if back else (lambda ap: ap)
                    link(dve.tensor_tensor_scan(flip(out), flip(gate), flip(data), neutral, op0, op1))
                    end = out[:, 0:1] if back else out[:, L - 1:L]
                    dve.tensor_copy(edge[:, :], end).then_inc(ask, 1)
                    asked[0] += 1
                    answered[0] += 1
                    dve.wait_ge(answer, answered[0])
                    order = slice(None, None, -1) if back else slice(None)
                    for n in range(2):
                        got = c_ps[0:1, n, 0:P].rearrange("p (s h) -> p h s", h=HEADS)
                        link(dve.tensor_copy(hm[:, n, :, :], got[:, :, order]))
                    flat = lambda ap: ap.rearrange("p h s -> p (h s)")
                    link(dve.tensor_tensor_scan(flat(run[:, :, :]), flat(hm[:, 0, :, :]), flat(hm[:, 1, :, :]),
                                                neutral, op0, op1))
                    took = run[:, :, 0:STRIPS - 1].rearrange("p h s -> p s h")
                    if back:
                        link(dve.memset(cin[:, STRIPS - 1:STRIPS, :], 0.0))
                        dve.tensor_copy(cin[:, 0:STRIPS - 1, :], took[:, ::-1, :]).then_inc(ask, 1)
                    else:
                        link(dve.memset(cin[:, 0:1, :], 0.0))
                        dve.tensor_copy(cin[:, 1:STRIPS, :], took).then_inc(ask, 1)
                    asked[0] += 1
                    answered[0] += 1
                    dve.wait_ge(answer, answered[0])
                    link(dve.tensor_copy(carry[:, :], c_ps[:, 2, 0:1]))
                    link(dve.tensor_tensor_scan(flip(out), flip(gate), flip(data), carry[:, :], op0, op1))

                dve.wait_ge(ea, len(groups))
                segments(fw[:, :], pen[:, 0:L], al[:, :], -BIG, ALU.add, ALU.max, False)
                segments(top[:, :], pen[:, 1:L + 1], fw[:, :], -BIG, ALU.add, ALU.max, True)
                dve.tensor_tensor(top[:, :], al[:, :], top[:, :], ALU.subtract).then_inc(sub, 1)
                dve.wait_ge(exped, 1)
                segments(fw[:, :], cont[:, 0:L], ex[:, :], 0.0, ALU.mult, ALU.add, False)
                segments(den[:, :], pen[:, 1:L + 1], fw[:, :], 0.0, ALU.add, ALU.max, True)
                link(dve.tensor_scalar(den[:, :], den[:, :], 1e-16, None, ALU.add))
                link(dve.reciprocal(den[:, :], den[:, :]))
                dve.tensor_tensor(ex[:, :], ex[:, :], den[:, :], ALU.mult).then_inc(att_ready, 1)


def sum_messages(nc, k, sem, he_d):
    SL, AHEAD, LAG, BK = 8, 6, 3, 4
    x_sb = k["x_sb"]
    with ExitStack() as ctx:
        s = Space(nc, ctx)
        ix = s.sb("ixm", [P, SL], U32)
        g = s.sb("g", [P, SL, HEADS, D])
        msg = s.sb("msg", [P, SL, HEADS, D])
        hot = s.sb("hot", [P, SL, P])
        m_ps = s.ps("m_ps", [P, 4, F])
        ixr, hots, summed, added = sem("m_indices"), sem("m_hot"), sem("m_summed"), sem("m_added")
        made = sem("m_made")
        got = [sem(f"m_rows_in{j}") for j in range(SL)]

        with nc.Block() as block:
            @block.gpsimd
            def _(pool):
                def gather(q, j):
                    pool.tensor_copy(ix[:, j:j + 1], k["target"][:, bass.ds(q, 1)]).then_inc(ixr, 1)
                    pool.wait_ge(ixr, q + 1)
                    pool.nop(nofuse=True)
                    pool.indirect_dma_start(g[:, j, :, :].rearrange("p h d -> p (h d)"), None, he_d,
                                            bass.IndirectOffsetOnAxis(ap=ix[:, j:j + 1], axis=0)).then_inc(got[j], 16)

                for q in range(SL):
                    gather(q, q)
                with pool.Fori(1, Q // SL) as i:
                    for j in range(SL):
                        pool.wait_ge(made, SL * i + j - SL + 1)
                        gather(SL * i + j, j)

            @block.vector
            def _(dve):
                def prepare(q, j, n):
                    dve.tensor_scalar(hot[:, j, :], k["iota"][:, :], k["local"][:, bass.ds(q, 1)], None,
                                      ALU.is_equal).then_inc(hots, 1)
                    dve.wait_ge(got[j], 16 * n + 16)
                    dve.tensor_tensor(msg[:, j, :, :], g[:, j, :, :],
                                      bcast(k["att"][:, bass.ds(q, 1), :].rearrange("p a h -> p (a h)"), 2, D),
                                      ALU.mult).then_inc(made, 1)

                def add(q, j):
                    b = dve.value_load(k["tile_block"][0:1, bass.ds(q, 1)], min_val=0, max_val=NB - 1)
                    dve.wait_ge(summed, q + 1)
                    sl = x_sb[:, bass.ds(b, 1), :].rearrange("p a f -> p (a f)")
                    dve.tensor_tensor(sl, m_ps[:, j % BK, :], sl, ALU.add).then_inc(added, 1)

                def step(q, j, n):
                    prepare(q, j, n)
                    if isinstance(q, int) and q < LAG:
                        return
                    if not (isinstance(q, int) and q == LAG):
                        dve.wait_ge(added, q - LAG)
                    add(q - LAG, (j - LAG) % SL)

                for q in range(SL):
                    step(q, q, 0)
                with dve.Fori(1, Q // SL) as i:
                    for j in range(SL):
                        step(SL * i + j, j, i)
                for q in range(Q - LAG, Q):
                    dve.wait_ge(added, q)
                    add(q, q % SL)

            @block.tensor
            def _(pe):
                def total(q, j):
                    pe.wait_ge(hots, q + 1)
                    pe.wait_ge(made, q + 1)
                    pe.matmul(m_ps[:, j % BK, :], hot[:, j, :], msg[:, j, :, :].rearrange("p h d -> p (h d)"),
                              start=True, stop=True).then_inc(summed, 1)

                for q in range(SL):
                    if q >= BK:
                        pe.wait_ge(added, q - BK + 1)
                    total(q, q)
                with pe.Fori(1, Q // SL) as i:
                    for j in range(SL):
                        q = SL * i + j
                        pe.wait_ge(added, q - BK + 1)
                        total(q, j)


def route(nc, k, sem, wg):
    x_sb = k["x_sb"]
    with ExitStack() as ctx:
        s = Space(nc, ctx)
        st = s.sb("st2", [P, NB, 6])
        mv = s.sb("mv2", [P, NB, 2])
        var = s.sb("var2", [P, NB])
        root = s.sb("root2", [P, NB])
        rstd = s.sb("rstd2", [P, NB])
        xn = s.sb("xn2", [P, 2, F])
        wg_sb = s.sb("wg_sb", [P, CH, EXPERTS])
        rankw = s.sb("rankw", [P, EXPERTS])
        lg = s.sb("lg", [P, NB, EXPERTS])
        g = s.sb("gate", [P, NB, EXPERTS])
        m1 = s.sb("mask1", [P, NB, EXPERTS])
        m2 = s.sb("mask2", [P, NB, EXPERTS])
        tmp = s.sb("tmp", [P, NB, EXPERTS])
        v1 = s.sb("v1", [P, NB])
        v2 = s.sb("v2", [P, NB])
        v3 = s.sb("v3", [P, NB])
        t_ps = s.ps("t2_ps", [P, 2, F])
        g_ps = s.ps("g_ps", [P, NB, EXPERTS])

        stats, chain, rready, rdone, wgin = sem("stats2"), sem("route_chain"), sem("var_ready2"), sem("root_done2"), sem("wg_in")
        xn_ready, tp, xt_ready, gated, lgr, exped = sem("xn_ready2"), sem("x_turned2"), sem("xt_ready2"), sem("gated"), sem("logits"), sem("gate_exped")

        with nc.Block() as block:
            @block.sync
            def _(sp):
                sp.dma_start(wg_sb[:, :, :], wg.rearrange("(c p) e -> p c e", p=P)).then_inc(wgin, 16)

            @block.scalar
            def _(act):
                act.wait_ge(rready, 1)
                act.activation(root[:, :], var[:, :], ACT.Sqrt).then_inc(rdone, 1)
                for b in range(NB):
                    act.wait_ge(tp, b + 1)
                    act.copy(k["xt_all"][:, :, b * P:(b + 1) * P], t_ps[:, b % 2, :].rearrange("p (c n) -> p c n", c=CH)).then_inc(xt_ready, 1)
                act.wait_ge(lgr, 1)
                act.activation(lg[:, :, :], lg[:, :, :], ACT.Exp).then_inc(exped, 1)

            @block.tensor
            def _(pe):
                pe.wait_ge(wgin, 16)
                for b in range(NB + 1):
                    if b < NB:
                        pe.wait_ge(xn_ready, b + 1)
                        if b >= 2:
                            pe.wait_ge(xt_ready, b - 1)
                        for c in range(CH):
                            last = pe.transpose(t_ps[:, b % 2, c * P:(c + 1) * P], xn[:, b % 2, c * P:(c + 1) * P], k["ident"][:, :])
                        last.then_inc(tp, 1)
                    if b >= 1:
                        pe.wait_ge(xt_ready, b)
                        for c in range(CH):
                            last = pe.matmul(g_ps[:, b - 1, :], k["xt_all"][:, c, (b - 1) * P:b * P], wg_sb[:, c, :],
                                             start=(c == 0), stop=(c == CH - 1))
                last.then_inc(gated, 1)

            @block.vector
            def _(dve):
                link = chained(dve, chain)
                for b in range(NB):
                    dve.bn_stats(st[:, b, :], x_sb[:, b, :]).then_inc(stats, 1)
                dve.wait_ge(stats, NB)
                for b in range(NB):
                    dve.bn_aggr(mv[:, b, :], st[:, b, :]).then_inc(stats, 1)
                dve.wait_ge(stats, 2 * NB)
                normalise_stats(dve, rready, rdone, link, mv, var[:, :], root[:, :], rstd[:, :])
                for b in range(NB):
                    if b >= 2:
                        dve.wait_ge(tp, b - 1)
                    dve.tensor_scalar(xn[:, b % 2, :], x_sb[:, b, :], mv[:, b, 0:1], rstd[:, b:b + 1],
                                      ALU.subtract, ALU.mult).then_inc(xn_ready, 1)
                dve.wait_ge(gated, 1)
                ex3 = lambda v: bcast(v[:, :], 2, EXPERTS)
                link(dve.tensor_scalar(rankw[:, :], k["iota"][:, 0:EXPERTS], -1.0, float(EXPERTS), ALU.mult, ALU.add))
                link(dve.tensor_copy(g[:, :, :], g_ps[:, :, :]))
                link(dve.tensor_reduce(v1[:, :], g[:, :, :], AX_X, ALU.max))
                dve.tensor_tensor(lg[:, :, :], g[:, :, :], ex3(v1), ALU.subtract).then_inc(lgr, 1)
                dve.wait_ge(exped, 1)
                link(dve.tensor_reduce(v1[:, :], lg[:, :, :], AX_X, ALU.add))
                link(dve.reciprocal(v1[:, :], v1[:, :]))
                link(dve.tensor_tensor(g[:, :, :], lg[:, :, :], ex3(v1), ALU.mult))

                def pick(src, mask, best):
                    link(dve.tensor_reduce(best[:, :], src[:, :, :], AX_X, ALU.max))
                    link(dve.tensor_tensor(mask[:, :, :], src[:, :, :], ex3(best), ALU.is_equal))
                    link(dve.tensor_tensor(mask[:, :, :], mask[:, :, :], bcast(rankw[:, :], 1, NB), ALU.mult))
                    link(dve.tensor_reduce(v3[:, :], mask[:, :, :], AX_X, ALU.max))
                    link(dve.tensor_tensor(mask[:, :, :], mask[:, :, :], ex3(v3), ALU.is_equal))

                pick(g, m1, v1)
                link(dve.scalar_tensor_tensor(tmp[:, :, :], m1[:, :, :], -2.0, g[:, :, :], ALU.mult, ALU.add))
                pick(tmp, m2, v2)
                link(dve.tensor_tensor(v1[:, :], v1[:, :], v2[:, :], ALU.add))
                link(dve.tensor_scalar(v1[:, :], v1[:, :], 1e-6, None, ALU.add))
                link(dve.reciprocal(v1[:, :], v1[:, :]))
                link(dve.tensor_tensor(m1[:, :, :], m1[:, :, :], m2[:, :, :], ALU.add))
                link(dve.tensor_tensor(m1[:, :, :], m1[:, :, :], g[:, :, :], ALU.mult))
                link(dve.tensor_tensor(k["score_b"][:, :, :], m1[:, :, :], ex3(v1), ALU.mult))
                link(dve.tensor_copy(k["score_e"][:, :, :].rearrange("p e b -> p b e"), k["score_b"][:, :, :]))


def experts(nc, k, sem, w1, b1, w2, b2, out):
    x_sb, xt = k["x_sb"], k["xt_all"]
    PER = 2 * NG
    with ExitStack() as ctx:
        s = Space(nc, ctx)
        w1_sb = s.sb("w1_sb", [P, 2, CH, HID])
        w2_sb = s.sb("w2_sb", [P, 2, HCH, F])
        b1_row = s.sb("b1_row", [EXPERTS * HCH, P])
        b1_col = s.sb("b1_col", [P, EXPERTS, HCH])
        b2_sb = s.sb("b2_sb", [EXPERTS, F])
        sc_t = s.sb("sc_t", [EXPERTS, 2, P])
        hid = s.sb("hid", [P, 2, HCH, 512])
        h_ps = s.ps("h_ps", [P, 4, 512])
        y_ps = s.ps("y_ps", [P, 4, 512])

        small, win = sem("biases_in"), [sem(f"expert_in{j}") for j in range(2)]
        bt, bready, st, sready, badd = sem("b1_turned"), sem("b1_ready"), sem("score_turned"), sem("score_t_ready"), sem("b2_added")
        b2s = sem("b2_summed")
        hdone, hready, ydone, added, stored = sem("hidden"), sem("hidden_ready"), sem("y_done"), sem("y_added"), sem("stored")

        with nc.Block() as block:
            @block.sync
            def _(sp):
                sp.dma_start(b1_row[:, :], b1.rearrange("e (c p) -> (e c) p", p=P)).then_inc(small, 16)
                sp.dma_start(b2_sb[:, :], b2).then_inc(small, 16)

                def load(e, j):
                    sp.dma_start(w1_sb[:, j, :, :], w1[bass.ds(e, 1), :, :].rearrange("a (c p) h -> p (a c) h", p=P)).then_inc(win[j], 16)
                    sp.dma_start(w2_sb[:, j, :, :], w2[bass.ds(e, 1), :, :].rearrange("a (c p) f -> p (a c) f", p=P)).then_inc(win[j], 16)

                load(0, 0)
                load(1, 1)
                with sp.Fori(1, EXPERTS // 2) as i:
                    for j in range(2):
                        sp.wait_ge(ydone, 4 * (PER * i - PER + NG * (j + 1)))
                        load(2 * i + j, j)
                sp.wait_ge(added, 4 * NG * EXPERTS)
                sp.dma_start(out[0:(NB - 1) * P, :].rearrange("(b p) f -> p b f", p=P), x_sb[:, 0:NB - 1, :]).then_inc(stored, 16)
                sp.dma_start(out[(NB - 1) * P:N, :], x_sb[0:TAIL, NB - 1, :]).then_inc(stored, 16)
                sp.wait_ge(stored, 32)

            @block.tensor
            def _(pe):
                pe.wait_ge(small, 32)
                pe.transpose(h_ps[:, 0, 0:EXPERTS * HCH], b1_row[:, :], k["ident"][0:EXPERTS * HCH, 0:EXPERTS * HCH]).then_inc(bt, 1)
                for b in range(NB + 1):
                    if b < NB:
                        if b >= 2:
                            pe.wait_ge(sready, b - 1)
                        pe.transpose(h_ps[0:EXPERTS, 2 + b % 2, 0:P], k["score_b"][:, b, :], k["ident"][:, :]).then_inc(st, 1)
                    if b >= 1:
                        pe.wait_ge(sready, b)
                        if b >= 3:
                            pe.wait_ge(badd, b - 2)
                        pe.matmul(y_ps[:, (b - 1) % 2, :], sc_t[:, (b - 1) % 2, :], b2_sb[:, :], start=True, stop=True).then_inc(b2s, 1)
                pe.wait_ge(badd, NB)
                pe.wait_ge(bready, 1)

                def up(tg, je, j):
                    for hb in range(HCH):
                        for c in range(CH):
                            last = pe.matmul(h_ps[:, 2 * j + hb, :], w1_sb[:, je, c, hb * P:(hb + 1) * P],
                                             xt[:, c, tg * 512:(tg + 1) * 512], start=(c == 0), stop=(c == CH - 1))
                        last.then_inc(hdone, 1)

                def down(n, je, j):
                    pe.wait_ge(hready, 2 * n + 2)
                    for t in range(4):
                        if not (isinstance(n, int) and n == 0):
                            pe.wait_ge(added, 4 * n - 3 + t)
                        for hb in range(HCH):
                            last = pe.matmul(y_ps[:, t, :], hid[:, j, hb, t * P:(t + 1) * P], w2_sb[:, je, hb, :],
                                             start=(hb == 0), stop=(hb == HCH - 1))
                        last.then_inc(ydone, 1)

                pe.wait_ge(win[0], 32)
                up(0, 0, 0)
                for m in range(PER - 1):
                    if m + 1 == NG:
                        pe.wait_ge(win[1], 32)
                    if m >= 1:
                        pe.wait_ge(hready, 2 * m)
                    up((m + 1) % NG, (m + 1) // NG, (m + 1) % 2)
                    down(m, m // NG, m % 2)
                with pe.Fori(1, EXPERTS // 2) as i:
                    for m in range(-1, PER - 1):
                        n = PER * i + m
                        if m + 1 == 0:
                            pe.wait_ge(win[0], 32 * i + 32)
                        if m + 1 == NG:
                            pe.wait_ge(win[1], 32 * i + 32)
                        pe.wait_ge(hready, 2 * n)
                        up((m + 1) % NG, (m + 1) // NG, (m + 1) % 2)
                        down(n, (m // NG) % 2, m % 2)
                down(PER * EXPERTS // 2 - 1, 1, 1)

            @block.scalar
            def _(act):
                act.wait_ge(bt, 1)
                act.copy(b1_col[:, :, :].rearrange("p e c -> p (e c)"), h_ps[:, 0, 0:EXPERTS * HCH]).then_inc(bready, 1)
                for b in range(NB):
                    act.wait_ge(st, b + 1)
                    if b >= 2:
                        act.wait_ge(b2s, b - 1)
                    act.copy(sc_t[:, b % 2, :], h_ps[0:EXPERTS, 2 + b % 2, 0:P]).then_inc(sready, 1)
                act.wait_ge(bready, 1)

                def gelu(n, e, j, first):
                    for hb in range(HCH):
                        act.wait_ge(hdone, 2 * n + hb + 1)
                        if hb == 0 and not first:
                            act.wait_ge(ydone, 4 * n - 4)
                        act.nop(nofuse=True)
                        act.activation(hid[:, j, hb, :], h_ps[:, 2 * j + hb, :], ACT.Gelu,
                                       bias=b1_col[:, bass.ds(e, 1), hb]).then_inc(hready, 1)

                for m in range(PER):
                    gelu(m, m // NG, m % 2, m < 2)
                with act.Fori(1, EXPERTS // 2) as i:
                    for m in range(PER):
                        gelu(PER * i + m, 2 * i + m // NG, m % 2, False)

            @block.vector
            def _(dve):
                for b in range(NB):
                    dve.wait_ge(b2s, b + 1)
                    dve.tensor_tensor(x_sb[:, b, :], y_ps[:, b % 2, :], x_sb[:, b, :], ALU.add).then_inc(badd, 1)
                dve.wait_ge(badd, NB)

                def add(n, e, tg):
                    for t in range(4):
                        b = 4 * tg + t
                        dve.wait_ge(ydone, 4 * n + t + 1)
                        dve.scalar_tensor_tensor(x_sb[:, b, :], y_ps[:, t, :], k["score_e"][:, bass.ds(e, 1), b],
                                                 x_sb[:, b, :], ALU.mult, ALU.add).then_inc(added, 1)

                for m in range(PER):
                    if m >= NG:
                        dve.wait_ge(added, 4 * (m - NG + 1))
                    add(m, m // NG, m % NG)
                with dve.Fori(1, EXPERTS // 2) as i:
                    for m in range(PER):
                        dve.wait_ge(added, 4 * (PER * i + m - NG + 1))
                        add(PER * i + m, 2 * i + m // NG, m % NG)


def kernel_body(nc, x, src, dst, we, wr, a, wg, w1, b1, w2, b2, out):
    dram = lambda name, shape, dt: nc.dram_tensor(name, shape, dt, kind="Internal").ap()
    sorted_d = dram("sorted_d", [CAP + DUMP, RW], U32)
    table_d = dram("table_d", [NB * P, TW], F32)
    he_d = dram("he_d", [NB * P, F], F32)
    with ExitStack() as ctx:
        s = Space(nc, ctx)
        sem = lambda name: ctx.enter_context(nc.semaphore(name))
        k = dict(
            iota_i=s.sb("iota_i", [P, P], I32), iota=s.sb("iota", [P, P]), ident=s.sb("ident", [P, P]),
            ident_bf=s.sb("ident_bf", [P, P], BF16), ones=s.sb("ones", [P, P]), before=s.sb("before", [P, P]),
            shift=s.sb("shift", [P, P]),
            ends=s.sb("ends3", [P, T, 3], U32), ids=s.sb("ids", [P, T, 2], U32),
            first_tile=s.sb("first_tile", [P, NB]),
        )
        build_constants(nc, k, sem)
        rank_edges(nc, k, sem, src, dst, sorted_d)
        k["x_sb"] = s.sb("x_sb", [P, NB, F])
        project(nc, k, sem, x, we, wr, a, table_d, he_d)
        score_edges(nc, k, sem, a, table_d, sorted_d)
        k["att"] = s.sb("att", [P, Q, HEADS])
        k["target"] = s.sb("target", [P, Q], U32)
        k["local"] = s.sb("local", [P, Q])
        k["tile_block"] = s.sb("tile_block", [P, Q], I32)
        edge_softmax(nc, k, sem, sorted_d)
        sum_messages(nc, k, sem, he_d)
        k["xt_all"] = s.sb("xt_all", [P, CH, NB * P])
        k["score_b"] = s.sb("score_b", [P, NB, EXPERTS])
        k["score_e"] = s.sb("score_e", [P, EXPERTS, NB])
        route(nc, k, sem, wg)
        experts(nc, k, sem, w1, b1, w2, b2, out)


_INS = ['x', 'src', 'dst', 'L0_gnn_W_e', 'L0_gnn_W_r', 'L0_gnn_a', 'L0_ffn_Wg', 'L0_ffn_W1', 'L0_ffn_b1', 'L0_ffn_W2', 'L0_ffn_b2']
_OUTS = [((N, F), 'float32')]


def kernel(**inputs):
    import numpy as _np
    import concourse.bacc as _bacc
    from concourse import mybir as _mybir
    from concourse.bass_utils import run_bass_kernel_spmd as _run

    nc = _bacc.Bacc("TRN2", target_bir_lowering=False, num_devices=1)
    arrays, args = {}, []
    for name in _INS:
        a = _np.ascontiguousarray(inputs[name])
        arrays[f"in_{name}_dram"] = a
        args.append(nc.dram_tensor(f"in_{name}_dram", a.shape, _mybir.dt.from_np(a.dtype), kind="ExternalInput").ap())
    for i, (shape, dtype) in enumerate(_OUTS):
        dt = _mybir.dt.from_np(_np.dtype(dtype))
        args.append(nc.dram_tensor(f"out_{i}_dram", shape, dt, kind="ExternalOutput").ap())
    kernel_body(nc, *args)
    r = _run(nc, [arrays], core_ids=[0])
    got = tuple(r.results[0][f"out_{i}_dram"] for i in range(len(_OUTS)))
    return got[0]
```

```python
from contextlib import ExitStack

import concourse.bass as bass
from concourse import mybir

F32 = mybir.dt.float32
BF16 = mybir.dt.bfloat16
I32 = mybir.dt.int32
U32 = mybir.dt.uint32
ALU = mybir.AluOpType
ACT = mybir.ActivationFunctionType
AX_X = mybir.AxisListType.X

P = 128
N = 2500
F = 512
NB = -(-N // P)
TAIL = N - (NB - 1) * P
HEADS = 8
D = F // HEADS
CH = F // P
E = 40000
EP = 125
T = E // EP
GT = 4
GROUPS = T // GT
Q = 336
STRIPS = P // HEADS
SQ = Q // STRIPS
CAP = Q * P
DUMP = (P - EP) * T
RW = 12
TW = F + 2 * HEADS
CPB = 16
SLOPE = 0.2
EPS = 1e-5
BIG = 1.0e30
EXPERTS = 8
HID = 256
HCH = HID // P
NG = 5
assert Q * P >= E + NB * (P - 1) and NB * P == NG * 512 and EP * T == E and GROUPS * GT == T


def bcast(ap, axis, n):
    ap = ap.unsqueeze(axis)
    shape = list(ap.shape)
    shape[axis] = n
    return ap.to_broadcast(shape)


class Space:

    def __init__(self, nc, ctx):
        self.nc, self.ctx = nc, ctx

    def sb(self, name, shape, dt=F32):
        return self.ctx.enter_context(self.nc.sbuf_tensor(name, shape, dt))

    def ps(self, name, shape, dt=F32):
        return self.ctx.enter_context(self.nc.psum_tensor(name, shape, dt))


def chained(eng, sem, before=0):
    count = [before]

    def link(ins):
        count[0] += 1
        ins.then_inc(sem, 1)
        eng.wait_ge(sem, count[0])

    return link


def build_constants(nc, k, sem):
    made = sem("constants_made")
    block_ctx = nc.Block()
    with block_ctx as block:
        @block.gpsimd
        def _(pool):
            link = chained(pool, made)
            link(pool.iota(k["iota_i"][:, :], pattern=[[1, P]], base=0, channel_multiplier=0))
            link(pool.tensor_copy(k["iota"][:, :], k["iota_i"][:, :]))
            link(pool.memset(k["ident"][:, :], 0.0))
            link(pool.affine_select(out=k["ident"][:, :], in_=k["ident"][:, :], compare_op=ALU.not_equal,
                                    fill=1.0, base=0, pattern=[[-1, P]], channel_multiplier=1))
            link(pool.tensor_copy(k["ident_bf"][:, :], k["ident"][:, :]))
            link(pool.memset(k["ones"][:, :], 1.0))
            link(pool.affine_select(out=k["before"][:, :], in_=k["ones"][:, :], compare_op=ALU.is_gt,
                                    fill=0.0, base=0, pattern=[[1, P]], channel_multiplier=-1))
            link(pool.memset(k["shift"][:, :], 0.0))
            link(pool.affine_select(out=k["shift"][:, :], in_=k["shift"][:, :], compare_op=ALU.not_equal,
                                    fill=1.0, base=HEADS, pattern=[[-1, P]], channel_multiplier=1))


def normalise_stats(dve, act_ready, act_done, link, mv, var, root, rstd):
    link(dve.tensor_scalar(var, mv[:, :, 1], EPS, None, ALU.add))
    dve.nop().then_inc(act_ready, 1)
    dve.wait_ge(act_done, 1)
    link(dve.reciprocal(rstd, root))
    link(dve.tensor_tensor(rstd, rstd, var, ALU.mult))
    link(dve.tensor_tensor(root, rstd, root, ALU.add))
    link(dve.tensor_scalar(root, root, 0.5, None, ALU.mult))
    link(dve.reciprocal(rstd, root))


def project(nc, k, sem, x, src, dst, we, wr, a, table_d, he_d, sorted_d):
    x_sb = k["x_sb"]
    with ExitStack() as ctx:
        s = Space(nc, ctx)
        w_e = s.sb("w_e", [P, CH, F])
        w_r = s.sb("w_r", [P, CH, F])
        a_all = s.sb("a_all", [P, HEADS, 5 * D])
        half = s.sb("half", [P, HEADS, D])
        prod = s.sb("prod", [P, CH, HEADS, D])
        lin = s.sb("lin", [P, CH, 2 * HEADS])
        dif = s.sb("dif", [P, CH, HEADS])
        st = s.sb("st", [P, NB, 6])
        mv = s.sb("mv", [P, NB, 2])
        var = s.sb("var", [P, NB])
        root = s.sb("root", [P, NB])
        rstd = s.sb("rstd", [P, NB])
        xn = s.sb("xn", [P, 2, F])
        xt = s.sb("xt", [P, 2, CH, P])
        row = s.sb("row", [P, 2, TW])
        he = s.sb("he", [P, 2, F])
        sq = s.sb("sq", [P, 2, HEADS, D])
        sqa = s.sb("sqa", [P, 2, HEADS, D])
        own = s.sb("own", [P, 2, HEADS])
        src_i = s.sb("src_i", [P, T], I32)
        dst_i = s.sb("dst_i", [P, T], I32)
        blk_i = s.sb("blk_i", [P, T], I32)
        blk = s.sb("blk", [P, T])
        dump_i = s.sb("dump_i", [P, T], I32)
        hot = s.sb("hot_loc", [P, 2, CPB, P], BF16)
        fill = s.sb("fill", [P, 21, RW], U32)
        loc, oh_blk, first = k["loc"], k["oh_blk"], k["first"]
        t_ps = s.ps("t_ps", [P, 2, F])
        r_ps = s.ps("r_ps", [P, 2, F])
        e_ps = s.ps("e_ps", [P, 2, F])
        lc_ps = s.ps("lc_ps", [P, 2, 512])
        l_ps = lc_ps[:, :, 0:2 * HEADS]
        counts_ps = lc_ps[:, :, 2 * HEADS:2 * HEADS + CPB * NB]

        xin = [sem(f"x_in{c}") for c in range(5)]
        win, ain, tailz = sem("weights_in"), sem("a_in"), sem("tail_zero")
        stats, chain, rready, rdone = sem("stats"), sem("project_chain"), sem("var_ready"), sem("root_done")
        linr, xn_ready, tp, xt_ready, proj = sem("lin_ready"), sem("xn_ready"), sem("x_turned"), sem("xt_ready"), sem("projected")
        he_ready, sq_ready, row_ready, sqa_ready = sem("he_ready"), sem("sq_ready"), sem("row_ready"), sem("sqa_ready")
        hr_copied, own_ready, pq = sem("hr_copied"), sem("own_ready"), sem("pq_ready")
        row_out = [sem(f"row_out{j}") for j in range(2)]
        he_out = [sem(f"he_out{j}") for j in range(2)]
        loaded, cleared, edge_ids = sem("edges_loaded"), sem("edges_cleared"), sem("edge_ids")
        valid, hots, counted, kept = sem("edges_valid"), sem("one_hots"), sem("tiles_counted"), sem("counts_kept")
        blk_hot = sem("block_one_hot")
        dumped, filled, fill_out, pool_chain = sem("dump_ready"), sem("fill_ready"), sem("fill_out"), sem("count_pool_chain")

        with nc.Block() as block:
            @block.sync
            def _(sp):
                sp.wait_ge(cleared, 2)
                sp.dma_start(src_i[0:EP, :], src.rearrange("(p t) -> p t", t=T)).then_inc(loaded, 16)
                sp.dma_start(dst_i[0:EP, :], dst.rearrange("(p t) -> p t", t=T)).then_inc(loaded, 16)
                for c in range(4):
                    sp.dma_start(x_sb[:, 4 * c:4 * c + 4, :],
                                 x[512 * c:512 * (c + 1), :].rearrange("(b p) f -> p b f", p=P)).then_inc(xin[c], 16)
                sp.dma_start(x_sb[:, 16:NB - 1, :],
                             x[2048:(NB - 1) * P, :].rearrange("(b p) f -> p b f", p=P)).then_inc(xin[4], 16)
                sp.wait_ge(tailz, 1)
                sp.dma_start(x_sb[0:TAIL, NB - 1, :], x[(NB - 1) * P:N, :]).then_inc(xin[4], 16)
                sp.wait_ge(filled, 3)
                rows = sorted_d[0:CAP, :].rearrange("(p g t) w -> p g t w", p=P, t=21)
                for g in range(Q // 21):
                    sp.dma_start(rows[:, g, :, :], fill[:, :, :]).then_inc(fill_out, 16)

                def store(b, j):
                    sp.wait_ge(row_ready, b + 1)
                    sp.dma_start(table_d[bass.ds(b * P, P), :], row[:, j, :]).then_inc(row_out[j], 16)
                    sp.wait_ge(he_ready, b + 1)
                    sp.dma_start(he_d[bass.ds(b * P, P), :], he[:, j, :]).then_inc(he_out[j], 16)

                with sp.Fori(0, NB // 2) as i:
                    for j in range(2):
                        store(2 * i + j, j)
                for j in range(2):
                    sp.wait_ge(row_out[j], 16 * NB // 2)
                    sp.wait_ge(he_out[j], 16 * NB // 2)
                sp.wait_ge(fill_out, 16 * (Q // 21))

            @block.gpsimd
            def _(pool):
                pool.memset(fill[:, :, :], 0).then_inc(filled, 1)
                pool.wait_ge(filled, 1)
                pool.memset(fill[:, :, HEADS:HEADS + 1], 4095).then_inc(filled, 2)
                pool.iota(dump_i[:, :], pattern=[[1, T]], base=CAP - EP * T, channel_multiplier=T).then_inc(pool_chain, 1)
                pool.wait_ge(pool_chain, 1)
                pool.tensor_copy(k["dump"][:, :], dump_i[:, :]).then_inc(pool_chain, 1)
                pool.wait_ge(pool_chain, 2)
                pool.affine_select(out=k["dump"][:, :], in_=k["dump"][:, :], compare_op=ALU.is_ge, fill=0.0,
                                   base=-EP, pattern=[[0, T]], channel_multiplier=1).then_inc(dumped, 1)
                pool.wait_ge(edge_ids, 4)
                pool.affine_select(out=blk[:, :], in_=blk[:, :], compare_op=ALU.is_ge, fill=-1.0,
                                   base=EP - 1, pattern=[[0, T]], channel_multiplier=-1).then_inc(valid, 1)
                pool.affine_select(out=loc[:, 0:T], in_=loc[:, 0:T], compare_op=ALU.is_ge, fill=-1.0,
                                   base=EP - 1, pattern=[[0, T]], channel_multiplier=-1).then_inc(valid, 1)
                pool.memset(k["same"][:, :, :], 1.0).then_inc(pool_chain, 1)
                pool.wait_ge(pool_chain, 3)
                pool.memset(k["same"][:, :, 0:1], 0.0).then_inc(pool_chain, 1)

            @block.scalar
            def _(act):
                act.dma_start(a_all[:, :, :], a.partition_broadcast(P)).then_inc(ain, 16)
                for c in range(CH):
                    act.dma_start(w_e[:, c, :].rearrange("p (h d) -> p h d", h=HEADS),
                                  we[:, c * P:(c + 1) * P, :].rearrange("h p d -> p h d")).then_inc(win, 16)
                    act.dma_start(w_r[:, c, :].rearrange("p (h d) -> p h d", h=HEADS),
                                  wr[:, c * P:(c + 1) * P, :].rearrange("h p d -> p h d")).then_inc(win, 16)
                act.wait_ge(rready, 1)
                act.activation(root[:, :], var[:, :], ACT.Sqrt).then_inc(rdone, 1)

                def turned(b, j):
                    act.wait_ge(tp, b + 1)
                    act.copy(xt[:, j, :, :], t_ps[:, j, :].rearrange("p (c n) -> p c n", c=CH)).then_inc(xt_ready, 1)

                def keep(b, j):
                    act.wait_ge(proj, b + 1)
                    act.activation(sq[:, j, :, :].rearrange("p h d -> p (h d)"), r_ps[:, j, :], ACT.Square).then_inc(sq_ready, 1)
                    act.copy(he[:, j, :], e_ps[:, j, :]).then_inc(he_ready, 1)

                def keep_counts(c, j):
                    act.wait_ge(counted, c + 1)
                    act.copy(first[:, :, bass.ds(c * CPB + 1, CPB)].rearrange("p b t -> p t b"),
                             counts_ps[:, j, :].rearrange("p (t b) -> p t b", b=NB)).then_inc(kept, 1)

                turned(0, 0)
                turned(1, 1)
                keep_counts(0, 0)
                keep(0, 0)

                def pair(i):
                    for j in range(2):
                        b = 2 * i + j
                        act.wait_ge(proj, b - 1)
                        turned(b, j)
                        keep_counts(b - 1, 1 - j)
                        if not (isinstance(b, int) and b == 2):
                            act.wait_ge(he_out[1 - j], 16 * (i + j) - 16)
                            act.wait_ge(row_ready, b - 2)
                        keep(b - 1, 1 - j)

                pair(1)
                with act.Fori(2, NB // 2) as i:
                    pair(i)
                keep_counts(NB - 1, 1)
                act.wait_ge(he_out[1], 16 * (NB // 2 - 1))
                act.wait_ge(row_ready, NB - 2)
                keep(NB - 1, 1)

            @block.tensor
            def _(pe):
                def turn(b, j):
                    pe.wait_ge(xn_ready, b + 1)
                    for c in range(CH):
                        last = pe.transpose(t_ps[:, j, c * P:(c + 1) * P], xn[:, j, c * P:(c + 1) * P], k["ident"][:, :])
                    last.then_inc(tp, 1)

                def multiply(b, j):
                    pe.wait_ge(xt_ready, b + 1)
                    for out, w in ((r_ps[:, j, :], w_r), (e_ps[:, j, :], w_e), (l_ps[:, j, :], lin)):
                        if w is lin:
                            pe.wait_ge(kept, b + 1)
                        for c in range(CH):
                            last = pe.matmul(out, xt[:, j, c, :], w[:, c, :], start=(c == 0), stop=(c == CH - 1))
                    last.then_inc(proj, 1)

                def count(c, j):
                    pe.wait_ge(hots, c + 1)
                    for t in range(CPB):
                        last = pe.matmul(counts_ps[:, j, t * NB:(t + 1) * NB], hot[:, j, t, :],
                                         oh_blk[:, bass.ds(c * CPB + t, 1), :].rearrange("p a b -> p (a b)"),
                                         start=True, stop=True)
                    last.then_inc(counted, 1)

                turn(0, 0)
                turn(1, 1)
                pe.wait_ge(win, 32 * CH)
                pe.wait_ge(linr, 1)
                pe.wait_ge(blk_hot, 1)
                count(0, 0)
                multiply(0, 0)

                def pair(i):
                    for j in range(2):
                        b = 2 * i + j
                        pe.wait_ge(xt_ready, b - 1)
                        turn(b, j)
                        if not (isinstance(b, int) and b == 2):
                            pe.wait_ge(row_ready, b - 2)
                            pe.wait_ge(he_ready, b - 2)
                        count(b - 1, 1 - j)
                        multiply(b - 1, 1 - j)

                pair(1)
                with pe.Fori(2, NB // 2) as i:
                    pair(i)
                pe.wait_ge(row_ready, NB - 2)
                pe.wait_ge(he_ready, NB - 2)
                count(NB - 1, 1)
                multiply(NB - 1, 1)

            @block.vector
            def _(dve):
                link = chained(dve, chain, 2)
                dve.memset(src_i[:, :], 0).then_inc(cleared, 1)
                dve.memset(dst_i[:, :], 0).then_inc(cleared, 1)
                dve.memset(x_sb[:, NB - 1, :], 0.0).then_inc(tailz, 1)
                dve.wait_ge(loaded, 32)
                dve.tensor_scalar(blk_i[:, :], src_i[:, :], 7, None, ALU.logical_shift_right).then_inc(edge_ids, 1)
                dve.tensor_copy(k["ends"][:, :, 0], src_i[:, :]).then_inc(chain, 1)
                dve.tensor_copy(k["ends"][:, :, 1], dst_i[:, :]).then_inc(chain, 1)
                dve.wait_ge(edge_ids, 1)
                dve.tensor_copy(blk[:, :], blk_i[:, :]).then_inc(edge_ids, 1)
                dve.tensor_scalar(src_i[:, :], src_i[:, :], P - 1, None, ALU.bitwise_and).then_inc(edge_ids, 1)
                dve.wait_ge(edge_ids, 3)
                dve.tensor_copy(loc[:, 0:T], src_i[:, :]).then_inc(edge_ids, 1)
                dve.memset(loc[:, T:T + GT], -1.0)
                for b in range(NB):
                    if b % 4 == 0:
                        dve.wait_ge(xin[b // 4], 16 if b < 16 else 32)
                    dve.bn_stats(st[:, b, :], x_sb[:, b, :]).then_inc(stats, 1)
                dve.wait_ge(stats, NB)
                for b in range(NB):
                    dve.bn_aggr(mv[:, b, :], st[:, b, :]).then_inc(stats, 1)
                dve.wait_ge(stats, 2 * NB)
                normalise_stats(dve, rready, rdone, link, mv, var[:, :], root[:, :], rstd[:, :])

                def normalise(b, j):
                    dve.tensor_scalar(xn[:, j, :], x_sb[:, bass.ds(b, 1), :].rearrange("p a f -> p (a f)"),
                                      mv[:, bass.ds(b, 1), 0], rstd[:, bass.ds(b, 1)],
                                      ALU.subtract, ALU.mult).then_inc(xn_ready, 1)

                def finish(b, j):
                    dve.wait_ge(sq_ready, b + 1)
                    dve.tensor_copy(row[:, j, 0:F], r_ps[:, j, :]).then_inc(hr_copied, 1)
                    dve.tensor_tensor(sqa[:, j, :, :], sq[:, j, :, :], half[:, :, :], ALU.mult).then_inc(sqa_ready, 1)
                    dve.wait_ge(sqa_ready, b + 1)
                    dve.tensor_reduce(own[:, j, :], sqa[:, j, :, :], AX_X, ALU.add).then_inc(own_ready, 1)
                    dve.wait_ge(own_ready, b + 1)
                    dve.wait_ge(hr_copied, b + 1)
                    dve.tensor_tensor(row[:, j, F:TW].rearrange("p (a h) -> p a h", a=2),
                                      l_ps[:, j, :].rearrange("p (a h) -> p a h", a=2),
                                      bcast(own[:, j, :], 1, 2), ALU.add).then_inc(row_ready, 1)

                def one_hots(c, j):
                    dve.tensor_tensor(hot[:, j, :, :], bcast(loc[:, bass.ds(c * CPB, CPB)], 2, P),
                                      bcast(k["iota"][:, :], 1, CPB), ALU.is_equal).then_inc(hots, 1)

                normalise(0, 0)
                normalise(1, 1)
                dve.wait_ge(valid, 2)
                one_hots(0, 0)
                one_hots(1, 1)
                dve.tensor_tensor(oh_blk[:, :, :], bcast(blk[:, :], 2, NB), bcast(k["iota"][:, 0:NB], 1, T),
                                  ALU.is_equal).then_inc(blk_hot, 1)
                dve.wait_ge(win, 32 * CH)
                dve.wait_ge(ain, 16)
                w4e = w_e[:, :, :].rearrange("p c (h d) -> p c h d", h=HEADS)
                w4r = w_r[:, :, :].rearrange("p c (h d) -> p c h d", h=HEADS)
                for w, part, out in ((w4r, 2, dif[:, :, :]), (w4e, 0, lin[:, :, 0:HEADS]), (w4e, 1, lin[:, :, HEADS:])):
                    link(dve.tensor_tensor(prod[:, :, :, :], w, bcast(a_all[:, :, part * D:(part + 1) * D], 1, CH), ALU.mult))
                    link(dve.tensor_reduce(out, prod[:, :, :, :], AX_X, ALU.add))
                link(dve.tensor_scalar(half[:, :, :], a_all[:, :, 4 * D:], 0.5, None, ALU.mult))
                dve.tensor_tensor(lin[:, :, 0:HEADS], lin[:, :, 0:HEADS], dif[:, :, :], ALU.subtract).then_inc(chain, 1)
                dve.tensor_tensor(lin[:, :, HEADS:], lin[:, :, HEADS:], dif[:, :, :], ALU.add).then_inc(linr, 1)
                finish(0, 0)

                def pair(i):
                    for j in range(2):
                        b = 2 * i + j
                        dve.wait_ge(tp, b - 1)
                        normalise(b, j)
                        if not (isinstance(b, int) and b == 2):
                            dve.wait_ge(row_out[1 - j], 16 * (i + j) - 16)
                        finish(b - 1, 1 - j)
                        dve.wait_ge(counted, b - 1)
                        one_hots(b, j)

                pair(1)
                with dve.Fori(2, NB // 2) as i:
                    pair(i)
                dve.wait_ge(row_out[1], 16 * (NB // 2 - 1))
                finish(NB - 1, 1)


def score_edges(nc, k, sem, a, table_d, sorted_d):
    RING = 4
    first, oh_blk = k["first"], k["oh_blk"]
    with ExitStack() as ctx:
        s = Space(nc, ctx)
        ix = s.sb("ix", [P, RING * GT, 2], U32)
        rowix = s.sb("rowix", [P, RING, GT], U32)
        gs = s.sb("gs", [P, RING * GT, TW])
        gd = s.sb("gd", [P, RING * GT, TW])
        ab = s.sb("ab", [P, 2, CH, GT * P])
        uv = s.sb("uv", [P, 2, CH, GT * P])
        ssum = s.sb("ssum", [HEADS, GT * P])
        rowt = s.sb("rowt", [P, RING, GT, RW], U32)
        sc = s.sb("sc", [P, 2, GT, HEADS])
        raw = s.sb("raw_a", [P, 2, CH])
        heads = s.sb("heads", [P, CH, HEADS])
        total = s.sb("total", [P, NB])
        bi = s.sb("bi", [P, NB], I32)
        nt = s.sb("nt", [P, NB])
        ends = s.sb("ends", [P, NB])
        start = s.sb("start", [P, NB])
        hot = s.sb("hot_e", [P, 2, GT, P], BF16)
        hot_t = s.sb("hot_t", [P, GT, P])
        earlier = s.sb("earlier", [P, 2, GT, P], BF16)
        picked = s.sb("picked", [P, GT, NB])
        pos = s.sb("pos", [P, GT])
        posi = s.sb("posi", [P, 3, GT], I32)
        posf = s.sb("posf", [P, GT])
        d_ps = s.ps("d_ps", [P, 2, GT * P])
        s_ps = s.ps("s_ps", [P, 2, 512])
        back_ps = s.ps("back_ps", [P, GT, HEADS])
        tr_ps = s.ps("tr_ps", [P, GT, P], BF16)
        same_ps = s.ps("same_ps", [P, GT, P])
        look_ps = s.ps("look_ps", [P, GT, NB])

        ain, az, wready, chain = sem("score_a_in"), sem("score_a_zero"), sem("score_weights"), sem("score_chain")
        tot, totps, firsts = sem("totals"), sem("totals_ps"), sem("firsts_ready")
        ixr = sem("indices_ready")
        got = [sem(f"rows_in{j}") for j in range(RING * GT)]
        out = [sem(f"scores_out{j}") for j in range(RING)]
        dready, dturned, abr, ur, vr, red = (sem("diff_ready"), sem("diff_turned"), sem("abs_ready"), sem("u_ready"),
                                             sem("v_ready"), sem("reduced"))
        ssr, back, s1, s2, scored, idr = (sem("sums_ready"), sem("sums_back"), sem("score_p"), sem("score_pq"),
                                          sem("scored"), sem("row_ids"))
        hotr, tr_done, htr, same_done, early_ready, look_done = (sem("rank_hot"), sem("rank_tr"), sem("rank_hot_t"),
                                                                 sem("rank_same"), sem("rank_early"), sem("rank_look"))
        pmul, pch, rowr = sem("rank_mul"), sem("rank_pos"), sem("rows_ready")

        with nc.Block() as block:
            @block.sync
            def _(sp):
                for half in range(2):
                    for n, part in enumerate((3, 4)):
                        sp.dma_start(raw[half * D:(half + 1) * D, n, :],
                                     a.rearrange("(c t) f -> f c t", t=2)[part * D:(part + 1) * D, :, half],
                                     allow_slow_non_contiguous=True).then_inc(ain, 16)

            @block.gpsimd
            def _(pool):
                def gather(g, r):
                    for t in range(GT):
                        j = r * GT + t
                        pool.tensor_copy(ix[:, j, :], k["ends"][:, bass.ds(g * GT + t, 1), :].rearrange("p a w -> p (a w)")
                                         ).then_inc(ixr, 1)
                    pool.wait_ge(ixr, g * GT + GT)
                    pool.nop(nofuse=True)
                    for t in range(GT):
                        j = r * GT + t
                        pool.indirect_dma_start(gs[:, j, :], None, table_d,
                                                bass.IndirectOffsetOnAxis(ap=ix[:, j, 0:1], axis=0)).then_inc(got[j], 16)
                        pool.indirect_dma_start(gd[:, j, :], None, table_d,
                                                bass.IndirectOffsetOnAxis(ap=ix[:, j, 1:2], axis=0)).then_inc(got[j], 16)

                def scatter(g, r):
                    pool.wait_ge(scored, g + 1)
                    pool.nop(nofuse=True)
                    for t in range(GT):
                        pool.indirect_dma_start(sorted_d, bass.IndirectOffsetOnAxis(ap=rowix[:, r, t:t + 1], axis=0),
                                                rowt[:, r, t, :], None).then_inc(out[r], 16)

                gather(0, 0)
                gather(1, 1)
                for g in range(2, RING):
                    gather(g, g)
                    scatter(g - 2, g - 2)
                with pool.Fori(1, GROUPS // RING) as i:
                    for r in range(RING):
                        gather(RING * i + r, r)
                        scatter(RING * i + r - 2, (r - 2) % RING)
                scatter(GROUPS - 2, RING - 2)
                scatter(GROUPS - 1, RING - 1)
                for r in range(RING):
                    pool.wait_ge(out[r], 16 * GT * (GROUPS // RING))

            @block.vector
            def _(dve):
                link = chained(dve, chain)
                dve.memset(heads[:, :, :], 0.0).then_inc(az, 1)
                dve.memset(rowt[:, :, :, :], 0).then_inc(az, 1)
                dve.tensor_reduce(total[:, :], first[:, :, 1:T + 1], AX_X, ALU.add).then_inc(tot, 1)
                dve.wait_ge(az, 2)
                dve.wait_ge(ain, 64)
                for c in range(CH):
                    for half in range(2):
                        h = 2 * c + half
                        dve.memset(heads[half * D:(half + 1) * D, c, h:h + 1], 1.0).then_inc(wready, 1)
                dve.tensor_scalar(raw[:, 1, :], raw[:, 1, :], -0.5, None, ALU.mult).then_inc(wready, 1)
                dve.wait_ge(totps, 1)
                link(dve.tensor_scalar(bi[:, :], s_ps[:, 1, 0:NB], float(P - 1), None, ALU.add))
                link(dve.tensor_scalar(bi[:, :], bi[:, :], 7, None, ALU.logical_shift_right))
                link(dve.tensor_copy(nt[:, :], bi[:, :]))
                link(dve.tensor_tensor_scan(ends[:, :], k["ones"][:, 0:NB], nt[:, :], 0.0, ALU.mult, ALU.add))
                link(dve.tensor_tensor(start[:, :], ends[:, :], nt[:, :], ALU.subtract))
                link(dve.tensor_copy(k["first_tile"][:, :], start[:, :]))
                link(dve.scalar_tensor_tensor(first[:, :, 0], start[:, :], float(P), s_ps[:, 0, 0:NB],
                                              ALU.mult, ALU.add))
                flat = first[:, :, :].rearrange("p b t -> p (b t)")
                dve.tensor_tensor_scan(flat, k["same"][:, :, :].rearrange("p b t -> p (b t)"), flat, 0.0,
                                       ALU.mult, ALU.add).then_inc(firsts, 1)

                def one_hot(g, j):
                    dve.tensor_tensor(hot[:, j, :, :], bcast(k["loc"][:, bass.ds(g * GT, GT)], 2, P),
                                      bcast(k["iota"][:, :], 1, GT), ALU.is_equal).then_inc(hotr, 1)

                def subtract(g, r, i):
                    for t in range(GT):
                        j = r * GT + t
                        dve.wait_ge(got[j], 32 * i + 32)
                        last = dve.tensor_tensor(gs[:, j, 0:F], gd[:, j, 0:F], gs[:, j, 0:F], ALU.subtract)
                    last.then_inc(dready, 1)

                def mark_earlier(g, j):
                    dve.wait_ge(same_done, g + 1)
                    dve.tensor_tensor(earlier[:, j, :, :], same_ps[:, :, :], bcast(k["before"][:, :], 1, GT),
                                      ALU.mult).then_inc(early_ready, 1)

                def combine(g, j):
                    for c in range(CH):
                        dve.wait_ge(ur, CH * g + c + 1)
                        dve.tensor_tensor(uv[:, j, c, :], uv[:, j, c, :], ab[:, j, c, :], ALU.mult).then_inc(vr, 1)

                def place(g, r):
                    dve.wait_ge(look_done, g + 1)
                    dve.tensor_tensor(picked[:, :, :], look_ps[:, :, :], oh_blk[:, bass.ds(g * GT, GT), :],
                                      ALU.mult).then_inc(pmul, 1)
                    dve.wait_ge(pmul, g + 1)
                    dve.tensor_reduce(pos[:, :], picked[:, :, :], AX_X, ALU.add).then_inc(pch, 1)
                    dve.wait_ge(pch, 5 * g + 1)
                    dve.tensor_copy(posi[:, 0, :], pos[:, :]).then_inc(pch, 1)
                    dve.wait_ge(pch, 5 * g + 2)
                    dve.tensor_scalar(posi[:, 1, :], posi[:, 0, :], P - 1, None, ALU.bitwise_and).then_inc(pch, 1)
                    dve.tensor_scalar(posi[:, 2, :], posi[:, 0, :], 7, None, ALU.logical_shift_right).then_inc(pch, 1)
                    dve.wait_ge(pch, 5 * g + 4)
                    dve.scalar_tensor_tensor(posf[:, :], posi[:, 1, :], float(Q), posi[:, 2, :],
                                             ALU.mult, ALU.add).then_inc(pch, 1)
                    dve.wait_ge(pch, 5 * g + 5)
                    dve.tensor_tensor(rowix[:, r, :], posf[:, :], k["dump"][:, bass.ds(g * GT, GT)], ALU.add).then_inc(rowr, 1)

                def keep_sums(g, j):
                    dve.wait_ge(red, g + 1)
                    dve.tensor_copy(ssum[:, :], s_ps[0:HEADS, j, :]).then_inc(ssr, 1)

                def score(g, j, r):
                    rows = slice(r * GT, (r + 1) * GT)
                    dve.wait_ge(back, g + 1)
                    dve.tensor_tensor(sc[:, j, :, :], back_ps[:, :, :], gs[:, rows, F:F + HEADS], ALU.add).then_inc(s1, 1)
                    dve.tensor_copy(rowt[:, r, :, HEADS:HEADS + 2], k["ends"][:, bass.ds(g * GT, GT), :]).then_inc(idr, 1)
                    dve.wait_ge(s1, g + 1)
                    dve.tensor_tensor(sc[:, j, :, :], sc[:, j, :, :], gd[:, rows, F + HEADS:TW], ALU.add).then_inc(s2, 1)
                    dve.wait_ge(s2, g + 1)
                    dve.wait_ge(idr, g + 1)
                    dve.wait_ge(rowr, g + 1)
                    dve.scalar_tensor_tensor(rowt[:, r, :, 0:HEADS].bitcast(F32), sc[:, j, :, :], SLOPE, sc[:, j, :, :],
                                             ALU.mult, ALU.max).then_inc(scored, 1)

                def step(g, r, i):
                    j = r % 2
                    known = isinstance(g, int)
                    inside = not (known and g >= GROUPS)
                    if inside:
                        subtract(g, r, i)
                        one_hot(g + 1, 1 - j)
                    if not (known and g == 0):
                        combine(g - 1, 1 - j)
                        keep_sums(g - 1, 1 - j)
                    if inside:
                        mark_earlier(g, j)
                    if not (known and g == 0):
                        rp = (r - 1) % RING
                        if not (known and g - 1 < RING):
                            dve.wait_ge(out[rp], 16 * GT * (i if r >= 1 else i - 1))
                        place(g - 1, rp)
                        score(g - 1, 1 - j, rp)

                one_hot(0, 0)
                for g in range(RING + 1):
                    step(g, g % RING, g // RING)
                for g in range(RING + 1, 2 * RING):
                    step(g, g % RING, 1)
                with dve.Fori(2, GROUPS // RING) as i:
                    for r in range(RING):
                        step(RING * i + r, r, i)
                step(GROUPS, 0, GROUPS // RING)

            @block.tensor
            def _(pe):
                pe.wait_ge(tot, 1)
                pe.matmul(s_ps[:, 0, 0:NB], k["before"][:, :], total[:, :], start=True, stop=True)
                pe.matmul(s_ps[:, 1, 0:NB], k["ones"][:, :], total[:, :], start=True, stop=True).then_inc(totps, 1)
                pe.wait_ge(wready, 2 * CH + 1)
                pe.wait_ge(firsts, 1)

                def turn_hot(g, j):
                    pe.wait_ge(hotr, g + 1)
                    for t in range(GT):
                        last = pe.transpose(tr_ps[:, t, :], hot[:, j, t, :], k["ident_bf"][:, :])
                    last.then_inc(tr_done, 1)

                def compare(g):
                    pe.wait_ge(htr, g + 1)
                    for t in range(GT):
                        last = pe.matmul(same_ps[:, t, :], hot_t[:, t, :], hot_t[:, t, :], start=True, stop=True)
                    last.then_inc(same_done, 1)

                def look(g, j):
                    pe.wait_ge(early_ready, g + 1)
                    if not (isinstance(g, int) and g == 0):
                        pe.wait_ge(pmul, g)
                    for t in range(GT):
                        pe.matmul(look_ps[:, t, :], earlier[:, j, t, :],
                                  oh_blk[:, bass.ds(g * GT + t, 1), :].rearrange("p a b -> p (a b)"),
                                  start=True, stop=False)
                        last = pe.matmul(look_ps[:, t, :], hot_t[:, t, :],
                                         first[:, :, bass.ds(g * GT + t, 1)].rearrange("p b a -> p (b a)"),
                                         start=False, stop=True)
                    last.then_inc(look_done, 1)

                def turn(g, r, c):
                    if c == 0:
                        pe.wait_ge(dready, g + 1)
                    if not (isinstance(g, int) and g == 0 and c < 2):
                        pe.wait_ge(abr, CH * g + c - 1)
                    for t in range(GT):
                        last = pe.transpose(d_ps[:, c % 2, t * P:(t + 1) * P], gs[:, r * GT + t, c * P:(c + 1) * P],
                                            k["ident"][:, :])
                    last.then_inc(dturned, 1)

                def reduce(g, j, c):
                    pe.wait_ge(vr, CH * g + c + 1)
                    last = pe.matmul(s_ps[0:HEADS, j, :], heads[:, c, :], uv[:, j, c, :], start=(c == 0), stop=(c == CH - 1))
                    if c == CH - 1:
                        last.then_inc(red, 1)

                def bring_back(g):
                    pe.wait_ge(ssr, g + 1)
                    pe.nop(nofuse=True)
                    for t in range(GT):
                        last = pe.transpose(back_ps[:, t, :], ssum[:, t * P:(t + 1) * P], k["ident"][0:HEADS, 0:HEADS])
                    last.then_inc(back, 1)

                def step(g, r):
                    j = r % 2
                    known = isinstance(g, int)
                    inside, after = not (known and g >= GROUPS), not (known and g == 0)
                    if after:
                        look(g - 1, 1 - j)
                    if inside:
                        turn_hot(g, j)
                        turn(g, r, 0)
                        turn(g, r, 1)
                    if after:
                        reduce(g - 1, 1 - j, 0)
                        reduce(g - 1, 1 - j, 1)
                    if inside:
                        compare(g)
                        turn(g, r, 2)
                        turn(g, r, 3)
                    if after:
                        reduce(g - 1, 1 - j, 2)
                        reduce(g - 1, 1 - j, 3)
                        bring_back(g - 1)

                for g in range(RING):
                    step(g, g)
                with pe.Fori(1, GROUPS // RING) as i:
                    for r in range(RING):
                        step(RING * i + r, r)
                step(GROUPS, 0)

            @block.scalar
            def _(act):
                act.wait_ge(wready, 2 * CH + 1)

                def step(g, j):
                    known = isinstance(g, int)
                    act.wait_ge(tr_done, g + 1)
                    if not (known and g == 0):
                        act.wait_ge(look_done, g)
                    act.copy(hot_t[:, :, :], tr_ps[:, :, :]).then_inc(htr, 1)
                    if not (known and g < 2):
                        act.wait_ge(red, g - 1)
                    for c in range(CH):
                        act.wait_ge(dturned, CH * g + c + 1)
                        act.activation(ab[:, j, c, :], d_ps[:, c % 2, :], ACT.Abs).then_inc(abr, 1)
                        act.wait_ge(abr, CH * g + c + 1)
                        act.activation(uv[:, j, c, :], ab[:, j, c, :], ACT.Identity, bias=raw[:, 0, c:c + 1],
                                       scale=raw[:, 1, c:c + 1]).then_inc(ur, 1)

                step(0, 0)
                step(1, 1)
                with act.Fori(1, GROUPS // 2) as i:
                    for j in range(2):
                        step(2 * i + j, j)


def edge_softmax(nc, k, sem, sorted_d):
    L = SQ * P
    with ExitStack() as ctx:
        s = Space(nc, ctx)
        rows = s.sb("rows", [P, Q, RW], U32)
        keys = s.sb("keys", [P, SQ, STRIPS, HEADS])
        scores = s.sb("scores", [P, SQ, STRIPS, HEADS])
        keyq = s.sb("keyq", [P, Q])
        cmp = s.sb("cmp", [P, Q, NB - 1], BF16)
        qi = s.sb("qi", [P, Q], I32)
        qf = s.sb("qf", [P, Q])
        tb = s.sb("tb", [P, Q])
        al = s.sb("al", [P, L])
        ky = s.sb("ky", [P, L])
        cont = s.sb("cont", [P, L + 1])
        pen = s.sb("pen", [P, L + 1])
        fw = s.sb("fw", [P, L])
        top = s.sb("top", [P, L])
        ex = s.sb("ex", [P, L])
        den = s.sb("den", [P, L])
        whole = s.sb("whole", [P, 4])
        edge = s.sb("edge", [P, 1])
        carry = s.sb("carry", [P, 1])
        hm = s.sb("hm", [1, 2, HEADS, STRIPS])
        run = s.sb("run", [1, HEADS, STRIPS])
        cin = s.sb("cin", [1, STRIPS, HEADS])
        shift_t = s.sb("shift_t", [P, P])
        a_ps = s.ps("a_ps", [P, 2, 512])
        k_ps = s.ps("k_ps", [P, 2, 512])
        c_ps = s.ps("c_ps", [P, 4, 512])

        rin, qr, kready, chain = sem("rows_in"), sem("tile_numbers"), sem("keys_ready"), sem("softmax_chain")
        kready0, scready = sem("key_read"), sem("scores_laid")
        ta, tk, ea, ek = sem("scores_turned"), sem("keys_turned"), sem("scores_kept"), sem("keys_kept")
        ask, answer = sem("carry_ask"), sem("carry_answer")
        sub, exped, att_ready, tb_done, tkept = sem("shifted"), sem("exped"), sem("att_ready"), sem("att_turned"), sem("att_kept")
        groups = [range(g, min(g + 4, SQ)) for g in range(0, SQ, 4)]

        with nc.Block() as block:
            @block.sync
            def _(sp):
                sp.dma_start(rows[:, :, :], sorted_d[0:CAP, :].rearrange("(p q) w -> p q w", p=P)).then_inc(rin, 16)

            @block.gpsimd
            def _(pool):
                pool.iota(qi[:, :], pattern=[[1, Q]], base=0, channel_multiplier=0).then_inc(qr, 1)
                pool.wait_ge(qr, 1)
                pool.tensor_copy(qf[:, :], qi[:, :]).then_inc(qr, 1)
                pool.wait_ge(rin, 16)
                pool.tensor_copy(k["target"][:, :], rows[:, :, HEADS + 1]).then_inc(qr, 1)

            @block.tensor
            def _(pe):
                pe.wait_ge(rin, 16)
                pe.wait_ge(kready, 1)
                pe.wait_ge(scready, 1)
                for g, ts in enumerate(groups):
                    if g >= 2:
                        pe.wait_ge(ea, g - 1)
                        pe.wait_ge(ek, g - 1)
                    for n, t in enumerate(ts):
                        la = pe.transpose(a_ps[:, g % 2, n * P:(n + 1) * P], scores[:, t, :, :].rearrange("p s h -> p (s h)"), k["ident"][:, :])
                    la.then_inc(ta, 1)
                    for n, t in enumerate(ts):
                        lk = pe.transpose(k_ps[:, g % 2, n * P:(n + 1) * P], keys[:, t, :, :].rearrange("p s h -> p (s h)"), k["ident"][:, :])
                    lk.then_inc(tk, 1)
                pe.wait_ge(ask, 1)
                pe.transpose(c_ps[:, 0, 0:P], k["shift"][:, :], k["ident"][:, :]).then_inc(answer, 1)
                pe.matmul(c_ps[:, 1, 0:1], k["shift"][:, :], ky[:, L - 1:L], start=True, stop=True).then_inc(answer, 1)
                pe.wait_ge(ask, 2)
                pe.matmul(c_ps[:, 2, 0:1], shift_t[:, :], cont[:, 0:1], start=True, stop=True).then_inc(answer, 1)
                n = 3
                for whole_col in (1, 3, 0, 3):
                    pe.wait_ge(ask, n)
                    pe.transpose(c_ps[0:1, 0, 0:P], whole[:, whole_col:whole_col + 1], k["ident"][:, :])
                    pe.transpose(c_ps[0:1, 1, 0:P], edge[:, :], k["ident"][:, :]).then_inc(answer, 1)
                    pe.wait_ge(ask, n + 1)
                    pe.transpose(c_ps[:, 2, 0:1], cin[:, :, :].rearrange("p s h -> p (s h)"), k["ident"][0:1, 0:1]).then_inc(answer, 1)
                    n += 2
                pe.wait_ge(att_ready, 1)
                for g, ts in enumerate(groups):
                    if g >= 2:
                        pe.wait_ge(tkept, g - 1)
                    for n, t in enumerate(ts):
                        last = pe.transpose(a_ps[:, g % 2, n * P:(n + 1) * P], ex[:, t * P:(t + 1) * P], k["ident"][:, :])
                    last.then_inc(tb_done, 1)

            @block.scalar
            def _(act):
                act.wait_ge(rin, 16)
                act.copy(scores[:, :, :, :],
                         rows[:, :, 0:HEADS].bitcast(F32).rearrange("p (s t) h -> p t s h", t=SQ)).then_inc(scready, 1)
                for g, ts in enumerate(groups):
                    act.wait_ge(ta, g + 1)
                    act.copy(al[:, ts[0] * P:(ts[-1] + 1) * P], a_ps[:, g % 2, 0:len(ts) * P]).then_inc(ea, 1)
                act.wait_ge(sub, 1)
                act.activation(ex[:, :], top[:, :], ACT.Exp).then_inc(exped, 1)
                att4 = k["att"][:, :, :].rearrange("p (s t) h -> p t s h", t=SQ)
                for g, ts in enumerate(groups):
                    act.wait_ge(tb_done, g + 1)
                    act.copy(att4[:, ts[0]:ts[-1] + 1, :, :],
                             a_ps[:, g % 2, 0:len(ts) * P].rearrange("p (t s h) -> p t s h", s=STRIPS, h=HEADS)).then_inc(tkept, 1)

            @block.vector
            def _(dve):
                link = chained(dve, chain)
                dve.wait_ge(rin, 16)
                dve.tensor_scalar(keyq[:, :], rows[:, :, HEADS], 1.0, None, ALU.add).then_inc(kready0, 1)
                dve.wait_ge(kready0, 1)
                dve.tensor_copy(keys[:, :, :, :], bcast(keyq[:, :].rearrange("p (s t) -> p t s", t=SQ), 3, HEADS)).then_inc(kready, 1)
                dve.wait_ge(qr, 2)
                link(dve.tensor_tensor(cmp[:, :, :], bcast(qf[:, :], 2, NB - 1), bcast(k["first_tile"][:, 1:NB], 1, Q), ALU.is_ge))
                link(dve.tensor_reduce(tb[:, :], cmp[:, :, :], AX_X, ALU.add))
                link(dve.tensor_copy(k["tile_block"][:, :], tb[:, :]))
                dve.wait_ge(kready, 1)
                link(dve.scalar_tensor_tensor(k["local"][:, :], tb[:, :], -float(P), keyq[:, :], ALU.mult, ALU.add))
                link(dve.tensor_scalar(k["local"][:, :], k["local"][:, :], -1.0, None, ALU.add))
                for g, ts in enumerate(groups):
                    dve.wait_ge(tk, g + 1)
                    dve.tensor_copy(ky[:, ts[0] * P:(ts[-1] + 1) * P], k_ps[:, g % 2, 0:len(ts) * P]).then_inc(ek, 1)
                dve.wait_ge(ek, len(groups))
                dve.nop().then_inc(ask, 1)
                dve.wait_ge(answer, 2)
                link(dve.tensor_copy(shift_t[:, :], c_ps[:, 0, 0:P]))
                link(dve.tensor_tensor(cont[:, 1:L], ky[:, 1:L], ky[:, 0:L - 1], ALU.is_equal))
                dve.tensor_tensor(cont[:, 0:1], ky[:, 0:1], c_ps[:, 1, 0:1], ALU.is_equal).then_inc(ask, 1)
                dve.wait_ge(answer, 3)
                link(dve.tensor_copy(cont[:, L:L + 1], c_ps[:, 2, 0:1]))
                link(dve.tensor_scalar(pen[:, :], cont[:, :], -1.0, BIG, ALU.add, ALU.mult))
                link(dve.tensor_reduce(whole[:, 0:1], cont[:, 0:L], AX_X, ALU.min))
                link(dve.tensor_reduce(whole[:, 1:2], pen[:, 0:L], AX_X, ALU.min))
                link(dve.tensor_reduce(whole[:, 3:4], pen[:, 1:L + 1], AX_X, ALU.min))
                link(dve.memset(cin[:, :, :], 0.0))
                asked = [2]
                answered = [3]

                def segments(out, gate, data, neutral, op0, op1, back):
                    flip = (lambda ap: ap[:, ::-1]) if back else (lambda ap: ap)
                    link(dve.tensor_tensor_scan(flip(out), flip(gate), flip(data), neutral, op0, op1))
                    end = out[:, 0:1] if back else out[:, L - 1:L]
                    dve.tensor_copy(edge[:, :], end).then_inc(ask, 1)
                    asked[0] += 1
                    answered[0] += 1
                    dve.wait_ge(answer, answered[0])
                    order = slice(None, None, -1) if back else slice(None)
                    for n in range(2):
                        got = c_ps[0:1, n, 0:P].rearrange("p (s h) -> p h s", h=HEADS)
                        link(dve.tensor_copy(hm[:, n, :, :], got[:, :, order]))
                    flat = lambda ap: ap.rearrange("p h s -> p (h s)")
                    link(dve.tensor_tensor_scan(flat(run[:, :, :]), flat(hm[:, 0, :, :]), flat(hm[:, 1, :, :]),
                                                neutral, op0, op1))
                    took = run[:, :, 0:STRIPS - 1].rearrange("p h s -> p s h")
                    if back:
                        link(dve.memset(cin[:, STRIPS - 1:STRIPS, :], 0.0))
                        dve.tensor_copy(cin[:, 0:STRIPS - 1, :], took[:, ::-1, :]).then_inc(ask, 1)
                    else:
                        link(dve.memset(cin[:, 0:1, :], 0.0))
                        dve.tensor_copy(cin[:, 1:STRIPS, :], took).then_inc(ask, 1)
                    asked[0] += 1
                    answered[0] += 1
                    dve.wait_ge(answer, answered[0])
                    link(dve.tensor_copy(carry[:, :], c_ps[:, 2, 0:1]))
                    link(dve.tensor_tensor_scan(flip(out), flip(gate), flip(data), carry[:, :], op0, op1))

                dve.wait_ge(ea, len(groups))
                segments(fw[:, :], pen[:, 0:L], al[:, :], -BIG, ALU.add, ALU.max, False)
                segments(top[:, :], pen[:, 1:L + 1], fw[:, :], -BIG, ALU.add, ALU.max, True)
                dve.tensor_tensor(top[:, :], al[:, :], top[:, :], ALU.subtract).then_inc(sub, 1)
                dve.wait_ge(exped, 1)
                segments(fw[:, :], cont[:, 0:L], ex[:, :], 0.0, ALU.mult, ALU.add, False)
                segments(den[:, :], pen[:, 1:L + 1], fw[:, :], 0.0, ALU.add, ALU.max, True)
                link(dve.tensor_scalar(den[:, :], den[:, :], 1e-16, None, ALU.add))
                link(dve.reciprocal(den[:, :], den[:, :]))
                dve.tensor_tensor(ex[:, :], ex[:, :], den[:, :], ALU.mult).then_inc(att_ready, 1)


def sum_messages(nc, k, sem, he_d):
    SL, AHEAD, LAG, BK = 8, 6, 3, 4
    x_sb = k["x_sb"]
    with ExitStack() as ctx:
        s = Space(nc, ctx)
        ix = s.sb("ixm", [P, SL], U32)
        g = s.sb("g", [P, SL, HEADS, D])
        msg = s.sb("msg", [P, SL, HEADS, D])
        hot = s.sb("hot", [P, SL, P])
        m_ps = s.ps("m_ps", [P, 4, F])
        ixr, hots, summed, added = sem("m_indices"), sem("m_hot"), sem("m_summed"), sem("m_added")
        made = sem("m_made")
        got = [sem(f"m_rows_in{j}") for j in range(SL)]

        with nc.Block() as block:
            @block.gpsimd
            def _(pool):
                def gather(q, j):
                    pool.tensor_copy(ix[:, j:j + 1], k["target"][:, bass.ds(q, 1)]).then_inc(ixr, 1)
                    pool.wait_ge(ixr, q + 1)
                    pool.nop(nofuse=True)
                    pool.indirect_dma_start(g[:, j, :, :].rearrange("p h d -> p (h d)"), None, he_d,
                                            bass.IndirectOffsetOnAxis(ap=ix[:, j:j + 1], axis=0)).then_inc(got[j], 16)

                for q in range(SL):
                    gather(q, q)
                with pool.Fori(1, Q // SL) as i:
                    for j in range(SL):
                        pool.wait_ge(made, SL * i + j - SL + 1)
                        gather(SL * i + j, j)

            @block.vector
            def _(dve):
                def prepare(q, j, n):
                    dve.tensor_scalar(hot[:, j, :], k["iota"][:, :], k["local"][:, bass.ds(q, 1)], None,
                                      ALU.is_equal).then_inc(hots, 1)
                    dve.wait_ge(got[j], 16 * n + 16)
                    dve.tensor_tensor(msg[:, j, :, :], g[:, j, :, :],
                                      bcast(k["att"][:, bass.ds(q, 1), :].rearrange("p a h -> p (a h)"), 2, D),
                                      ALU.mult).then_inc(made, 1)

                def add(q, j):
                    b = dve.value_load(k["tile_block"][0:1, bass.ds(q, 1)], min_val=0, max_val=NB - 1)
                    dve.wait_ge(summed, q + 1)
                    sl = x_sb[:, bass.ds(b, 1), :].rearrange("p a f -> p (a f)")
                    dve.tensor_tensor(sl, m_ps[:, j % BK, :], sl, ALU.add).then_inc(added, 1)

                def step(q, j, n):
                    prepare(q, j, n)
                    if isinstance(q, int) and q < LAG:
                        return
                    if not (isinstance(q, int) and q == LAG):
                        dve.wait_ge(added, q - LAG)
                    add(q - LAG, (j - LAG) % SL)

                for q in range(SL):
                    step(q, q, 0)
                with dve.Fori(1, Q // SL) as i:
                    for j in range(SL):
                        step(SL * i + j, j, i)
                for q in range(Q - LAG, Q):
                    dve.wait_ge(added, q)
                    add(q, q % SL)

            @block.tensor
            def _(pe):
                def total(q, j):
                    pe.wait_ge(hots, q + 1)
                    pe.wait_ge(made, q + 1)
                    pe.matmul(m_ps[:, j % BK, :], hot[:, j, :], msg[:, j, :, :].rearrange("p h d -> p (h d)"),
                              start=True, stop=True).then_inc(summed, 1)

                for q in range(SL):
                    if q >= BK:
                        pe.wait_ge(added, q - BK + 1)
                    total(q, q)
                with pe.Fori(1, Q // SL) as i:
                    for j in range(SL):
                        q = SL * i + j
                        pe.wait_ge(added, q - BK + 1)
                        total(q, j)


def route(nc, k, sem, wg):
    x_sb = k["x_sb"]
    with ExitStack() as ctx:
        s = Space(nc, ctx)
        st = s.sb("st2", [P, NB, 6])
        mv = s.sb("mv2", [P, NB, 2])
        var = s.sb("var2", [P, NB])
        root = s.sb("root2", [P, NB])
        rstd = s.sb("rstd2", [P, NB])
        xn = s.sb("xn2", [P, 2, F])
        wg_sb = s.sb("wg_sb", [P, CH, EXPERTS])
        rankw = s.sb("rankw", [P, EXPERTS])
        lg = s.sb("lg", [P, NB, EXPERTS])
        g = s.sb("gate", [P, NB, EXPERTS])
        m1 = s.sb("mask1", [P, NB, EXPERTS])
        m2 = s.sb("mask2", [P, NB, EXPERTS])
        tmp = s.sb("tmp", [P, NB, EXPERTS])
        v1 = s.sb("v1", [P, NB])
        v2 = s.sb("v2", [P, NB])
        v3 = s.sb("v3", [P, NB])
        t_ps = s.ps("t2_ps", [P, 2, F])
        g_ps = s.ps("g_ps", [P, NB, EXPERTS])

        stats, chain, rready, rdone, wgin = sem("stats2"), sem("route_chain"), sem("var_ready2"), sem("root_done2"), sem("wg_in")
        xn_ready, tp, xt_ready, gated, lgr, exped = sem("xn_ready2"), sem("x_turned2"), sem("xt_ready2"), sem("gated"), sem("logits"), sem("gate_exped")

        with nc.Block() as block:
            @block.sync
            def _(sp):
                sp.dma_start(wg_sb[:, :, :], wg.rearrange("(c p) e -> p c e", p=P)).then_inc(wgin, 16)

            @block.scalar
            def _(act):
                act.wait_ge(rready, 1)
                act.activation(root[:, :], var[:, :], ACT.Sqrt).then_inc(rdone, 1)
                for b in range(NB):
                    act.wait_ge(tp, b + 1)
                    act.copy(k["xt_all"][:, :, b * P:(b + 1) * P], t_ps[:, b % 2, :].rearrange("p (c n) -> p c n", c=CH)).then_inc(xt_ready, 1)
                act.wait_ge(lgr, 1)
                act.activation(lg[:, :, :], lg[:, :, :], ACT.Exp).then_inc(exped, 1)

            @block.tensor
            def _(pe):
                pe.wait_ge(wgin, 16)
                for b in range(NB + 1):
                    if b < NB:
                        pe.wait_ge(xn_ready, b + 1)
                        if b >= 2:
                            pe.wait_ge(xt_ready, b - 1)
                        for c in range(CH):
                            last = pe.transpose(t_ps[:, b % 2, c * P:(c + 1) * P], xn[:, b % 2, c * P:(c + 1) * P], k["ident"][:, :])
                        last.then_inc(tp, 1)
                    if b >= 1:
                        pe.wait_ge(xt_ready, b)
                        for c in range(CH):
                            last = pe.matmul(g_ps[:, b - 1, :], k["xt_all"][:, c, (b - 1) * P:b * P], wg_sb[:, c, :],
                                             start=(c == 0), stop=(c == CH - 1))
                last.then_inc(gated, 1)

            @block.vector
            def _(dve):
                link = chained(dve, chain)
                for b in range(NB):
                    dve.bn_stats(st[:, b, :], x_sb[:, b, :]).then_inc(stats, 1)
                dve.wait_ge(stats, NB)
                for b in range(NB):
                    dve.bn_aggr(mv[:, b, :], st[:, b, :]).then_inc(stats, 1)
                dve.wait_ge(stats, 2 * NB)
                normalise_stats(dve, rready, rdone, link, mv, var[:, :], root[:, :], rstd[:, :])
                for b in range(NB):
                    if b >= 2:
                        dve.wait_ge(tp, b - 1)
                    dve.tensor_scalar(xn[:, b % 2, :], x_sb[:, b, :], mv[:, b, 0:1], rstd[:, b:b + 1],
                                      ALU.subtract, ALU.mult).then_inc(xn_ready, 1)
                dve.wait_ge(gated, 1)
                ex3 = lambda v: bcast(v[:, :], 2, EXPERTS)
                link(dve.tensor_scalar(rankw[:, :], k["iota"][:, 0:EXPERTS], -1.0, float(EXPERTS), ALU.mult, ALU.add))
                link(dve.tensor_copy(g[:, :, :], g_ps[:, :, :]))
                link(dve.tensor_reduce(v1[:, :], g[:, :, :], AX_X, ALU.max))
                dve.tensor_tensor(lg[:, :, :], g[:, :, :], ex3(v1), ALU.subtract).then_inc(lgr, 1)
                dve.wait_ge(exped, 1)
                link(dve.tensor_reduce(v1[:, :], lg[:, :, :], AX_X, ALU.add))
                link(dve.reciprocal(v1[:, :], v1[:, :]))
                link(dve.tensor_tensor(g[:, :, :], lg[:, :, :], ex3(v1), ALU.mult))

                def pick(src, mask, best):
                    link(dve.tensor_reduce(best[:, :], src[:, :, :], AX_X, ALU.max))
                    link(dve.tensor_tensor(mask[:, :, :], src[:, :, :], ex3(best), ALU.is_equal))
                    link(dve.tensor_tensor(mask[:, :, :], mask[:, :, :], bcast(rankw[:, :], 1, NB), ALU.mult))
                    link(dve.tensor_reduce(v3[:, :], mask[:, :, :], AX_X, ALU.max))
                    link(dve.tensor_tensor(mask[:, :, :], mask[:, :, :], ex3(v3), ALU.is_equal))

                pick(g, m1, v1)
                link(dve.scalar_tensor_tensor(tmp[:, :, :], m1[:, :, :], -2.0, g[:, :, :], ALU.mult, ALU.add))
                pick(tmp, m2, v2)
                link(dve.tensor_tensor(v1[:, :], v1[:, :], v2[:, :], ALU.add))
                link(dve.tensor_scalar(v1[:, :], v1[:, :], 1e-6, None, ALU.add))
                link(dve.reciprocal(v1[:, :], v1[:, :]))
                link(dve.tensor_tensor(m1[:, :, :], m1[:, :, :], m2[:, :, :], ALU.add))
                link(dve.tensor_tensor(m1[:, :, :], m1[:, :, :], g[:, :, :], ALU.mult))
                link(dve.tensor_tensor(k["score_b"][:, :, :], m1[:, :, :], ex3(v1), ALU.mult))
                link(dve.tensor_copy(k["score_e"][:, :, :].rearrange("p e b -> p b e"), k["score_b"][:, :, :]))


def experts(nc, k, sem, w1, b1, w2, b2, out):
    x_sb, xt = k["x_sb"], k["xt_all"]
    PER = 2 * NG
    with ExitStack() as ctx:
        s = Space(nc, ctx)
        w1_sb = s.sb("w1_sb", [P, 2, CH, HID])
        w2_sb = s.sb("w2_sb", [P, 2, HCH, F])
        b1_row = s.sb("b1_row", [EXPERTS * HCH, P])
        b1_col = s.sb("b1_col", [P, EXPERTS, HCH])
        b2_sb = s.sb("b2_sb", [EXPERTS, F])
        sc_t = s.sb("sc_t", [EXPERTS, 2, P])
        hid = s.sb("hid", [P, 2, HCH, 512])
        h_ps = s.ps("h_ps", [P, 4, 512])
        y_ps = s.ps("y_ps", [P, 4, 512])

        small, win = sem("biases_in"), [sem(f"expert_in{j}") for j in range(2)]
        bt, bready, st, sready, badd = sem("b1_turned"), sem("b1_ready"), sem("score_turned"), sem("score_t_ready"), sem("b2_added")
        b2s = sem("b2_summed")
        hdone, hready, ydone, added, stored = sem("hidden"), sem("hidden_ready"), sem("y_done"), sem("y_added"), sem("stored")

        with nc.Block() as block:
            @block.sync
            def _(sp):
                sp.dma_start(b1_row[:, :], b1.rearrange("e (c p) -> (e c) p", p=P)).then_inc(small, 16)
                sp.dma_start(b2_sb[:, :], b2).then_inc(small, 16)

                def load(e, j):
                    sp.dma_start(w1_sb[:, j, :, :], w1[bass.ds(e, 1), :, :].rearrange("a (c p) h -> p (a c) h", p=P)).then_inc(win[j], 16)
                    sp.dma_start(w2_sb[:, j, :, :], w2[bass.ds(e, 1), :, :].rearrange("a (c p) f -> p (a c) f", p=P)).then_inc(win[j], 16)

                load(0, 0)
                load(1, 1)
                with sp.Fori(1, EXPERTS // 2) as i:
                    for j in range(2):
                        sp.wait_ge(ydone, 4 * (PER * i - PER + NG * (j + 1)))
                        load(2 * i + j, j)
                sp.wait_ge(added, 4 * NG * EXPERTS)
                sp.dma_start(out[0:(NB - 1) * P, :].rearrange("(b p) f -> p b f", p=P), x_sb[:, 0:NB - 1, :]).then_inc(stored, 16)
                sp.dma_start(out[(NB - 1) * P:N, :], x_sb[0:TAIL, NB - 1, :]).then_inc(stored, 16)
                sp.wait_ge(stored, 32)

            @block.tensor
            def _(pe):
                pe.wait_ge(small, 32)
                pe.transpose(h_ps[:, 0, 0:EXPERTS * HCH], b1_row[:, :], k["ident"][0:EXPERTS * HCH, 0:EXPERTS * HCH]).then_inc(bt, 1)
                for b in range(NB + 1):
                    if b < NB:
                        if b >= 2:
                            pe.wait_ge(sready, b - 1)
                        pe.transpose(h_ps[0:EXPERTS, 2 + b % 2, 0:P], k["score_b"][:, b, :], k["ident"][:, :]).then_inc(st, 1)
                    if b >= 1:
                        pe.wait_ge(sready, b)
                        if b >= 3:
                            pe.wait_ge(badd, b - 2)
                        pe.matmul(y_ps[:, (b - 1) % 2, :], sc_t[:, (b - 1) % 2, :], b2_sb[:, :], start=True, stop=True).then_inc(b2s, 1)
                pe.wait_ge(badd, NB)
                pe.wait_ge(bready, 1)

                def up(tg, je, j):
                    for hb in range(HCH):
                        for c in range(CH):
                            last = pe.matmul(h_ps[:, 2 * j + hb, :], w1_sb[:, je, c, hb * P:(hb + 1) * P],
                                             xt[:, c, tg * 512:(tg + 1) * 512], start=(c == 0), stop=(c == CH - 1))
                        last.then_inc(hdone, 1)

                def down(n, je, j):
                    pe.wait_ge(hready, 2 * n + 2)
                    for t in range(4):
                        if not (isinstance(n, int) and n == 0):
                            pe.wait_ge(added, 4 * n - 3 + t)
                        for hb in range(HCH):
                            last = pe.matmul(y_ps[:, t, :], hid[:, j, hb, t * P:(t + 1) * P], w2_sb[:, je, hb, :],
                                             start=(hb == 0), stop=(hb == HCH - 1))
                        last.then_inc(ydone, 1)

                pe.wait_ge(win[0], 32)
                up(0, 0, 0)
                for m in range(PER - 1):
                    if m + 1 == NG:
                        pe.wait_ge(win[1], 32)
                    if m >= 1:
                        pe.wait_ge(hready, 2 * m)
                    up((m + 1) % NG, (m + 1) // NG, (m + 1) % 2)
                    down(m, m // NG, m % 2)
                with pe.Fori(1, EXPERTS // 2) as i:
                    for m in range(-1, PER - 1):
                        n = PER * i + m
                        if m + 1 == 0:
                            pe.wait_ge(win[0], 32 * i + 32)
                        if m + 1 == NG:
                            pe.wait_ge(win[1], 32 * i + 32)
                        pe.wait_ge(hready, 2 * n)
                        up((m + 1) % NG, (m + 1) // NG, (m + 1) % 2)
                        down(n, (m // NG) % 2, m % 2)
                down(PER * EXPERTS // 2 - 1, 1, 1)

            @block.scalar
            def _(act):
                act.wait_ge(bt, 1)
                act.copy(b1_col[:, :, :].rearrange("p e c -> p (e c)"), h_ps[:, 0, 0:EXPERTS * HCH]).then_inc(bready, 1)
                for b in range(NB):
                    act.wait_ge(st, b + 1)
                    if b >= 2:
                        act.wait_ge(b2s, b - 1)
                    act.copy(sc_t[:, b % 2, :], h_ps[0:EXPERTS, 2 + b % 2, 0:P]).then_inc(sready, 1)
                act.wait_ge(bready, 1)

                def gelu(n, e, j, first):
                    for hb in range(HCH):
                        act.wait_ge(hdone, 2 * n + hb + 1)
                        if hb == 0 and not first:
                            act.wait_ge(ydone, 4 * n - 4)
                        act.nop(nofuse=True)
                        act.activation(hid[:, j, hb, :], h_ps[:, 2 * j + hb, :], ACT.Gelu,
                                       bias=b1_col[:, bass.ds(e, 1), hb]).then_inc(hready, 1)

                for m in range(PER):
                    gelu(m, m // NG, m % 2, m < 2)
                with act.Fori(1, EXPERTS // 2) as i:
                    for m in range(PER):
                        gelu(PER * i + m, 2 * i + m // NG, m % 2, False)

            @block.vector
            def _(dve):
                for b in range(NB):
                    dve.wait_ge(b2s, b + 1)
                    dve.tensor_tensor(x_sb[:, b, :], y_ps[:, b % 2, :], x_sb[:, b, :], ALU.add).then_inc(badd, 1)
                dve.wait_ge(badd, NB)

                def add(n, e, tg):
                    for t in range(4):
                        b = 4 * tg + t
                        dve.wait_ge(ydone, 4 * n + t + 1)
                        dve.scalar_tensor_tensor(x_sb[:, b, :], y_ps[:, t, :], k["score_e"][:, bass.ds(e, 1), b],
                                                 x_sb[:, b, :], ALU.mult, ALU.add).then_inc(added, 1)

                for m in range(PER):
                    if m >= NG:
                        dve.wait_ge(added, 4 * (m - NG + 1))
                    add(m, m // NG, m % NG)
                with dve.Fori(1, EXPERTS // 2) as i:
                    for m in range(PER):
                        dve.wait_ge(added, 4 * (PER * i + m - NG + 1))
                        add(PER * i + m, 2 * i + m // NG, m % NG)


def kernel_body(nc, x, src, dst, we, wr, a, wg, w1, b1, w2, b2, out):
    dram = lambda name, shape, dt: nc.dram_tensor(name, shape, dt, kind="Internal").ap()
    sorted_d = dram("sorted_d", [CAP + DUMP, RW], U32)
    table_d = dram("table_d", [NB * P, TW], F32)
    he_d = dram("he_d", [NB * P, F], F32)
    with ExitStack() as ctx:
        s = Space(nc, ctx)
        sem = lambda name: ctx.enter_context(nc.semaphore(name))
        k = dict(
            iota_i=s.sb("iota_i", [P, P], I32), iota=s.sb("iota", [P, P]), ident=s.sb("ident", [P, P]),
            ident_bf=s.sb("ident_bf", [P, P], BF16), ones=s.sb("ones", [P, P]), before=s.sb("before", [P, P]),
            shift=s.sb("shift", [P, P]),
            first_tile=s.sb("first_tile", [P, NB]), x_sb=s.sb("x_sb", [P, NB, F]),
        )
        build_constants(nc, k, sem)
        with ExitStack() as scoring:
            e = Space(nc, scoring)
            k.update(
                ends=e.sb("edge_ends", [P, T, 2], U32),
                loc=e.sb("edge_loc", [P, T + GT]),
                oh_blk=e.sb("oh_blk", [P, T, NB], BF16),
                first=e.sb("first", [P, NB, T + 1]),
                same=e.sb("same", [P, NB, T + 1], BF16),
                dump=e.sb("dump", [P, T]),
            )
            project(nc, k, sem, x, src, dst, we, wr, a, table_d, he_d, sorted_d)
            score_edges(nc, k, sem, a, table_d, sorted_d)
        k["att"] = s.sb("att", [P, Q, HEADS])
        k["target"] = s.sb("target", [P, Q], U32)
        k["local"] = s.sb("local", [P, Q])
        k["tile_block"] = s.sb("tile_block", [P, Q], I32)
        edge_softmax(nc, k, sem, sorted_d)
        sum_messages(nc, k, sem, he_d)
        k["xt_all"] = s.sb("xt_all", [P, CH, NB * P])
        k["score_b"] = s.sb("score_b", [P, NB, EXPERTS])
        k["score_e"] = s.sb("score_e", [P, EXPERTS, NB])
        route(nc, k, sem, wg)
        experts(nc, k, sem, w1, b1, w2, b2, out)


_INS = ['x', 'src', 'dst', 'L0_gnn_W_e', 'L0_gnn_W_r', 'L0_gnn_a', 'L0_ffn_Wg', 'L0_ffn_W1', 'L0_ffn_b1', 'L0_ffn_W2', 'L0_ffn_b2']
_OUTS = [((N, F), 'float32')]


def kernel(**inputs):
    import numpy as _np
    import concourse.bacc as _bacc
    from concourse import mybir as _mybir
    from concourse.bass_utils import run_bass_kernel_spmd as _run

    nc = _bacc.Bacc("TRN2", target_bir_lowering=False, num_devices=1)
    arrays, args = {}, []
    for name in _INS:
        a = _np.ascontiguousarray(inputs[name])
        arrays[f"in_{name}_dram"] = a
        args.append(nc.dram_tensor(f"in_{name}_dram", a.shape, _mybir.dt.from_np(a.dtype), kind="ExternalInput").ap())
    for i, (shape, dtype) in enumerate(_OUTS):
        dt = _mybir.dt.from_np(_np.dtype(dtype))
        args.append(nc.dram_tensor(f"out_{i}_dram", shape, dt, kind="ExternalOutput").ap())
    kernel_body(nc, *args)
    r = _run(nc, [arrays], core_ids=[0])
    got = tuple(r.results[0][f"out_{i}_dram"] for i in range(len(_OUTS)))
    return got[0]
```

```python
from contextlib import ExitStack

import concourse.bass as bass
from concourse import mybir

F32 = mybir.dt.float32
BF16 = mybir.dt.bfloat16
I32 = mybir.dt.int32
U32 = mybir.dt.uint32
ALU = mybir.AluOpType
ACT = mybir.ActivationFunctionType
AX_X = mybir.AxisListType.X

P = 128
N = 2500
F = 512
NB = -(-N // P)
TAIL = N - (NB - 1) * P
HEADS = 8
D = F // HEADS
CH = F // P
E = 40000
EP = 125
T = E // EP
GT = 4
GROUPS = T // GT
Q = 336
STRIPS = P // HEADS
SQ = Q // STRIPS
CAP = Q * P
DUMP = (P - EP) * T
RW = 12
TW = F + 2 * HEADS
CPB = 16
SLOPE = 0.2
EPS = 1e-5
BIG = 1.0e30
EXPERTS = 8
HID = 256
HCH = HID // P
NT = (2 * N + EXPERTS * (P - 1)) // P
assert Q * P >= E + NB * (P - 1) and EP * T == E and Q * (NB - 1) <= NB * (T + 1) and GROUPS * GT == T


def bcast(ap, axis, n):
    ap = ap.unsqueeze(axis)
    shape = list(ap.shape)
    shape[axis] = n
    return ap.to_broadcast(shape)


class Space:

    def __init__(self, nc, ctx):
        self.nc, self.ctx = nc, ctx

    def sb(self, name, shape, dt=F32):
        return self.ctx.enter_context(self.nc.sbuf_tensor(name, shape, dt))

    def ps(self, name, shape, dt=F32):
        return self.ctx.enter_context(self.nc.psum_tensor(name, shape, dt))


class Chain:

    def __init__(self, sem):
        self.sem, self.count = sem, 0

    def on(self, eng):
        def link(ins):
            self.mark(ins)
            eng.wait_ge(self.sem, self.count)

        return link

    def mark(self, ins):
        self.count += 1
        ins.then_inc(self.sem, 1)


def build_constants(nc, k, sem):
    made = sem("constants_made")
    with nc.sbuf_tensor("number_i", [P, Q], I32) as number_i, nc.Block() as block:
        @block.gpsimd
        def _(pool):
            link = Chain(made).on(pool)
            link(pool.iota(number_i[:, :], pattern=[[1, Q]], base=0, channel_multiplier=0))
            link(pool.tensor_copy(k["iota"][:, :], number_i[:, 0:P]))
            link(pool.tensor_copy(k["tile_block"][:, :], number_i[:, :]))
            link(pool.memset(k["ident"][:, :], 0.0))
            link(pool.affine_select(out=k["ident"][:, :], in_=k["ident"][:, :], compare_op=ALU.not_equal,
                                    fill=1.0, base=0, pattern=[[-1, P]], channel_multiplier=1))
            link(pool.tensor_copy(k["ident_bf"][:, :], k["ident"][:, :]))
            link(pool.memset(k["ones"][:, :], 1.0))
            link(pool.affine_select(out=k["before"][:, :], in_=k["ones"][:, :], compare_op=ALU.is_gt,
                                    fill=0.0, base=0, pattern=[[1, P]], channel_multiplier=-1))
            link(pool.memset(k["shift"][:, :], 0.0))
            link(pool.affine_select(out=k["shift"][:, :], in_=k["shift"][:, :], compare_op=ALU.not_equal,
                                    fill=1.0, base=HEADS, pattern=[[-1, P]], channel_multiplier=1))


def normalise_stats(dve, act_ready, act_done, link, mv, var, root, rstd):
    link(dve.tensor_scalar(var, mv[:, :, 1], EPS, None, ALU.add))
    dve.nop().then_inc(act_ready, 1)
    dve.wait_ge(act_done, 1)
    link(dve.reciprocal(rstd, root))
    link(dve.tensor_tensor(rstd, rstd, var, ALU.mult))
    link(dve.tensor_tensor(root, rstd, root, ALU.add))
    link(dve.tensor_scalar(root, root, 0.5, None, ALU.mult))
    link(dve.reciprocal(rstd, root))


def project(nc, k, sem, x, src, dst, we, wr, a, table_d, he_d, sorted_d):
    x_sb = k["x_sb"]
    with ExitStack() as ctx:
        s = Space(nc, ctx)
        w_e = s.sb("w_e", [P, CH, F])
        w_r = s.sb("w_r", [P, CH, F])
        a_all = s.sb("a_all", [P, HEADS, 5 * D])
        half = s.sb("half", [P, HEADS, D])
        prod = s.sb("prod", [P, CH, HEADS, D])
        lin = s.sb("lin", [P, CH, 2 * HEADS])
        dif = s.sb("dif", [P, CH, HEADS])
        st = s.sb("st", [P, NB, 6])
        mv = s.sb("mv", [P, NB, 2])
        var = s.sb("var", [P, NB])
        root = s.sb("root", [P, NB])
        rstd = s.sb("rstd", [P, NB])
        xn = s.sb("xn", [P, 2, F])
        xt = s.sb("xt", [P, 2, CH, P])
        row = s.sb("row", [P, 2, TW])
        he = s.sb("he", [P, 2, F])
        sq = s.sb("sq", [P, 2, HEADS, D])
        sqa = s.sb("sqa", [P, 2, HEADS, D])
        own = s.sb("own", [P, 2, HEADS])
        src_i = s.sb("src_i", [P, T], I32)
        dst_i = s.sb("dst_i", [P, T], I32)
        blk_i = s.sb("blk_i", [P, T], I32)
        blk = s.sb("blk", [P, T])
        dump_i = s.sb("dump_i", [P, T], I32)
        hot = s.sb("hot_loc", [P, 2, CPB, P], BF16)
        fill = s.sb("fill", [P, 21, RW], U32)
        loc, oh_blk, first = k["loc"], k["oh_blk"], k["first"]
        t_ps = s.ps("t_ps", [P, 2, F])
        r_ps = s.ps("r_ps", [P, 2, F])
        e_ps = s.ps("e_ps", [P, 2, F])
        lc_ps = s.ps("lc_ps", [P, 2, 512])
        l_ps = lc_ps[:, :, 0:2 * HEADS]
        counts_ps = lc_ps[:, :, 2 * HEADS:2 * HEADS + CPB * NB]

        xin = [sem(f"x_in{c}") for c in range(5)]
        win, ain = sem("weights_in"), sem("a_in")
        stats, rready, rdone = sem("stats"), sem("var_ready"), sem("root_done")
        linr, xn_ready, tp, xt_ready, proj = sem("lin_ready"), sem("xn_ready"), sem("x_turned"), sem("xt_ready"), sem("projected")
        he_ready, sq_ready, row_ready, sqa_ready = sem("he_ready"), sem("sq_ready"), sem("row_ready"), sem("sqa_ready")
        hr_copied, own_ready, pq = sem("hr_copied"), sem("own_ready"), sem("pq_ready")
        row_out = [sem(f"row_out{j}") for j in range(2)]
        he_out = [sem(f"he_out{j}") for j in range(2)]
        loaded, cleared, edge_ids = sem("edges_loaded"), sem("edges_cleared"), sem("edge_ids")
        valid, hots, counted, kept = sem("edges_valid"), sem("one_hots"), sem("tiles_counted"), sem("counts_kept")
        blk_hot = sem("block_one_hot")
        dumped, filled, fill_out, pool_chain = sem("dump_ready"), sem("fill_ready"), sem("fill_out"), sem("count_pool_chain")

        with nc.Block() as block:
            @block.sync
            def _(sp):
                sp.wait_ge(cleared, 2)
                sp.dma_start(src_i[0:EP, :], src.rearrange("(p t) -> p t", t=T)).then_inc(loaded, 16)
                sp.dma_start(dst_i[0:EP, :], dst.rearrange("(p t) -> p t", t=T)).then_inc(loaded, 16)
                for c in range(4):
                    sp.dma_start(x_sb[:, 4 * c:4 * c + 4, :],
                                 x[512 * c:512 * (c + 1), :].rearrange("(b p) f -> p b f", p=P)).then_inc(xin[c], 16)
                sp.dma_start(x_sb[:, 16:NB - 1, :],
                             x[2048:(NB - 1) * P, :].rearrange("(b p) f -> p b f", p=P)).then_inc(xin[4], 16)
                sp.wait_ge(cleared, 3)
                sp.dma_start(x_sb[0:TAIL, NB - 1, :], x[(NB - 1) * P:N, :]).then_inc(xin[4], 16)
                sp.wait_ge(filled, 3)
                rows = sorted_d[0:CAP, :].rearrange("(p g t) w -> p g t w", p=P, t=21)
                for g in range(Q // 21):
                    sp.dma_start(rows[:, g, :, :], fill[:, :, :]).then_inc(fill_out, 16)

                def store(b, j):
                    sp.wait_ge(row_ready, b + 1)
                    sp.dma_start(table_d[bass.ds(b * P, P), :], row[:, j, :]).then_inc(row_out[j], 16)
                    sp.wait_ge(he_ready, b + 1)
                    sp.dma_start(he_d[bass.ds(b * P, P), :], he[:, j, :]).then_inc(he_out[j], 16)

                with sp.Fori(0, NB // 2) as i:
                    for j in range(2):
                        store(2 * i + j, j)
                for j in range(2):
                    sp.wait_ge(row_out[j], 16 * NB // 2)
                    sp.wait_ge(he_out[j], 16 * NB // 2)
                sp.wait_ge(fill_out, 16 * (Q // 21))

            @block.gpsimd
            def _(pool):
                pool.memset(fill[:, :, :], 0).then_inc(filled, 1)
                pool.wait_ge(filled, 1)
                pool.memset(fill[:, :, HEADS:HEADS + 1], 4095).then_inc(filled, 2)
                pool.iota(dump_i[:, :], pattern=[[1, T]], base=CAP - EP * T, channel_multiplier=T).then_inc(pool_chain, 1)
                pool.wait_ge(pool_chain, 1)
                pool.tensor_copy(k["dump"][:, :], dump_i[:, :]).then_inc(pool_chain, 1)
                pool.wait_ge(pool_chain, 2)
                pool.affine_select(out=k["dump"][:, :], in_=k["dump"][:, :], compare_op=ALU.is_ge, fill=0.0,
                                   base=-EP, pattern=[[0, T]], channel_multiplier=1).then_inc(dumped, 1)
                pool.wait_ge(edge_ids, 4)
                pool.affine_select(out=blk[:, :], in_=blk[:, :], compare_op=ALU.is_ge, fill=-1.0,
                                   base=EP - 1, pattern=[[0, T]], channel_multiplier=-1).then_inc(valid, 1)
                pool.affine_select(out=loc[:, 0:T], in_=loc[:, 0:T], compare_op=ALU.is_ge, fill=-1.0,
                                   base=EP - 1, pattern=[[0, T]], channel_multiplier=-1).then_inc(valid, 1)
                pool.memset(k["same"][:, :, :], 1.0).then_inc(pool_chain, 1)
                pool.wait_ge(pool_chain, 3)
                pool.memset(k["same"][:, :, 0:1], 0.0).then_inc(pool_chain, 1)

            @block.scalar
            def _(act):
                act.dma_start(a_all[:, :, :], a.partition_broadcast(P)).then_inc(ain, 16)
                for c in range(CH):
                    act.dma_start(w_e[:, c, :].rearrange("p (h d) -> p h d", h=HEADS),
                                  we[:, c * P:(c + 1) * P, :].rearrange("h p d -> p h d")).then_inc(win, 16)
                    act.dma_start(w_r[:, c, :].rearrange("p (h d) -> p h d", h=HEADS),
                                  wr[:, c * P:(c + 1) * P, :].rearrange("h p d -> p h d")).then_inc(win, 16)
                act.wait_ge(rready, 1)
                act.activation(root[:, :], var[:, :], ACT.Sqrt).then_inc(rdone, 1)

                def turned(b, j):
                    act.wait_ge(tp, b + 1)
                    act.copy(xt[:, j, :, :], t_ps[:, j, :].rearrange("p (c n) -> p c n", c=CH)).then_inc(xt_ready, 1)

                def keep(b, j):
                    act.wait_ge(proj, b + 1)
                    act.activation(sq[:, j, :, :].rearrange("p h d -> p (h d)"), r_ps[:, j, :], ACT.Square).then_inc(sq_ready, 1)
                    act.copy(he[:, j, :], e_ps[:, j, :]).then_inc(he_ready, 1)

                def keep_counts(c, j):
                    act.wait_ge(counted, c + 1)
                    act.copy(first[:, :, bass.ds(c * CPB + 1, CPB)].rearrange("p b t -> p t b"),
                             counts_ps[:, j, :].rearrange("p (t b) -> p t b", b=NB)).then_inc(kept, 1)

                turned(0, 0)
                turned(1, 1)
                keep_counts(0, 0)
                keep(0, 0)

                def pair(i):
                    for j in range(2):
                        b = 2 * i + j
                        act.wait_ge(proj, b - 1)
                        turned(b, j)
                        keep_counts(b - 1, 1 - j)
                        if not (isinstance(b, int) and b == 2):
                            act.wait_ge(he_out[1 - j], 16 * (i + j) - 16)
                            act.wait_ge(row_ready, b - 2)
                        keep(b - 1, 1 - j)

                pair(1)
                with act.Fori(2, NB // 2) as i:
                    pair(i)
                keep_counts(NB - 1, 1)
                act.wait_ge(he_out[1], 16 * (NB // 2 - 1))
                act.wait_ge(row_ready, NB - 2)
                keep(NB - 1, 1)

            @block.tensor
            def _(pe):
                def turn(b, j):
                    pe.wait_ge(xn_ready, b + 1)
                    for c in range(CH):
                        last = pe.transpose(t_ps[:, j, c * P:(c + 1) * P], xn[:, j, c * P:(c + 1) * P], k["ident"][:, :])
                    last.then_inc(tp, 1)

                def multiply(b, j):
                    pe.wait_ge(xt_ready, b + 1)
                    for out, w in ((r_ps[:, j, :], w_r), (e_ps[:, j, :], w_e), (l_ps[:, j, :], lin)):
                        if w is lin:
                            pe.wait_ge(kept, b + 1)
                        for c in range(CH):
                            last = pe.matmul(out, xt[:, j, c, :], w[:, c, :], start=(c == 0), stop=(c == CH - 1))
                    last.then_inc(proj, 1)

                def count(c, j):
                    pe.wait_ge(hots, c + 1)
                    for t in range(CPB):
                        last = pe.matmul(counts_ps[:, j, t * NB:(t + 1) * NB], hot[:, j, t, :],
                                         oh_blk[:, bass.ds(c * CPB + t, 1), :].rearrange("p a b -> p (a b)"),
                                         start=True, stop=True)
                    last.then_inc(counted, 1)

                turn(0, 0)
                turn(1, 1)
                pe.wait_ge(win, 32 * CH)
                pe.wait_ge(linr, 1)
                pe.wait_ge(blk_hot, 1)
                count(0, 0)
                multiply(0, 0)

                def pair(i):
                    for j in range(2):
                        b = 2 * i + j
                        pe.wait_ge(xt_ready, b - 1)
                        turn(b, j)
                        if not (isinstance(b, int) and b == 2):
                            pe.wait_ge(row_ready, b - 2)
                            pe.wait_ge(he_ready, b - 2)
                        count(b - 1, 1 - j)
                        multiply(b - 1, 1 - j)

                pair(1)
                with pe.Fori(2, NB // 2) as i:
                    pair(i)
                pe.wait_ge(row_ready, NB - 2)
                pe.wait_ge(he_ready, NB - 2)
                count(NB - 1, 1)
                multiply(NB - 1, 1)

            @block.vector
            def _(dve):
                link = k["dve_chain"].on(dve)
                dve.memset(src_i[:, :], 0).then_inc(cleared, 1)
                dve.memset(dst_i[:, :], 0).then_inc(cleared, 1)
                dve.memset(x_sb[:, NB - 1, :], 0.0).then_inc(cleared, 1)
                dve.wait_ge(loaded, 32)
                dve.tensor_scalar(blk_i[:, :], src_i[:, :], 7, None, ALU.logical_shift_right).then_inc(edge_ids, 1)
                k["dve_chain"].mark(dve.tensor_copy(k["ends"][:, :, 0], src_i[:, :]))
                k["dve_chain"].mark(dve.tensor_copy(k["ends"][:, :, 1], dst_i[:, :]))
                dve.wait_ge(edge_ids, 1)
                dve.tensor_copy(blk[:, :], blk_i[:, :]).then_inc(edge_ids, 1)
                dve.tensor_scalar(src_i[:, :], src_i[:, :], P - 1, None, ALU.bitwise_and).then_inc(edge_ids, 1)
                dve.wait_ge(edge_ids, 3)
                dve.tensor_copy(loc[:, 0:T], src_i[:, :]).then_inc(edge_ids, 1)
                dve.memset(loc[:, T:T + GT], -1.0)
                for b in range(NB):
                    if b % 4 == 0:
                        dve.wait_ge(xin[b // 4], 16 if b < 16 else 32)
                    dve.bn_stats(st[:, b, :], x_sb[:, b, :]).then_inc(stats, 1)
                dve.wait_ge(stats, NB)
                for b in range(NB):
                    dve.bn_aggr(mv[:, b, :], st[:, b, :]).then_inc(stats, 1)
                dve.wait_ge(stats, 2 * NB)
                normalise_stats(dve, rready, rdone, link, mv, var[:, :], root[:, :], rstd[:, :])

                def normalise(b, j):
                    dve.tensor_scalar(xn[:, j, :], x_sb[:, bass.ds(b, 1), :].rearrange("p a f -> p (a f)"),
                                      mv[:, bass.ds(b, 1), 0], rstd[:, bass.ds(b, 1)],
                                      ALU.subtract, ALU.mult).then_inc(xn_ready, 1)

                def finish(b, j):
                    dve.wait_ge(sq_ready, b + 1)
                    dve.tensor_copy(row[:, j, 0:F], r_ps[:, j, :]).then_inc(hr_copied, 1)
                    dve.tensor_tensor(sqa[:, j, :, :], sq[:, j, :, :], half[:, :, :], ALU.mult).then_inc(sqa_ready, 1)
                    dve.wait_ge(sqa_ready, b + 1)
                    dve.tensor_reduce(own[:, j, :], sqa[:, j, :, :], AX_X, ALU.add).then_inc(own_ready, 1)
                    dve.wait_ge(own_ready, b + 1)
                    dve.wait_ge(hr_copied, b + 1)
                    dve.tensor_tensor(row[:, j, F:TW].rearrange("p (a h) -> p a h", a=2),
                                      l_ps[:, j, :].rearrange("p (a h) -> p a h", a=2),
                                      bcast(own[:, j, :], 1, 2), ALU.add).then_inc(row_ready, 1)

                def one_hots(c, j):
                    dve.tensor_tensor(hot[:, j, :, :], bcast(loc[:, bass.ds(c * CPB, CPB)], 2, P),
                                      bcast(k["iota"][:, :], 1, CPB), ALU.is_equal).then_inc(hots, 1)

                normalise(0, 0)
                normalise(1, 1)
                dve.wait_ge(tp, 1)
                normalise(2, 0)
                dve.wait_ge(valid, 2)
                one_hots(0, 0)
                one_hots(1, 1)
                dve.tensor_tensor(oh_blk[:, :, :], bcast(blk[:, :], 2, NB), bcast(k["iota"][:, 0:NB], 1, T),
                                  ALU.is_equal).then_inc(blk_hot, 1)
                dve.wait_ge(win, 32 * CH)
                dve.wait_ge(ain, 16)
                w4e = w_e[:, :, :].rearrange("p c (h d) -> p c h d", h=HEADS)
                w4r = w_r[:, :, :].rearrange("p c (h d) -> p c h d", h=HEADS)
                for w, part, out in ((w4r, 2, dif[:, :, :]), (w4e, 0, lin[:, :, 0:HEADS]), (w4e, 1, lin[:, :, HEADS:])):
                    link(dve.tensor_tensor(prod[:, :, :, :], w, bcast(a_all[:, :, part * D:(part + 1) * D], 1, CH), ALU.mult))
                    link(dve.tensor_reduce(out, prod[:, :, :, :], AX_X, ALU.add))
                link(dve.tensor_scalar(half[:, :, :], a_all[:, :, 4 * D:], 0.5, None, ALU.mult))
                k["dve_chain"].mark(dve.tensor_tensor(lin[:, :, 0:HEADS], lin[:, :, 0:HEADS], dif[:, :, :], ALU.subtract))
                dve.tensor_tensor(lin[:, :, HEADS:], lin[:, :, HEADS:], dif[:, :, :], ALU.add).then_inc(linr, 1)
                finish(0, 0)

                def pair(i):
                    for j in range(2):
                        b = 2 * i + j
                        if not (isinstance(b, int) and b == NB - 1):
                            dve.wait_ge(tp, b)
                            normalise(b + 1, 1 - j)
                        dve.wait_ge(counted, b - 1)
                        one_hots(b, j)
                        if not (isinstance(b, int) and b == 2):
                            dve.wait_ge(row_out[1 - j], 16 * (i + j) - 16)
                        finish(b - 1, 1 - j)

                pair(1)
                with dve.Fori(2, NB // 2 - 1) as i:
                    pair(i)
                pair(NB // 2 - 1)
                dve.wait_ge(row_out[1], 16 * (NB // 2 - 1))
                finish(NB - 1, 1)


def score_edges(nc, k, sem, a, table_d, sorted_d):
    RING = 4
    first, oh_blk = k["first"], k["oh_blk"]
    with ExitStack() as ctx:
        s = Space(nc, ctx)
        ix = s.sb("ix", [P, RING * GT, 2], U32)
        rowix = s.sb("rowix", [P, RING, GT], U32)
        gs = s.sb("gs", [P, RING * GT, TW])
        gd = s.sb("gd", [P, RING * GT, TW])
        ab = s.sb("ab", [P, 2, CH, GT * P])
        uv = s.sb("uv", [P, 2, CH, GT * P])
        ssum = s.sb("ssum", [HEADS, GT * P])
        rowt = s.sb("rowt", [P, RING, GT, RW], U32)
        sc = s.sb("sc", [P, 2, GT, HEADS])
        raw = s.sb("raw_a", [P, 2, CH])
        heads = s.sb("heads", [P, CH, HEADS])
        total = s.sb("total", [P, NB])
        bi = s.sb("bi", [P, NB], I32)
        nt = s.sb("nt", [P, NB])
        ends = s.sb("ends", [P, NB])
        start = s.sb("start", [P, NB])
        hot = s.sb("hot_e", [P, 2, GT, P], BF16)
        hot_t = s.sb("hot_t", [P, GT, P])
        earlier = s.sb("earlier", [P, 2, GT, P], BF16)
        picked = s.sb("picked", [P, GT, NB])
        pos = s.sb("pos", [P, GT])
        posi = s.sb("posi", [P, 3, GT], I32)
        posf = s.sb("posf", [P, GT])
        d_ps = s.ps("d_ps", [P, 2, GT * P])
        s_ps = s.ps("s_ps", [P, 2, 512])
        back_ps = s.ps("back_ps", [P, GT, HEADS])
        tr_ps = s.ps("tr_ps", [P, GT, P], BF16)
        same_ps = s.ps("same_ps", [P, GT, P])
        look_ps = s.ps("look_ps", [P, GT, NB])

        ain, az, wready = sem("score_a_in"), sem("score_a_zero"), sem("score_weights")
        tot, totps, firsts = sem("totals"), sem("totals_ps"), sem("firsts_ready")
        ixr = sem("indices_ready")
        got = [sem(f"rows_in{j}") for j in range(RING)]
        out = [sem(f"scores_out{j}") for j in range(RING)]
        dready, dturned, abr, ur, vr, red = (sem("diff_ready"), sem("diff_turned"), sem("abs_ready"), sem("u_ready"),
                                             sem("v_ready"), sem("reduced"))
        ssr, back, s1, s2, scored, idr = (sem("sums_ready"), sem("sums_back"), sem("score_p"), sem("score_pq"),
                                          sem("scored"), sem("row_ids"))
        hotr, tr_done, htr, same_done, early_ready, look_done = (sem("rank_hot"), sem("rank_tr"), sem("rank_hot_t"),
                                                                 sem("rank_same"), sem("rank_early"), sem("rank_look"))
        pmul, pch, rowr = sem("rank_mul"), sem("rank_pos"), sem("rows_ready")

        with nc.Block() as block:
            @block.sync
            def _(sp):
                for half in range(2):
                    for n, part in enumerate((3, 4)):
                        sp.dma_start(raw[half * D:(half + 1) * D, n, :],
                                     a.rearrange("(c t) f -> f c t", t=2)[part * D:(part + 1) * D, :, half],
                                     allow_slow_non_contiguous=True).then_inc(ain, 16)

            @block.gpsimd
            def _(pool):
                def gather(g, r):
                    pool.tensor_copy(ix[:, r * GT:(r + 1) * GT, :], k["ends"][:, bass.ds(g * GT, GT), :]).then_inc(ixr, 1)
                    pool.wait_ge(ixr, g + 1)
                    pool.nop(nofuse=True)
                    for t in range(GT):
                        j = r * GT + t
                        pool.indirect_dma_start(gs[:, j, :], None, table_d,
                                                bass.IndirectOffsetOnAxis(ap=ix[:, j, 0:1], axis=0)).then_inc(got[r], 16)
                        pool.indirect_dma_start(gd[:, j, :], None, table_d,
                                                bass.IndirectOffsetOnAxis(ap=ix[:, j, 1:2], axis=0)).then_inc(got[r], 16)

                def scatter(g, r):
                    pool.wait_ge(scored, g + 1)
                    pool.nop(nofuse=True)
                    for t in range(GT):
                        pool.indirect_dma_start(sorted_d, bass.IndirectOffsetOnAxis(ap=rowix[:, r, t:t + 1], axis=0),
                                                rowt[:, r, t, :], None).then_inc(out[r], 16)

                LAG = RING - 1
                for g in range(RING):
                    gather(g, g)
                scatter(0, 0)
                with pool.Fori(1, GROUPS // RING) as i:
                    for r in range(RING):
                        gather(RING * i + r, r)
                        scatter(RING * i + r - LAG, (r - LAG) % RING)
                for g in range(GROUPS - LAG, GROUPS):
                    scatter(g, g % RING)
                for r in range(RING):
                    pool.wait_ge(out[r], 16 * GT * (GROUPS // RING))

            @block.vector
            def _(dve):
                link = k["dve_chain"].on(dve)
                dve.memset(heads[:, :, :], 0.0).then_inc(az, 1)
                dve.memset(rowt[:, :, :, :], 0).then_inc(az, 1)
                dve.tensor_reduce(total[:, :], first[:, :, 1:T + 1], AX_X, ALU.add).then_inc(tot, 1)
                dve.wait_ge(az, 2)
                dve.wait_ge(ain, 64)
                for c in range(CH):
                    for half in range(2):
                        h = 2 * c + half
                        dve.memset(heads[half * D:(half + 1) * D, c, h:h + 1], 1.0).then_inc(wready, 1)
                dve.tensor_scalar(raw[:, 1, :], raw[:, 1, :], -0.5, None, ALU.mult).then_inc(wready, 1)
                dve.wait_ge(totps, 1)
                link(dve.tensor_scalar(bi[:, :], s_ps[:, 1, 0:NB], float(P - 1), None, ALU.add))
                link(dve.tensor_scalar(bi[:, :], bi[:, :], 7, None, ALU.logical_shift_right))
                link(dve.tensor_copy(nt[:, :], bi[:, :]))
                link(dve.tensor_tensor_scan(ends[:, :], k["ones"][:, 0:NB], nt[:, :], 0.0, ALU.mult, ALU.add))
                link(dve.tensor_tensor(start[:, :], ends[:, :], nt[:, :], ALU.subtract))
                link(dve.tensor_copy(k["first_tile"][:, :], start[:, :]))
                link(dve.scalar_tensor_tensor(first[:, :, 0], start[:, :], float(P), s_ps[:, 0, 0:NB],
                                              ALU.mult, ALU.add))
                flat = first[:, :, :].rearrange("p b t -> p (b t)")
                dve.tensor_tensor_scan(flat, k["same"][:, :, :].rearrange("p b t -> p (b t)"), flat, 0.0,
                                       ALU.mult, ALU.add).then_inc(firsts, 1)

                def tile_blocks():
                    dve.wait_ge(firsts, 1)
                    cmp = k["same"][:, :, :].rearrange("p b t -> p (b t)")[:, 0:Q * (NB - 1)].rearrange("p (q b) -> p q b", q=Q)
                    link(dve.tensor_tensor(cmp, bcast(k["tile_block"][:, :], 2, NB - 1),
                                           bcast(k["first_tile"][:, 1:NB], 1, Q), ALU.is_ge))
                    link(dve.tensor_reduce(k["tile_block"][:, :], cmp, AX_X, ALU.add))

                def one_hot(g, j):
                    dve.tensor_tensor(hot[:, j, :, :], bcast(k["loc"][:, bass.ds(g * GT, GT)], 2, P),
                                      bcast(k["iota"][:, :], 1, GT), ALU.is_equal).then_inc(hotr, 1)

                def subtract(g, r, i):
                    dve.wait_ge(got[r], 32 * GT * (i + 1))
                    for t in range(GT):
                        j = r * GT + t
                        last = dve.tensor_tensor(gs[:, j, 0:F], gd[:, j, 0:F], gs[:, j, 0:F], ALU.subtract)
                    last.then_inc(dready, 1)

                def mark_earlier(g, j):
                    dve.wait_ge(same_done, g + 1)
                    dve.tensor_tensor(earlier[:, j, :, :], same_ps[:, :, :], bcast(k["before"][:, :], 1, GT),
                                      ALU.mult).then_inc(early_ready, 1)

                def combine(g, j):
                    for c in range(CH):
                        dve.wait_ge(ur, CH * g + c + 1)
                        dve.tensor_tensor(uv[:, j, c, :], uv[:, j, c, :], ab[:, j, c, :], ALU.mult).then_inc(vr, 1)

                def place(g, r):
                    dve.wait_ge(look_done, g + 1)
                    dve.tensor_tensor(picked[:, :, :], look_ps[:, :, :], oh_blk[:, bass.ds(g * GT, GT), :],
                                      ALU.mult).then_inc(pmul, 1)
                    dve.wait_ge(pmul, g + 1)
                    dve.tensor_reduce(pos[:, :], picked[:, :, :], AX_X, ALU.add).then_inc(pch, 1)
                    dve.wait_ge(pch, 5 * g + 1)
                    dve.tensor_copy(posi[:, 0, :], pos[:, :]).then_inc(pch, 1)
                    dve.wait_ge(pch, 5 * g + 2)
                    dve.tensor_scalar(posi[:, 1, :], posi[:, 0, :], P - 1, None, ALU.bitwise_and).then_inc(pch, 1)
                    dve.tensor_scalar(posi[:, 2, :], posi[:, 0, :], 7, None, ALU.logical_shift_right).then_inc(pch, 1)
                    dve.wait_ge(pch, 5 * g + 4)
                    dve.scalar_tensor_tensor(posf[:, :], posi[:, 1, :], float(Q), posi[:, 2, :],
                                             ALU.mult, ALU.add).then_inc(pch, 1)
                    dve.wait_ge(pch, 5 * g + 5)
                    dve.tensor_tensor(rowix[:, r, :], posf[:, :], k["dump"][:, bass.ds(g * GT, GT)], ALU.add).then_inc(rowr, 1)

                def keep_sums(g, j):
                    dve.wait_ge(red, g + 1)
                    dve.tensor_copy(ssum[:, :], s_ps[0:HEADS, j, :]).then_inc(ssr, 1)

                def score(g, j, r):
                    rows = slice(r * GT, (r + 1) * GT)
                    dve.wait_ge(back, g + 1)
                    dve.tensor_tensor(sc[:, j, :, :], back_ps[:, :, :], gs[:, rows, F:F + HEADS], ALU.add).then_inc(s1, 1)
                    dve.tensor_copy(rowt[:, r, :, HEADS:HEADS + 2], k["ends"][:, bass.ds(g * GT, GT), :]).then_inc(idr, 1)
                    dve.wait_ge(s1, g + 1)
                    dve.tensor_tensor(sc[:, j, :, :], sc[:, j, :, :], gd[:, rows, F + HEADS:TW], ALU.add).then_inc(s2, 1)
                    dve.wait_ge(s2, g + 1)
                    dve.wait_ge(idr, g + 1)
                    dve.wait_ge(rowr, g + 1)
                    dve.scalar_tensor_tensor(rowt[:, r, :, 0:HEADS].bitcast(F32), sc[:, j, :, :], SLOPE, sc[:, j, :, :],
                                             ALU.mult, ALU.max).then_inc(scored, 1)

                def step(g, r, i):
                    j = r % 2
                    known = isinstance(g, int)
                    inside = not (known and g >= GROUPS)
                    if inside:
                        one_hot(g + 1, 1 - j)
                    if not (known and g == 0):
                        combine(g - 1, 1 - j)
                    if inside:
                        subtract(g, r, i)
                        mark_earlier(g, j)
                    if not (known and g == 0):
                        keep_sums(g - 1, 1 - j)
                        rp = (r - 1) % RING
                        if not (known and g - 1 < RING):
                            dve.wait_ge(out[rp], 16 * GT * (i if r >= 1 else i - 1))
                        place(g - 1, rp)
                        score(g - 1, 1 - j, rp)

                one_hot(0, 0)
                tile_blocks()
                for g in range(RING + 1):
                    step(g, g % RING, g // RING)
                for g in range(RING + 1, 2 * RING):
                    step(g, g % RING, 1)
                with dve.Fori(2, GROUPS // RING) as i:
                    for r in range(RING):
                        step(RING * i + r, r, i)
                step(GROUPS, 0, GROUPS // RING)

            @block.tensor
            def _(pe):
                pe.wait_ge(tot, 1)
                pe.matmul(s_ps[:, 0, 0:NB], k["before"][:, :], total[:, :], start=True, stop=True)
                pe.matmul(s_ps[:, 1, 0:NB], k["ones"][:, :], total[:, :], start=True, stop=True).then_inc(totps, 1)
                pe.wait_ge(wready, 2 * CH + 1)
                pe.wait_ge(firsts, 1)

                def turn_hot(g, j):
                    pe.wait_ge(hotr, g + 1)
                    for t in range(GT):
                        last = pe.transpose(tr_ps[:, t, :], hot[:, j, t, :], k["ident_bf"][:, :])
                    last.then_inc(tr_done, 1)

                def compare(g):
                    pe.wait_ge(htr, g + 1)
                    for t in range(GT):
                        last = pe.matmul(same_ps[:, t, :], hot_t[:, t, :], hot_t[:, t, :], start=True, stop=True)
                    last.then_inc(same_done, 1)

                def look(g, j):
                    pe.wait_ge(early_ready, g + 1)
                    if not (isinstance(g, int) and g == 0):
                        pe.wait_ge(pmul, g)
                    for t in range(GT):
                        pe.matmul(look_ps[:, t, :], earlier[:, j, t, :],
                                  oh_blk[:, bass.ds(g * GT + t, 1), :].rearrange("p a b -> p (a b)"),
                                  start=True, stop=False)
                        last = pe.matmul(look_ps[:, t, :], hot_t[:, t, :],
                                         first[:, :, bass.ds(g * GT + t, 1)].rearrange("p b a -> p (b a)"),
                                         start=False, stop=True)
                    last.then_inc(look_done, 1)

                def turn(g, r, c):
                    if c == 0:
                        pe.wait_ge(dready, g + 1)
                    if not (isinstance(g, int) and g == 0 and c < 2):
                        pe.wait_ge(abr, CH * g + c - 1)
                    for t in range(GT):
                        last = pe.transpose(d_ps[:, c % 2, t * P:(t + 1) * P], gs[:, r * GT + t, c * P:(c + 1) * P],
                                            k["ident"][:, :])
                    last.then_inc(dturned, 1)

                def reduce(g, j, c):
                    pe.wait_ge(vr, CH * g + c + 1)
                    last = pe.matmul(s_ps[0:HEADS, j, :], heads[:, c, :], uv[:, j, c, :], start=(c == 0), stop=(c == CH - 1))
                    if c == CH - 1:
                        last.then_inc(red, 1)

                def bring_back(g):
                    pe.wait_ge(ssr, g + 1)
                    pe.nop(nofuse=True)
                    for t in range(GT):
                        last = pe.transpose(back_ps[:, t, :], ssum[:, t * P:(t + 1) * P], k["ident"][0:HEADS, 0:HEADS])
                    last.then_inc(back, 1)

                def step(g, r):
                    j = r % 2
                    known = isinstance(g, int)
                    inside, after = not (known and g >= GROUPS), not (known and g == 0)
                    if after:
                        look(g - 1, 1 - j)
                    if inside:
                        turn_hot(g, j)
                    if after:
                        reduce(g - 1, 1 - j, 0)
                        reduce(g - 1, 1 - j, 1)
                    if inside:
                        compare(g)
                    if after:
                        reduce(g - 1, 1 - j, 2)
                        reduce(g - 1, 1 - j, 3)
                    if inside:
                        turn(g, r, 0)
                        turn(g, r, 1)
                    if after:
                        bring_back(g - 1)
                    if inside:
                        turn(g, r, 2)
                        turn(g, r, 3)

                for g in range(RING):
                    step(g, g)
                with pe.Fori(1, GROUPS // RING) as i:
                    for r in range(RING):
                        step(RING * i + r, r)
                step(GROUPS, 0)

            @block.scalar
            def _(act):
                act.wait_ge(wready, 2 * CH + 1)

                def step(g, j):
                    known = isinstance(g, int)
                    act.wait_ge(tr_done, g + 1)
                    if not (known and g == 0):
                        act.wait_ge(look_done, g)
                    act.copy(hot_t[:, :, :], tr_ps[:, :, :]).then_inc(htr, 1)
                    if not (known and g < 2):
                        act.wait_ge(red, g - 1)
                    for c in range(CH):
                        act.wait_ge(dturned, CH * g + c + 1)
                        act.activation(ab[:, j, c, :], d_ps[:, c % 2, :], ACT.Abs).then_inc(abr, 1)
                        act.wait_ge(abr, CH * g + c + 1)
                        act.activation(uv[:, j, c, :], ab[:, j, c, :], ACT.Identity, bias=raw[:, 0, c:c + 1],
                                       scale=raw[:, 1, c:c + 1]).then_inc(ur, 1)

                step(0, 0)
                step(1, 1)
                with act.Fori(1, GROUPS // 2) as i:
                    for j in range(2):
                        step(2 * i + j, j)


def edge_softmax(nc, k, sem, sorted_d):
    L = SQ * P
    with ExitStack() as ctx:
        s = Space(nc, ctx)
        rows = s.sb("rows", [P, Q, RW], U32)
        keys = s.sb("keys", [P, SQ, STRIPS, HEADS])
        scores = s.sb("scores", [P, SQ, STRIPS, HEADS])
        keyq = s.sb("keyq", [P, Q])
        al = s.sb("al", [P, L])
        ky = s.sb("ky", [P, L])
        cont = s.sb("cont", [P, L + 1])
        pen = s.sb("pen", [P, L + 1])
        fw = s.sb("fw", [P, L])
        top = s.sb("top", [P, L])
        ex = s.sb("ex", [P, L])
        den = s.sb("den", [P, L])
        whole = s.sb("whole", [P, 4])
        edge = s.sb("edge", [P, 1])
        carry = s.sb("carry", [P, 1])
        hm = s.sb("hm", [1, 2, HEADS, STRIPS])
        run = s.sb("run", [1, HEADS, STRIPS])
        cin = s.sb("cin", [1, STRIPS, HEADS])
        shift_t = s.sb("shift_t", [P, P])
        a_ps = s.ps("a_ps", [P, 2, 512])
        k_ps = s.ps("k_ps", [P, 2, 512])
        c_ps = s.ps("c_ps", [P, 4, 512])

        rin, targets, kready = sem("rows_in"), sem("targets_ready"), sem("keys_ready")
        kready0, scready = sem("key_read"), sem("scores_laid")
        ta, tk, ea, ek = sem("scores_turned"), sem("keys_turned"), sem("scores_kept"), sem("keys_kept")
        ask, answer = sem("carry_ask"), sem("carry_answer")
        sub, exped, att_ready, tb_done, tkept = sem("shifted"), sem("exped"), sem("att_ready"), sem("att_turned"), sem("att_kept")
        groups = [range(g, min(g + 4, SQ)) for g in range(0, SQ, 4)]

        with nc.Block() as block:
            @block.sync
            def _(sp):
                sp.dma_start(rows[:, :, :], sorted_d[0:CAP, :].rearrange("(p q) w -> p q w", p=P)).then_inc(rin, 16)

            @block.gpsimd
            def _(pool):
                pool.wait_ge(rin, 16)
                pool.tensor_copy(k["target"][:, :], rows[:, :, HEADS + 1]).then_inc(targets, 1)

            @block.tensor
            def _(pe):
                pe.wait_ge(rin, 16)
                pe.wait_ge(kready, 1)
                pe.wait_ge(scready, 1)
                for g, ts in enumerate(groups):
                    if g >= 2:
                        pe.wait_ge(ea, g - 1)
                        pe.wait_ge(ek, g - 1)
                    for n, t in enumerate(ts):
                        la = pe.transpose(a_ps[:, g % 2, n * P:(n + 1) * P], scores[:, t, :, :].rearrange("p s h -> p (s h)"), k["ident"][:, :])
                    la.then_inc(ta, 1)
                    for n, t in enumerate(ts):
                        lk = pe.transpose(k_ps[:, g % 2, n * P:(n + 1) * P], keys[:, t, :, :].rearrange("p s h -> p (s h)"), k["ident"][:, :])
                    lk.then_inc(tk, 1)
                pe.wait_ge(ask, 1)
                pe.transpose(c_ps[:, 0, 0:P], k["shift"][:, :], k["ident"][:, :]).then_inc(answer, 1)
                pe.matmul(c_ps[:, 1, 0:1], k["shift"][:, :], ky[:, L - 1:L], start=True, stop=True).then_inc(answer, 1)
                pe.wait_ge(ask, 2)
                pe.matmul(c_ps[:, 2, 0:1], shift_t[:, :], cont[:, 0:1], start=True, stop=True).then_inc(answer, 1)
                n = 3
                for whole_col in (1, 3, 0, 3):
                    pe.wait_ge(ask, n)
                    pe.transpose(c_ps[0:1, 0, 0:P], whole[:, whole_col:whole_col + 1], k["ident"][:, :])
                    pe.transpose(c_ps[0:1, 1, 0:P], edge[:, :], k["ident"][:, :]).then_inc(answer, 1)
                    pe.wait_ge(ask, n + 1)
                    pe.transpose(c_ps[:, 2, 0:1], cin[:, :, :].rearrange("p s h -> p (s h)"), k["ident"][0:1, 0:1]).then_inc(answer, 1)
                    n += 2
                for g, ts in enumerate(groups):
                    pe.wait_ge(att_ready, g + 1)
                    if g >= 2:
                        pe.wait_ge(tkept, g - 1)
                    for n, t in enumerate(ts):
                        last = pe.transpose(a_ps[:, g % 2, n * P:(n + 1) * P], ex[:, t * P:(t + 1) * P], k["ident"][:, :])
                    last.then_inc(tb_done, 1)

            @block.scalar
            def _(act):
                act.wait_ge(rin, 16)
                act.copy(scores[:, :, :, :],
                         rows[:, :, 0:HEADS].bitcast(F32).rearrange("p (s t) h -> p t s h", t=SQ)).then_inc(scready, 1)
                for g, ts in enumerate(groups):
                    act.wait_ge(ta, g + 1)
                    act.copy(al[:, ts[0] * P:(ts[-1] + 1) * P], a_ps[:, g % 2, 0:len(ts) * P]).then_inc(ea, 1)
                act.wait_ge(sub, 1)
                act.activation(ex[:, :], top[:, :], ACT.Exp).then_inc(exped, 1)
                att4 = k["att"][:, :, :].rearrange("p (s t) h -> p t s h", t=SQ)
                for g, ts in enumerate(groups):
                    act.wait_ge(tb_done, g + 1)
                    act.copy(att4[:, ts[0]:ts[-1] + 1, :, :],
                             a_ps[:, g % 2, 0:len(ts) * P].rearrange("p (t s h) -> p t s h", s=STRIPS, h=HEADS)).then_inc(tkept, 1)

            @block.vector
            def _(dve):
                link = k["dve_chain"].on(dve)
                dve.wait_ge(rin, 16)
                dve.tensor_scalar(keyq[:, :], rows[:, :, HEADS], 1.0, None, ALU.add).then_inc(kready0, 1)
                dve.wait_ge(kready0, 1)
                dve.tensor_copy(keys[:, :, :, :], bcast(keyq[:, :].rearrange("p (s t) -> p t s", t=SQ), 3, HEADS)).then_inc(kready, 1)
                link(dve.tensor_copy(k["tile_block_i"][:, :], k["tile_block"][:, :]))
                dve.wait_ge(kready, 1)
                link(dve.scalar_tensor_tensor(k["neg_local"][:, :], k["tile_block"][:, :], float(P), keyq[:, :], ALU.mult, ALU.subtract))
                link(dve.tensor_scalar(k["neg_local"][:, :], k["neg_local"][:, :], 1.0, None, ALU.add))
                for g, ts in enumerate(groups):
                    dve.wait_ge(tk, g + 1)
                    dve.tensor_copy(ky[:, ts[0] * P:(ts[-1] + 1) * P], k_ps[:, g % 2, 0:len(ts) * P]).then_inc(ek, 1)
                dve.wait_ge(ek, len(groups))
                dve.nop().then_inc(ask, 1)
                dve.wait_ge(answer, 2)
                link(dve.tensor_copy(shift_t[:, :], c_ps[:, 0, 0:P]))
                link(dve.tensor_tensor(cont[:, 1:L], ky[:, 1:L], ky[:, 0:L - 1], ALU.is_equal))
                dve.tensor_tensor(cont[:, 0:1], ky[:, 0:1], c_ps[:, 1, 0:1], ALU.is_equal).then_inc(ask, 1)
                dve.wait_ge(answer, 3)
                link(dve.tensor_copy(cont[:, L:L + 1], c_ps[:, 2, 0:1]))
                link(dve.tensor_scalar(pen[:, :], cont[:, :], -1.0, BIG, ALU.add, ALU.mult))
                link(dve.tensor_reduce(whole[:, 0:1], cont[:, 0:L], AX_X, ALU.min))
                link(dve.tensor_reduce(whole[:, 1:2], pen[:, 0:L], AX_X, ALU.min))
                link(dve.tensor_reduce(whole[:, 3:4], pen[:, 1:L + 1], AX_X, ALU.min))
                link(dve.memset(cin[:, :, :], 0.0))
                asked = [2]
                answered = [3]

                def segments(out, gate, data, neutral, op0, op1, back):
                    flip = (lambda ap: ap[:, ::-1]) if back else (lambda ap: ap)
                    link(dve.tensor_tensor_scan(flip(out), flip(gate), flip(data), neutral, op0, op1))
                    end = out[:, 0:1] if back else out[:, L - 1:L]
                    dve.tensor_copy(edge[:, :], end).then_inc(ask, 1)
                    asked[0] += 1
                    answered[0] += 1
                    dve.wait_ge(answer, answered[0])
                    order = slice(None, None, -1) if back else slice(None)
                    for n in range(2):
                        got = c_ps[0:1, n, 0:P].rearrange("p (s h) -> p h s", h=HEADS)
                        link(dve.tensor_copy(hm[:, n, :, :], got[:, :, order]))
                    flat = lambda ap: ap.rearrange("p h s -> p (h s)")
                    link(dve.tensor_tensor_scan(flat(run[:, :, :]), flat(hm[:, 0, :, :]), flat(hm[:, 1, :, :]),
                                                neutral, op0, op1))
                    took = run[:, :, 0:STRIPS - 1].rearrange("p h s -> p s h")
                    if back:
                        link(dve.memset(cin[:, STRIPS - 1:STRIPS, :], 0.0))
                        dve.tensor_copy(cin[:, 0:STRIPS - 1, :], took[:, ::-1, :]).then_inc(ask, 1)
                    else:
                        link(dve.memset(cin[:, 0:1, :], 0.0))
                        dve.tensor_copy(cin[:, 1:STRIPS, :], took).then_inc(ask, 1)
                    asked[0] += 1
                    answered[0] += 1
                    dve.wait_ge(answer, answered[0])
                    link(dve.tensor_copy(carry[:, :], c_ps[:, 2, 0:1]))
                    link(dve.tensor_tensor_scan(flip(out), flip(gate), flip(data), carry[:, :], op0, op1))

                dve.wait_ge(ea, len(groups))
                segments(fw[:, :], pen[:, 0:L], al[:, :], -BIG, ALU.add, ALU.max, False)
                segments(top[:, :], pen[:, 1:L + 1], fw[:, :], -BIG, ALU.add, ALU.max, True)
                dve.tensor_tensor(top[:, :], al[:, :], top[:, :], ALU.subtract).then_inc(sub, 1)
                dve.wait_ge(exped, 1)
                segments(fw[:, :], cont[:, 0:L], ex[:, :], 0.0, ALU.mult, ALU.add, False)
                segments(den[:, :], pen[:, 1:L + 1], fw[:, :], 0.0, ALU.add, ALU.max, True)
                link(dve.tensor_scalar(den[:, :], den[:, :], 1e-16, None, ALU.add))
                for ts in groups:
                    cols = slice(ts[0] * P, (ts[-1] + 1) * P)
                    link(dve.reciprocal(den[:, cols], den[:, cols]))
                    dve.tensor_tensor(ex[:, cols], ex[:, cols], den[:, cols], ALU.mult).then_inc(att_ready, 1)


def sum_messages(nc, k, sem, he_d):
    B, RING, BK = 4, 4, 8
    SL = B * RING
    HV = 6
    x_sb = k["x_sb"]
    with ExitStack() as ctx:
        s = Space(nc, ctx)
        ix = s.sb("ixm", [P, SL], U32)
        g = s.sb("g", [P, SL, HEADS, D])
        msg = s.sb("msg", [P, SL, HEADS, D])
        off = s.sb("off", [P, SL, P])
        hot = s.sb("hot", [P, SL, P])
        m_ps = s.ps("m_ps", [P, BK, F])
        ixr, hots, summed, added = sem("m_indices"), sem("m_hot"), sem("m_summed"), sem("m_added")
        made, made_act, offs = sem("m_made"), sem("m_made_act"), sem("m_off")
        got = [sem(f"m_rows_in{r}") for r in range(RING)]

        with nc.Block() as block:
            @block.gpsimd
            def _(pool):
                def gather(m, r):
                    pool.tensor_copy(ix[:, r * B:(r + 1) * B], k["target"][:, bass.ds(m * B, B)]).then_inc(ixr, 1)
                    pool.wait_ge(ixr, m + 1)
                    pool.nop(nofuse=True)
                    for j in range(r * B, (r + 1) * B):
                        pool.indirect_dma_start(g[:, j, :, :].rearrange("p h d -> p (h d)"), None, he_d,
                                                bass.IndirectOffsetOnAxis(ap=ix[:, j:j + 1], axis=0)).then_inc(got[r], 16)

                for m in range(RING):
                    gather(m, m)
                with pool.Fori(1, Q // SL) as i:
                    for r in range(RING):
                        pool.wait_ge(made, SL * i + r * B - SL + B)
                        pool.wait_ge(made_act, SL * i + r * B - SL + B)
                        gather(RING * i + r, r)

            @block.scalar
            def _(act):
                def one_hots(q, r):
                    act.nop(nofuse=True)
                    for t in range(B):
                        act.activation(off[:, r * B + t, :], k["iota"][:, :], ACT.Abs,
                                       bias=k["neg_local"][:, bass.ds(q + t, 1)]).then_inc(offs, 1)
                    for t in range(B):
                        act.wait_ge(offs, q + t + 1)
                        act.activation(hot[:, r * B + t, :], off[:, r * B + t, :], ACT.Relu, bias=1.0, scale=-1.0).then_inc(hots, 1)

                def weight(q, r, i):
                    act.wait_ge(got[r], 16 * B * (i + 1))
                    act.nop(nofuse=True)
                    for t in range(B):
                        for h in range(HV, HEADS):
                            last = act.activation(msg[:, r * B + t, h, :], g[:, r * B + t, h, :], ACT.Copy,
                                                  scale=k["att"][:, bass.ds(q + t, 1), h])
                        last.then_inc(made_act, 1)

                for r in range(RING):
                    one_hots(r * B, r)
                    weight(r * B, r, 0)
                with act.Fori(1, Q // SL) as i:
                    for r in range(RING):
                        act.wait_ge(summed, SL * i + r * B - SL + B)
                        one_hots(SL * i + r * B, r)
                        weight(SL * i + r * B, r, i)

            @block.vector
            def _(dve):
                def batch(q, r, i):
                    known = isinstance(q, int)
                    before = not (known and q == 0)
                    if before:
                        _, blocks = nc.values_load_multi_w_load_instructions(
                            k["tile_block_i"][0:1, bass.ds(q - B, B)], engines=[mybir.EngineType.DVE], min_val=0, max_val=NB - 1,
                            skip_runtime_bounds_check_because="a tile's block counts comparisons with NB - 1 blocks")
                    if not (known and q == Q):
                        dve.wait_ge(got[r], 16 * B * (i + 1))
                    for t in range(B):
                        j = r * B + t
                        if not (known and q == Q):
                            dve.tensor_tensor(msg[:, j, 0:HV, :], g[:, j, 0:HV, :],
                                              bcast(k["att"][:, bass.ds(q + t, 1), 0:HV].rearrange("p a h -> p (a h)"), 2, D),
                                              ALU.mult).then_inc(made, 1)
                        if before:
                            if not (known and q == B and t == 0):
                                dve.wait_ge(added, q - B + t)
                            dve.wait_ge(summed, q - B + t + 1)
                            sl = x_sb[:, bass.ds(blocks[t], 1), :].rearrange("p a f -> p (a f)")
                            dve.tensor_tensor(sl, m_ps[:, (r - 1) % 2 * B + t, :], sl, ALU.add).then_inc(added, 1)

                for r in range(RING):
                    batch(r * B, r, 0)
                with dve.Fori(1, Q // SL) as i:
                    for r in range(RING):
                        batch(SL * i + r * B, r, i)
                batch(Q, 0, Q // SL)

            @block.tensor
            def _(pe):
                def total(q, r):
                    for t in range(B):
                        j = r * B + t
                        if not (isinstance(q, int) and q < BK):
                            pe.wait_ge(added, q + t - BK + 1)
                        pe.wait_ge(hots, q + t + 1)
                        pe.wait_ge(made, q + t + 1)
                        pe.wait_ge(made_act, q + t + 1)
                        pe.matmul(m_ps[:, j % BK, :], hot[:, j, :], msg[:, j, :, :].rearrange("p h d -> p (h d)"),
                                  start=True, stop=True).then_inc(summed, 1)

                for r in range(RING):
                    total(r * B, r)
                with pe.Fori(1, Q // SL) as i:
                    for r in range(RING):
                        total(SL * i + r * B, r)


def route(nc, k, sem, wg, w1, b1, w2, b2, xn_d, slot_d):
    x_sb = k["x_sb"]
    XR = 10
    GB = 4
    with ExitStack() as ctx:
        s = Space(nc, ctx)
        st = s.sb("st2", [P, NB, 6])
        mv = s.sb("mv2", [P, NB, 2])
        var = s.sb("var2", [P, NB])
        root = s.sb("root2", [P, NB])
        rstd = s.sb("rstd2", [P, NB])
        xn = s.sb("xn2", [P, XR, F])
        spare = s.sb("spare", [P, NT, 2], I32)
        xt = s.sb("xt2", [P, 2, CH, GB * P])
        lt = s.sb("logits_t", [EXPERTS, GB * P])
        wg_sb = s.sb("wg_sb", [P, CH, EXPERTS])
        rankw = s.sb("rankw", [P, EXPERTS])
        lg = s.sb("lg", [P, NB, EXPERTS])
        g = s.sb("gate", [P, NB, EXPERTS])
        mask = s.sb("mask", [P, 2, NB, EXPERTS])
        tmp = s.sb("tmp", [P, NB, EXPERTS])
        best = s.sb("best", [P, 2, NB])
        v3 = s.sb("v3", [P, NB])
        token_i = s.sb("token_i", [P, NB], I32)
        valid = s.sb("token_valid", [P, NB])
        gate = s.sb("new_expert", [P, EXPERTS, NB])
        used = s.sb("used", [P, EXPERTS, NB])
        slot = s.sb("slot", [P, EXPERTS, NB])
        count = s.sb("count", [P, EXPERTS])
        bi = s.sb("bi2", [P, EXPERTS], I32)
        nt = s.sb("nt2", [P, EXPERTS])
        ends = s.sb("ends2", [P, EXPERTS])
        start = s.sb("start2", [P, EXPERTS])
        base = s.sb("base", [P, EXPERTS])
        picked = s.sb("picked2", [P, NB, EXPERTS])
        pos = s.sb("pos2", [P, 2, NB])
        posi = s.sb("posi2", [P, 3, 2, NB], I32)
        posf = s.sb("posf2", [P, 2, NB])
        dump_i = s.sb("dump2_i", [P, 2, NB], I32)
        dump = s.sb("dump2", [P, 2, NB])
        rowid = s.sb("slot_row", [P, 2, NB], U32)
        words = s.sb("slot_words", [P, 2, NB, 2], I32)
        ti = s.sb("tile_i", [P, NT], I32)
        tf = s.sb("tile_f", [P, NT])
        cmp = s.sb("cmp2", [P, NT, EXPERTS - 1])
        te = s.sb("te", [P, NT])
        t_ps = s.ps("t2_ps", [P, 2, F])
        g_ps = s.ps("g_ps", [P, NB, EXPERTS])
        l_ps = s.ps("l2_ps", [EXPERTS, GB * P])
        c_ps = s.ps("c2_ps", [P, 2, 512])

        stats, rready, rdone, wgin = sem("stats2"), sem("var_ready2"), sem("root_done2"), sem("wg_in")
        xn_ready, tp, xt_ready, gated, lgr, exped = sem("xn_ready2"), sem("x_turned2"), sem("xt_ready2"), sem("gated"), sem("logits"), sem("gate_exped")
        xn_out = [sem(f"xn_out{j}") for j in range(XR // 2)]
        ready, filled = sem("spare_ready"), sem("spare_filled")
        ids, counted, offsets, rowr = sem("token_ids"), sem("tokens_counted"), sem("offsets"), sem("slot_rows")
        logit, kept = sem("logits_t_done"), sem("logits_t_kept")
        scattered, slots_in = sem("slots_scattered"), sem("slots_in")

        with nc.Block() as block:
            @block.sync
            def _(sp):
                sp.dma_start(wg_sb[:, :, :], wg.rearrange("(c p) e -> p c e", p=P)).then_inc(wgin, 16)
                sp.wait_ge(ready, 2)
                sp.dma_start(slot_d[0:NT * P, :].rearrange("(p t) w -> p t w", p=P), spare[:, :, :]).then_inc(filled, 16)
                for c in range(NB // 2):
                    j = c % (XR // 2)
                    sp.wait_ge(xn_ready, 2 * c + 2)
                    sp.dma_start(xn_d[2 * c * P:(2 * c + 2) * P, :].rearrange("(b p) f -> p b f", p=P),
                                 xn[:, 2 * j:2 * j + 2, :]).then_inc(xn_out[j], 16)
                win = k["weights_in"]
                for e in range(EXPERTS):
                    sp.dma_start(k["w1_sb"][:, e, :, :], w1[e, :, :].rearrange("(c p) h -> p c h", p=P)).then_inc(win, 16)
                sp.dma_start(k["b1_sb"][:, :, :].rearrange("p e h -> p (e h)"),
                             b1.rearrange("e h -> (e h)").partition_broadcast(P)).then_inc(win, 16)
                for e in range(EXPERTS):
                    sp.dma_start(k["w2_sb"][:, e, :, :], w2[e, :, :].rearrange("(c p) f -> p c f", p=P)).then_inc(win, 16)
                sp.dma_start(k["b2_sb"][:, :, :].rearrange("p e f -> p (e f)"),
                             b2.rearrange("e f -> (e f)").partition_broadcast(P)).then_inc(win, 16)
                for j in range(XR // 2):
                    sp.wait_ge(xn_out[j], 16 * (NB // XR))
                sp.wait_ge(scattered, 16 * 2 * NB)
                sp.dma_start(k["slots"][:, :, :], slot_d[0:NT * P, :].rearrange("(p t) w -> p t w", p=P)).then_inc(slots_in, 16)
                sp.wait_ge(slots_in, 16)

            @block.gpsimd
            def _(pool):
                pool.iota(spare[:, :, 1:2], pattern=[[1, NT], [0, 1]], base=2 * NB * P, channel_multiplier=NT).then_inc(ready, 1)
                pool.memset(spare[:, :, 0:1], 0).then_inc(ready, 1)
                pool.iota(token_i[:, :], pattern=[[P, NB]], base=0, channel_multiplier=1).then_inc(ids, 1)
                pool.iota(words[:, :, :, 1], pattern=[[NB * P, 2], [P, NB]], base=0, channel_multiplier=1).then_inc(ids, 1)
                pool.iota(dump_i[:, :, :], pattern=[[P, 2], [0, NB]], base=NT * P, channel_multiplier=1).then_inc(ids, 1)
                pool.iota(ti[:, :], pattern=[[1, NT]], base=0, channel_multiplier=0).then_inc(ids, 1)
                pool.memset(gate[:, :, :], 1.0).then_inc(ids, 1)
                pool.wait_ge(ids, 5)
                pool.tensor_copy(words[:, 0, :, 0], token_i[:, :]).then_inc(ids, 1)
                pool.tensor_copy(words[:, 1, :, 0], token_i[:, :]).then_inc(ids, 1)
                pool.tensor_copy(tf[:, :], ti[:, :]).then_inc(ids, 1)
                pool.memset(gate[:, :, 0:1], 0.0).then_inc(ids, 1)
                pool.wait_ge(ids, 9)
                pool.wait_ge(rowr, 1)
                pool.wait_ge(filled, 16)
                for b in range(NB):
                    for c in range(2):
                        pool.indirect_dma_start(slot_d, bass.IndirectOffsetOnAxis(ap=rowid[:, c, b:b + 1], axis=0),
                                                words[:, c, b, :], None).then_inc(scattered, 16)
                pool.wait_ge(scattered, 16 * 2 * NB)

            @block.scalar
            def _(act):
                act.wait_ge(rready, 1)
                act.activation(root[:, :], var[:, :], ACT.Sqrt).then_inc(rdone, 1)

                def keep(group):
                    act.wait_ge(logit, group + 1)
                    if group >= 1:
                        act.wait_ge(gated, group)
                    act.copy(lt[:, :], l_ps[:, :]).then_inc(kept, 1)

                for b in range(NB):
                    act.wait_ge(tp, b + 1)
                    group, t = b // GB, b % GB
                    if group >= 2 and t == 0:
                        act.wait_ge(logit, group - 1)
                    act.copy(xt[:, group % 2, :, t * P:(t + 1) * P],
                             t_ps[:, b % 2, :].rearrange("p (c n) -> p c n", c=CH)).then_inc(xt_ready, 1)
                    if b % GB == 1 and group >= 1:
                        keep(group - 1)
                keep(NB // GB - 1)
                act.wait_ge(lgr, 1)
                act.activation(lg[:, :, :], lg[:, :, :], ACT.Exp).then_inc(exped, 1)

            @block.tensor
            def _(pe):
                pe.wait_ge(wgin, 16)

                def logits(group):
                    pe.wait_ge(xt_ready, (group + 1) * GB)
                    if group >= 1:
                        pe.wait_ge(kept, group)
                    for c in range(CH):
                        last = pe.matmul(l_ps[:, :], wg_sb[:, c, :], xt[:, group % 2, c, :], start=(c == 0), stop=(c == CH - 1))
                    last.then_inc(logit, 1)

                def turn_back(group):
                    pe.wait_ge(kept, group + 1)
                    for t in range(GB):
                        last = pe.transpose(g_ps[:, group * GB + t, :], lt[:, t * P:(t + 1) * P],
                                            k["ident"][0:EXPERTS, 0:EXPERTS])
                    last.then_inc(gated, 1)

                for b in range(NB):
                    pe.wait_ge(xn_ready, b + 1)
                    if b >= 2:
                        pe.wait_ge(xt_ready, b - 1)
                    for c in range(CH):
                        last = pe.transpose(t_ps[:, b % 2, c * P:(c + 1) * P], xn[:, b % XR, c * P:(c + 1) * P], k["ident"][:, :])
                    last.then_inc(tp, 1)
                    if b % GB == 0 and b >= GB:
                        logits(b // GB - 1)
                    if b % GB == GB - 1 and b >= GB:
                        turn_back(b // GB - 1)
                logits(NB // GB - 1)
                turn_back(NB // GB - 1)
                pe.wait_ge(counted, 1)
                pe.matmul(c_ps[:, 0, 0:EXPERTS], k["before"][:, :], count[:, :], start=True, stop=True)
                pe.matmul(c_ps[:, 1, 0:EXPERTS], k["ones"][:, :], count[:, :], start=True, stop=True).then_inc(offsets, 1)

            @block.vector
            def _(dve):
                link = k["dve_chain"].on(dve)
                for b in range(NB):
                    dve.bn_stats(st[:, b, :], x_sb[:, b, :]).then_inc(stats, 1)
                dve.wait_ge(stats, NB)
                for b in range(NB):
                    dve.bn_aggr(mv[:, b, :], st[:, b, :]).then_inc(stats, 1)
                dve.wait_ge(stats, 2 * NB)
                normalise_stats(dve, rready, rdone, link, mv, var[:, :], root[:, :], rstd[:, :])
                for b in range(NB):
                    if b >= XR:
                        dve.wait_ge(tp, b - XR + 1)
                        dve.wait_ge(xn_out[b % XR // 2], 16 * (b // XR))
                    dve.tensor_scalar(xn[:, b % XR, :], x_sb[:, b, :], mv[:, b, 0:1], rstd[:, b:b + 1],
                                      ALU.subtract, ALU.mult).then_inc(xn_ready, 1)
                dve.wait_ge(ids, 9)
                link(dve.tensor_copy(valid[:, :], token_i[:, :]))
                link(dve.tensor_scalar(valid[:, :], valid[:, :], float(N), None, ALU.is_lt))
                link(dve.tensor_copy(dump[:, :, :], dump_i[:, :, :]))
                link(dve.tensor_scalar(v3[:, :], valid[:, :], -1.0, 1.0, ALU.mult, ALU.add))
                link(dve.tensor_tensor(dump[:, :, :], dump[:, :, :], bcast(v3[:, :], 1, 2), ALU.mult))
                link(dve.tensor_scalar(rankw[:, :], k["iota"][:, 0:EXPERTS], -1.0, float(EXPERTS), ALU.mult, ALU.add))
                dve.wait_ge(gated, NB // GB)
                ex3 = lambda v: bcast(v, 2, EXPERTS)
                link(dve.tensor_copy(g[:, :, :], g_ps[:, :, :]))
                link(dve.tensor_reduce(v3[:, :], g[:, :, :], AX_X, ALU.max))
                dve.tensor_tensor(lg[:, :, :], g[:, :, :], ex3(v3[:, :]), ALU.subtract).then_inc(lgr, 1)
                dve.wait_ge(exped, 1)
                link(dve.tensor_reduce(v3[:, :], lg[:, :, :], AX_X, ALU.add))
                link(dve.reciprocal(v3[:, :], v3[:, :]))
                link(dve.tensor_tensor(g[:, :, :], lg[:, :, :], ex3(v3[:, :]), ALU.mult))

                def pick(src, n):
                    m = mask[:, n, :, :]
                    link(dve.tensor_reduce(best[:, n, :], src[:, :, :], AX_X, ALU.max))
                    link(dve.tensor_tensor(m, src[:, :, :], ex3(best[:, n, :]), ALU.is_equal))
                    link(dve.tensor_tensor(m, m, bcast(rankw[:, :], 1, NB), ALU.mult))
                    link(dve.tensor_reduce(v3[:, :], m, AX_X, ALU.max))
                    link(dve.tensor_tensor(m, m, ex3(v3[:, :]), ALU.is_equal))

                pick(g, 0)
                link(dve.scalar_tensor_tensor(tmp[:, :, :], mask[:, 0, :, :], -2.0, g[:, :, :], ALU.mult, ALU.add))
                pick(tmp, 1)
                for n in range(2):
                    link(dve.tensor_tensor(mask[:, n, :, :], mask[:, n, :, :], ex3(valid[:, :]), ALU.mult))
                link(dve.tensor_tensor(used[:, :, :].rearrange("p e b -> p b e"), mask[:, 0, :, :], mask[:, 1, :, :], ALU.add))
                dve.tensor_reduce(count[:, :], used[:, :, :], AX_X, ALU.add).then_inc(counted, 1)
                flat = lambda ap: ap.rearrange("p e b -> p (e b)")
                link(dve.tensor_tensor_scan(flat(slot[:, :, :]), flat(gate[:, :, :]), flat(used[:, :, :]), 0.0, ALU.mult, ALU.add))
                link(dve.tensor_tensor(slot[:, :, :], slot[:, :, :], used[:, :, :], ALU.subtract))
                dve.wait_ge(offsets, 1)
                link(dve.tensor_scalar(bi[:, :], c_ps[:, 1, 0:EXPERTS], float(P - 1), None, ALU.add))
                link(dve.tensor_scalar(bi[:, :], bi[:, :], 7, None, ALU.logical_shift_right))
                link(dve.tensor_copy(nt[:, :], bi[:, :]))
                link(dve.tensor_tensor_scan(ends[:, :], k["ones"][:, 0:EXPERTS], nt[:, :], 0.0, ALU.mult, ALU.add))
                link(dve.tensor_tensor(start[:, :], ends[:, :], nt[:, :], ALU.subtract))
                link(dve.scalar_tensor_tensor(base[:, :], start[:, :], float(P), c_ps[:, 0, 0:EXPERTS], ALU.mult, ALU.add))
                link(dve.tensor_tensor(slot[:, :, :], slot[:, :, :], bcast(base[:, :], 2, NB), ALU.add))
                for n in range(2):
                    link(dve.tensor_tensor(picked[:, :, :], mask[:, n, :, :], slot[:, :, :].rearrange("p e b -> p b e"), ALU.mult))
                    link(dve.tensor_reduce(pos[:, n, :], picked[:, :, :], AX_X, ALU.add))
                link(dve.tensor_copy(posi[:, 0, :, :], pos[:, :, :]))
                link(dve.tensor_scalar(posi[:, 1, :, :], posi[:, 0, :, :], P - 1, None, ALU.bitwise_and))
                link(dve.tensor_scalar(posi[:, 2, :, :], posi[:, 0, :, :], 7, None, ALU.logical_shift_right))
                link(dve.scalar_tensor_tensor(posf[:, :, :], posi[:, 1, :, :], float(NT), posi[:, 2, :, :], ALU.mult, ALU.add))
                dve.tensor_tensor(rowid[:, :, :], posf[:, :, :], dump[:, :, :], ALU.add).then_inc(rowr, 1)
                link(dve.tensor_tensor(cmp[:, :, :], bcast(tf[:, :], 2, EXPERTS - 1), bcast(start[:, 1:], 1, NT), ALU.is_ge))
                link(dve.tensor_reduce(te[:, :], cmp[:, :, :], AX_X, ALU.add))
                dve.tensor_copy(k["tile_expert"][:, :], te[:, :])
                link(dve.tensor_tensor(v3[:, :], best[:, 0, :], best[:, 1, :], ALU.add))
                link(dve.tensor_scalar(v3[:, :], v3[:, :], 1e-6, None, ALU.add))
                link(dve.reciprocal(v3[:, :], v3[:, :]))
                dve.tensor_tensor(k["share"][:, :, :], best[:, :, :], bcast(v3[:, :], 1, 2), ALU.mult)


def experts(nc, k, sem, xn_d, pairs_d):
    R = 4
    w1, w2, b1, b2 = k["w1_sb"], k["w2_sb"], k["b1_sb"], k["b2_sb"]
    with ExitStack() as ctx:
        s = Space(nc, ctx)
        token = s.sb("token_ix", [P, R], U32)
        pair = s.sb("pair_ix", [P, R], U32)
        xr = s.sb("xr", [P, R, F])
        xt = s.sb("xt3", [P, 2, CH, P])
        hb = s.sb("hid_in", [P, 2, HID])
        ga = s.sb("hid_act", [P, 2, HID])
        ht = s.sb("hid_t", [P, 2, HCH, P])
        y = s.sb("y", [P, R, F])
        xt_ps = s.ps("xt3_ps", [P, 2, F])
        h_ps = s.ps("h_ps", [P, 2, 512])
        ht_ps = s.ps("ht_ps", [P, 2, 512])
        y_ps = s.ps("y_ps", [P, 2, F])
        gix, six = sem("token_ready"), sem("pair_ready")
        got = [sem(f"tokens_in{j}") for j in range(R)]
        y_out = [sem(f"y_out{j}") for j in range(R)]
        turned, xtr, up_done, h_ready, act_done = sem("xr_turned"), sem("xt3_ready"), sem("up_done"), sem("hid_ready"), sem("gelu_done")
        h_turned, ht_ready, down_done, y_ready = sem("hid_turned"), sem("hid_t_ready"), sem("down_done"), sem("y_ready")

        def expert_of(n, engine):
            _, (e,) = nc.values_load_multi_w_load_instructions(
                k["tile_expert"][0:1, bass.ds(n, 1)], engines=[engine], min_val=0, max_val=EXPERTS - 1,
                skip_runtime_bounds_check_because="a tile's expert counts comparisons with EXPERTS - 1 experts")
            return e

        def tiles(eng, step, last):
            rounds = (last - 3) // R
            for n in range(R):
                step(n, n, 0)
            with eng.Fori(1, rounds) as i:
                for r in range(R):
                    step(R * i + r, r, i)
            for n in range(R * rounds, last):
                step(n, n % R, n // R)

        with nc.Block() as block:
            @block.gpsimd
            def _(pool):
                def gather(n, r):
                    pool.tensor_copy(token[:, r:r + 1], k["slots"][:, bass.ds(n, 1), 0]).then_inc(gix, 1)
                    pool.wait_ge(gix, n + 1)
                    pool.nop(nofuse=True)
                    pool.indirect_dma_start(xr[:, r, :], None, xn_d,
                                            bass.IndirectOffsetOnAxis(ap=token[:, r:r + 1], axis=0)).then_inc(got[r], 16)

                def scatter(n, r, i):
                    if not (isinstance(i, int) and i == 0):
                        pool.wait_ge(y_out[r], 16 * i)
                    pool.tensor_copy(pair[:, r:r + 1], k["slots"][:, bass.ds(n, 1), 1]).then_inc(six, 1)
                    pool.wait_ge(six, n + 1)
                    pool.wait_ge(y_ready, n + 1)
                    pool.nop(nofuse=True)
                    pool.indirect_dma_start(pairs_d, bass.IndirectOffsetOnAxis(ap=pair[:, r:r + 1], axis=0),
                                            y[:, r, :], None).then_inc(y_out[r], 16)

                for n in range(R):
                    gather(n, n)

                def step(n, r, i):
                    if not (isinstance(n, int) and n + R >= NT):
                        pool.wait_ge(turned, n + 1)
                        gather(n + R, r)
                    scatter(n, r, i)

                step(0, 0, 0)
                step(1, 1, 0)
                step(2, 2, 0)
                step(3, 3, 0)
                rounds = NT // R - 1
                with pool.Fori(1, rounds) as i:
                    for r in range(R):
                        step(R * i + r, r, i)
                for n in range(R * rounds, NT):
                    step(n, n % R, n // R)
                for r in range(R):
                    pool.wait_ge(y_out[r], 16 * len(range(r, NT, R)))

            @block.tensor
            def _(pe):
                def turn_hidden(n, j):
                    pe.wait_ge(act_done, n + 1)
                    if not (isinstance(n, int) and n < 2):
                        pe.wait_ge(ht_ready, n - 1)
                    for c in range(HCH):
                        last = pe.transpose(ht_ps[:, j, c * P:(c + 1) * P], ga[:, j, c * P:(c + 1) * P], k["ident"][:, :])
                    last.then_inc(h_turned, 1)

                def turn(n, r, i):
                    j = r % 2
                    pe.wait_ge(got[r], 16 * i + 16)
                    if not (isinstance(n, int) and n < 2):
                        pe.wait_ge(xtr, n - 1)
                    for c in range(CH):
                        last = pe.transpose(xt_ps[:, j, c * P:(c + 1) * P], xr[:, r, c * P:(c + 1) * P], k["ident"][:, :])
                    last.then_inc(turned, 1)

                def up(n, j):
                    e = expert_of(n, mybir.EngineType.PE)
                    pe.wait_ge(xtr, n + 1)
                    if not (isinstance(n, int) and n < 2):
                        pe.wait_ge(h_ready, n - 1)
                    for c in range(CH):
                        last = pe.matmul(h_ps[:, j, 0:HID], xt[:, j, c, :],
                                         w1[:, bass.ds(e, 1), c, :].rearrange("p a h -> p (a h)"),
                                         start=(c == 0), stop=(c == CH - 1))
                    last.then_inc(up_done, 1)

                def down(n, j):
                    e = expert_of(n, mybir.EngineType.PE)
                    pe.wait_ge(ht_ready, n + 1)
                    if not (isinstance(n, int) and n < 2):
                        pe.wait_ge(y_ready, n - 1)
                    for c in range(HCH):
                        last = pe.matmul(y_ps[:, j, :], ht[:, j, c, :],
                                         w2[:, bass.ds(e, 1), c, :].rearrange("p a f -> p (a f)"),
                                         start=(c == 0), stop=(c == HCH - 1))
                    last.then_inc(down_done, 1)

                def step(n, r, i):
                    j = r % 2
                    known = isinstance(n, int)
                    if not (known and n < 2):
                        turn_hidden(n - 2, j)
                    if not (known and n >= NT):
                        turn(n, r, i)
                    if not (known and (n == 0 or n > NT)):
                        up(n - 1, 1 - j)
                    if not (known and n < 2):
                        down(n - 2, j)

                pe.wait_ge(k["weights_in"], 16 * (2 * EXPERTS + 2))
                tiles(pe, step, NT + 2)

            @block.scalar
            def _(act):
                def step(n, r, i):
                    j = r % 2
                    known = isinstance(n, int)
                    if not (known and n < 2):
                        act.wait_ge(h_turned, n - 1)
                        if not (known and n < 4):
                            act.wait_ge(down_done, n - 3)
                        act.copy(ht[:, j, :, :], ht_ps[:, j, 0:HID].rearrange("p (c n) -> p c n", c=HCH)).then_inc(ht_ready, 1)
                    if not (known and n >= NT):
                        act.wait_ge(turned, n + 1)
                        if not (known and n < 2):
                            act.wait_ge(up_done, n - 1)
                        act.copy(xt[:, j, :, :], xt_ps[:, j, :].rearrange("p (c n) -> p c n", c=CH)).then_inc(xtr, 1)
                    if not (known and (n == 0 or n > NT)):
                        act.wait_ge(h_ready, n)
                        if not (known and n < 3):
                            act.wait_ge(h_turned, n - 2)
                        act.activation(ga[:, 1 - j, :], hb[:, 1 - j, :], ACT.Gelu).then_inc(act_done, 1)

                tiles(act, step, NT + 2)

            @block.vector
            def _(dve):
                def step(n, r, i):
                    j = r % 2
                    known = isinstance(n, int)
                    if not (known and (n == 0 or n > NT)):
                        e = expert_of(n - 1, mybir.EngineType.DVE)
                        dve.wait_ge(up_done, n)
                        if not (known and n < 3):
                            dve.wait_ge(act_done, n - 2)
                        dve.tensor_tensor(hb[:, 1 - j, :], h_ps[:, 1 - j, 0:HID],
                                          b1[:, bass.ds(e, 1), :].rearrange("p a h -> p (a h)"), ALU.add).then_inc(h_ready, 1)
                    if not (known and n < 2):
                        e = expert_of(n - 2, mybir.EngineType.DVE)
                        q = (r - 2) % R
                        dve.wait_ge(down_done, n - 1)
                        if not (known and n - 2 < R):
                            dve.wait_ge(y_out[q], 16 * (i if r >= 2 else i - 1))
                        dve.tensor_tensor(y[:, q, :], y_ps[:, j, :],
                                          b2[:, bass.ds(e, 1), :].rearrange("p a f -> p (a f)"), ALU.add).then_inc(y_ready, 1)

                for n in range(2 * R):
                    step(n, n % R, n // R)
                rounds = NT // R - 1
                with dve.Fori(2, rounds) as i:
                    for r in range(R):
                        step(R * i + r, r, i)
                for n in range(R * rounds, NT + 2):
                    step(n, n % R, n // R)


def combine(nc, k, sem, pairs_d, out):
    x_sb = k["x_sb"]
    G = 4
    with ExitStack() as ctx:
        s = Space(nc, ctx)
        y = s.sb("pair_rows", [P, 2, NB, F])
        pin = [sem(f"pairs_in{g}") for g in range(NB // G)]
        first, both, stored = sem("first_added"), sem("both_added"), sem("stored")

        with nc.Block() as block:
            @block.sync
            def _(sp):
                for g in range(NB // G):
                    full = G if g < NB // G - 1 else G - 1
                    for c in range(2):
                        row = (c * NB + g * G) * P
                        sp.dma_start(y[:, c, g * G:g * G + full, :],
                                     pairs_d[row:row + full * P, :].rearrange("(b p) f -> p b f", p=P)).then_inc(pin[g], 16)
                        if full < G:
                            sp.dma_start(y[0:TAIL, c, NB - 1, :],
                                         pairs_d[row + full * P:row + full * P + TAIL, :]).then_inc(pin[g], 16)
                for g in range(NB // G):
                    full = G if g < NB // G - 1 else G - 1
                    sp.wait_ge(both, (g + 1) * G)
                    sp.dma_start(out[g * G * P:(g * G + full) * P, :].rearrange("(b p) f -> p b f", p=P),
                                 x_sb[:, g * G:g * G + full, :]).then_inc(stored, 16)
                sp.dma_start(out[(NB - 1) * P:N, :], x_sb[0:TAIL, NB - 1, :]).then_inc(stored, 16)
                sp.wait_ge(stored, 16 * (NB // G + 1))

            @block.vector
            def _(dve):
                for b in range(NB):
                    rows = slice(0, P if b < NB - 1 else TAIL)
                    if b % G == 0:
                        dve.wait_ge(pin[b // G], 32 if b // G < NB // G - 1 else 64)
                    for c, done in ((0, first), (1, both)):
                        if c == 1:
                            dve.wait_ge(first, b + 1)
                        dve.scalar_tensor_tensor(x_sb[rows, b, :], y[rows, c, b, :], k["share"][rows, c, b:b + 1],
                                                 x_sb[rows, b, :], ALU.mult, ALU.add).then_inc(done, 1)


def kernel_body(nc, x, src, dst, we, wr, a, wg, w1, b1, w2, b2, out):
    dram = lambda name, shape, dt: nc.dram_tensor(name, shape, dt, kind="Internal").ap()
    sorted_d = dram("sorted_d", [CAP + DUMP, RW], U32)
    table_d = dram("table_d", [NB * P, TW], F32)
    he_d = dram("he_d", [NB * P, F], F32)
    xn_d = dram("xn_d", [NB * P, F], F32)
    slot_d = dram("slot_d", [(NT + 2) * P, 2], I32)
    pairs_d = dram("pairs_d", [(2 * NB + NT) * P, F], F32)
    with ExitStack() as ctx:
        s = Space(nc, ctx)
        sem = lambda name: ctx.enter_context(nc.semaphore(name))
        k = dict(
            iota=s.sb("iota", [P, P]), ident=s.sb("ident", [P, P]),
            ident_bf=s.sb("ident_bf", [P, P], BF16), ones=s.sb("ones", [P, P]), before=s.sb("before", [P, P]),
            shift=s.sb("shift", [P, P]),
            first_tile=s.sb("first_tile", [P, NB]), x_sb=s.sb("x_sb", [P, NB, F]),
        )
        k["dve_chain"] = Chain(sem("dve_chain"))
        k["tile_block"] = s.sb("tile_block", [P, Q])
        build_constants(nc, k, sem)
        with ExitStack() as scoring:
            e = Space(nc, scoring)
            k.update(
                ends=e.sb("edge_ends", [P, T, 2], U32),
                loc=e.sb("edge_loc", [P, T + GT]),
                oh_blk=e.sb("oh_blk", [P, T, NB], BF16),
                first=e.sb("first", [P, NB, T + 1]),
                same=e.sb("same", [P, NB, T + 1], BF16),
                dump=e.sb("dump", [P, T]),
            )
            project(nc, k, sem, x, src, dst, we, wr, a, table_d, he_d, sorted_d)
            score_edges(nc, k, sem, a, table_d, sorted_d)
        k["att"] = s.sb("att", [P, Q, HEADS])
        k["target"] = s.sb("target", [P, Q], U32)
        k["neg_local"] = s.sb("neg_local", [P, Q])
        k["tile_block_i"] = s.sb("tile_block_i", [P, Q], I32)
        edge_softmax(nc, k, sem, sorted_d)
        sum_messages(nc, k, sem, he_d)
        k["share"] = s.sb("share", [P, 2, NB])
        k["weights_in"] = sem("expert_weights_in")
        with ExitStack() as ffn:
            w = Space(nc, ffn)
            k.update(
                slots=w.sb("slots", [P, NT, 2], I32),
                tile_expert=w.sb("tile_expert", [P, NT], I32),
                w1_sb=w.sb("w1_sb", [P, EXPERTS, CH, HID]), w2_sb=w.sb("w2_sb", [P, EXPERTS, HCH, F]),
                b1_sb=w.sb("b1_sb", [P, EXPERTS, HID]), b2_sb=w.sb("b2_sb", [P, EXPERTS, F]),
            )
            route(nc, k, sem, wg, w1, b1, w2, b2, xn_d, slot_d)
            experts(nc, k, sem, xn_d, pairs_d)
        combine(nc, k, sem, pairs_d, out)


_INS = ['x', 'src', 'dst', 'L0_gnn_W_e', 'L0_gnn_W_r', 'L0_gnn_a', 'L0_ffn_Wg', 'L0_ffn_W1', 'L0_ffn_b1', 'L0_ffn_W2', 'L0_ffn_b2']
_OUTS = [((N, F), 'float32')]


def kernel(**inputs):
    import numpy as _np
    import concourse.bacc as _bacc
    from concourse import mybir as _mybir
    from concourse.bass_utils import run_bass_kernel_spmd as _run

    nc = _bacc.Bacc("TRN2", target_bir_lowering=False, num_devices=1)
    arrays, args = {}, []
    for name in _INS:
        a = _np.ascontiguousarray(inputs[name])
        arrays[f"in_{name}_dram"] = a
        args.append(nc.dram_tensor(f"in_{name}_dram", a.shape, _mybir.dt.from_np(a.dtype), kind="ExternalInput").ap())
    for i, (shape, dtype) in enumerate(_OUTS):
        dt = _mybir.dt.from_np(_np.dtype(dtype))
        args.append(nc.dram_tensor(f"out_{i}_dram", shape, dt, kind="ExternalOutput").ap())
    kernel_body(nc, *args)
    r = _run(nc, [arrays], core_ids=[0])
    got = tuple(r.results[0][f"out_{i}_dram"] for i in range(len(_OUTS)))
    return got[0]
```
